# Optimizing a Trainium2 kernel written in Bass

```python
import numpy as np
import jax
import jax.numpy as jnp

def _softmax(x, axis=-1):
    return jax.nn.softmax(x, axis=axis)

def _gelu(x):
    return jax.nn.gelu(x, approximate=True)

def _silu(x):
    return jax.nn.silu(x)

def _sigmoid(x):
    return jax.nn.sigmoid(x)

def _layernorm(x, axis=-1, eps=1e-05):
    m = jnp.mean(x, axis=axis, keepdims=True)
    v = jnp.var(x, axis=axis, keepdims=True)
    return (x - m) / jnp.sqrt(v + eps)

def _scatter_add(tgt, idx, src, axis=0):
    return tgt.at[idx].add(src)

def _segment_sum(src, seg, n):
    return jax.ops.segment_sum(src, seg, n)
kernel_name = 'mk_decoder_preln_d1_seqx_r4_9b3c09'

def setup_inputs(seed: int=0):
    np.random.seed(seed)
    _w = jnp.asarray

    def _rec_inputs():
        import jax
        import jax.numpy as jnp
        _rk = jax.random.key(seed)
        x = -0.0005146 + 1 * jax.random.normal(jax.random.fold_in(_rk, 1), (8, 512, 256), jnp.float32)
        _lenS = 512 - jax.random.randint(jax.random.fold_in(_rk, 7), (8,), 0, max(1, 512 // 4) + 1, jnp.int32)
        _lenS2 = 1601 - jax.random.randint(jax.random.fold_in(_rk, 8), (8,), 0, max(1, 1601 // 4) + 1, jnp.int32)
        _ctx_768P = jax.random.normal(jax.random.fold_in(_rk, 11), (8, 16, 192), jnp.float32)
        _ctx_768c = jax.random.dirichlet(jax.random.fold_in(_rk, 511), 0.3 * jnp.ones((16,), jnp.float32), (8, 1601))
        _ctx_768t = jnp.einsum('bsk,bkd->bsd', _ctx_768c, _ctx_768P)
        _ctx_768t = _ctx_768t * jax.lax.rsqrt(jnp.mean(jnp.square(_ctx_768t)) + 1e-12) * 0.953939
        ctx_768 = -0.00040386 + 0.999972 * (_ctx_768t + 0.3 * jax.random.normal(jax.random.fold_in(_rk, 611), (8, 1601, 192), jnp.float32))
        _validS = jnp.arange(512)[None, :] < _lenS[:, None]
        _validS2 = jnp.arange(1601)[None, :] < _lenS2[:, None]
        _causal = jnp.tril(jnp.ones((512, 512), dtype=bool))
        mask_BxS2_bk0 = jnp.logical_not(jnp.broadcast_to(_validS2[:, :], (8, 1601)))
        return (x, ctx_768, mask_BxS2_bk0)
    x, ctx_768, mask_BxS2_bk0 = _rec_inputs()

    def _L0_attn_setup():
        import jax, jax.numpy as jnp
        import numpy as np
        B, S, D = (4, 512, 256)
        H = 16
        HS = D // H
        SCALE = HS ** 0.5
        key = jax.random.key(seed)
        ks = jax.random.split(key, 9)
        std = 1.0 / np.sqrt(D)

        def lin(kw, kb, fan_in, fan_out):
            w = jax.random.uniform(kw, (fan_in, fan_out), minval=-std, maxval=std, dtype=jnp.float32)
            b = jax.random.uniform(kb, (fan_out,), minval=-std, maxval=std, dtype=jnp.float32)
            return (w, b)
        Wq, bq = lin(ks[0], ks[1], D, D)
        Wk, bk = lin(ks[2], ks[3], D, D)
        Wv, bv = lin(ks[4], ks[5], D, D)
        Wm, bm = lin(ks[6], ks[7], D, D)
        x = jax.random.normal(ks[8], (B, S, D), dtype=jnp.float32)
        return {'x': x, 'Wq': Wq, 'bq': bq, 'Wk': Wk, 'bk': bk, 'Wv': Wv, 'bv': bv, 'Wm': Wm, 'bm': bm}
    _L0_attn_all = _L0_attn_setup()
    _L0_attn_in = {k: v for k, v in _L0_attn_all.items() if k in ('Wq', 'bq', 'Wk', 'bk', 'Wv', 'bv', 'Wm', 'bm')}
    del _L0_attn_all

    def _L0_xattn_setup():
        import jax, jax.numpy as jnp
        import numpy as np
        DIM_IN, DIM_LAT, DIM_HEAD = (192, 256, 64)
        INNER = max(DIM_LAT, DIM_IN)
        HEADS = INNER // DIM_HEAD
        SCALE = DIM_HEAD ** (-0.5)
        RMS_EPS = 1e-08
        LN_EPS = 1e-05

        def layernorm(x, g, b):
            mu = jnp.mean(x, axis=-1, keepdims=True)
            var = jnp.mean((x - mu) ** 2, axis=-1, keepdims=True)
            return (x - mu) * jax.lax.rsqrt(var + LN_EPS) * g + b

        def rmsnorm(x, gamma):
            norm = jnp.sqrt(jnp.sum(x * x, axis=-1, keepdims=True)) * x.shape[-1] ** (-0.5)
            return x / jnp.maximum(norm, RMS_EPS) * gamma
        key = jax.random.key(seed)
        ks = jax.random.split(key, 12)
        b, n, m = (4, 1024, 128)
        x = jax.random.normal(ks[0], (b, n, DIM_IN), jnp.float32)
        latents = jax.random.normal(ks[1], (b, m, DIM_LAT), jnp.float32)
        mask = jax.random.randint(ks[2], (b, n), 0, 2).astype(bool)
        s = lambda k, sh, fan: jax.random.normal(k, sh, jnp.float32) * fan ** (-0.5)
        return {'x': x, 'latents': latents, 'mask': mask, 'ln_x_g': jnp.ones((DIM_IN,), jnp.float32), 'ln_x_b': jnp.zeros((DIM_IN,), jnp.float32), 'ln_l_g': jnp.ones((DIM_LAT,), jnp.float32), 'ln_l_b': jnp.zeros((DIM_LAT,), jnp.float32), 'qn_g': jnp.ones((DIM_HEAD,), jnp.float32), 'kn_g': jnp.ones((DIM_HEAD,), jnp.float32), 'Wq': s(ks[3], (INNER, DIM_LAT), DIM_LAT), 'Wkv': s(ks[4], (2 * INNER, DIM_IN), DIM_IN), 'Wlkv': s(ks[5], (2 * INNER, DIM_LAT), DIM_LAT), 'Wo': s(ks[6], (DIM_LAT, INNER), INNER), 'bo': jnp.zeros((DIM_LAT,), jnp.float32)}
    _L0_xattn_all = _L0_xattn_setup()
    _L0_xattn_in = {k: v for k, v in _L0_xattn_all.items() if k in ('ln_x_g', 'ln_x_b', 'ln_l_g', 'ln_l_b', 'qn_g', 'kn_g', 'Wq', 'Wkv', 'Wlkv', 'Wo', 'bo')}
    del _L0_xattn_all

    def _L0_ffn_setup():
        import jax, jax.numpy as jnp
        import numpy as np
        B, S, D, H, E, K = (4, 512, 256, 1024, 8, 2)
        CAPACITY_FACTOR = 1.5
        C = int(CAPACITY_FACTOR * B * S * K / E)
        key = jax.random.key(seed)
        ks = jax.random.split(key, 6)
        x = jax.random.normal(ks[0], (B, S, D), dtype=jnp.float32)
        w_router = jax.random.normal(ks[1], (D, E), dtype=jnp.float32) * 0.02
        w1 = jax.random.normal(ks[2], (E, D, H), dtype=jnp.float32) * 0.02
        b1 = jnp.zeros((E, H), dtype=jnp.float32)
        w2 = jax.random.normal(ks[3], (E, H, D), dtype=jnp.float32) * 0.02
        b2 = jnp.zeros((E, D), dtype=jnp.float32)
        return {'x': x, 'w_router': w_router, 'w1': w1, 'b1': b1, 'w2': w2, 'b2': b2}
    _L0_ffn_all = _L0_ffn_setup()
    _L0_ffn_in = {k: v for k, v in _L0_ffn_all.items() if k in ('w_router', 'w1', 'b1', 'w2', 'b2')}
    del _L0_ffn_all
    return {'x': x, 'ctx_768': ctx_768, 'mask_BxS2_bk0': mask_BxS2_bk0, 'L0_attn_Wq': _L0_attn_in['Wq'], 'L0_attn_bq': _L0_attn_in['bq'], 'L0_attn_Wk': _L0_attn_in['Wk'], 'L0_attn_bk': _L0_attn_in['bk'], 'L0_attn_Wv': _L0_attn_in['Wv'], 'L0_attn_bv': _L0_attn_in['bv'], 'L0_attn_Wm': _L0_attn_in['Wm'], 'L0_attn_bm': _L0_attn_in['bm'], 'L0_xattn_ln_x_g': _L0_xattn_in['ln_x_g'], 'L0_xattn_ln_x_b': _L0_xattn_in['ln_x_b'], 'L0_xattn_ln_l_g': _L0_xattn_in['ln_l_g'], 'L0_xattn_ln_l_b': _L0_xattn_in['ln_l_b'], 'L0_xattn_qn_g': _L0_xattn_in['qn_g'], 'L0_xattn_kn_g': _L0_xattn_in['kn_g'], 'L0_xattn_Wq': _L0_xattn_in['Wq'], 'L0_xattn_Wkv': _L0_xattn_in['Wkv'], 'L0_xattn_Wlkv': _L0_xattn_in['Wlkv'], 'L0_xattn_Wo': _L0_xattn_in['Wo'], 'L0_xattn_bo': _L0_xattn_in['bo'], 'L0_ffn_w_router': _L0_ffn_in['w_router'], 'L0_ffn_w1': _L0_ffn_in['w1'], 'L0_ffn_b1': _L0_ffn_in['b1'], 'L0_ffn_w2': _L0_ffn_in['w2'], 'L0_ffn_b2': _L0_ffn_in['b2']}

def reference(x, ctx_768, mask_BxS2_bk0, L0_attn_Wq, L0_attn_bq, L0_attn_Wk, L0_attn_bk, L0_attn_Wv, L0_attn_bv, L0_attn_Wm, L0_attn_bm, L0_xattn_ln_x_g, L0_xattn_ln_x_b, L0_xattn_ln_l_g, L0_xattn_ln_l_b, L0_xattn_qn_g, L0_xattn_kn_g, L0_xattn_Wq, L0_xattn_Wkv, L0_xattn_Wlkv, L0_xattn_Wo, L0_xattn_bo, L0_ffn_w_router, L0_ffn_w1, L0_ffn_b1, L0_ffn_w2, L0_ffn_b2):
    import jax
    import jax.numpy as jnp

    def _L0_attn_ref(x, Wq, bq, Wk, bk, Wv, bv, Wm, bm):
        import jax, jax.numpy as jnp
        import numpy as np
        B, S, D = (4, 512, 256)
        H = 16
        HS = D // H
        SCALE = HS ** 0.5
        bs, seq, _ = x.shape

        def heads(w, b):
            return (x @ w + b).reshape(bs, seq, H, HS).transpose(0, 2, 1, 3)
        q = heads(Wq, bq)
        k = heads(Wk, bk)
        v = heads(Wv, bv)
        scores = jnp.einsum('bhqd,bhkd->bhqk', q, k) / SCALE
        causal_mask = jnp.arange(seq)[None, :] > jnp.arange(seq)[:, None]
        scores = jnp.where(causal_mask, jnp.float32(-1000000000000.0), scores)
        probs = jax.nn.softmax(scores, axis=-1)
        attn = jnp.einsum('bhqk,bhkd->bhqd', probs, v)
        attn = attn.transpose(0, 2, 1, 3).reshape(bs, seq, H * HS)
        return attn @ Wm + bm

    def _L0_xattn_ref(x, latents, mask, ln_x_g, ln_x_b, ln_l_g, ln_l_b, qn_g, kn_g, Wq, Wkv, Wlkv, Wo, bo):
        import jax, jax.numpy as jnp
        import numpy as np
        DIM_IN, DIM_LAT, DIM_HEAD = (192, 256, 64)
        INNER = max(DIM_LAT, DIM_IN)
        HEADS = INNER // DIM_HEAD
        SCALE = DIM_HEAD ** (-0.5)
        RMS_EPS = 1e-08
        LN_EPS = 1e-05

        def layernorm(x, g, b):
            mu = jnp.mean(x, axis=-1, keepdims=True)
            var = jnp.mean((x - mu) ** 2, axis=-1, keepdims=True)
            return (x - mu) * jax.lax.rsqrt(var + LN_EPS) * g + b

        def rmsnorm(x, gamma):
            norm = jnp.sqrt(jnp.sum(x * x, axis=-1, keepdims=True)) * x.shape[-1] ** (-0.5)
            return x / jnp.maximum(norm, RMS_EPS) * gamma
        b, n, _ = x.shape
        m = latents.shape[1]
        xn = layernorm(x, ln_x_g, ln_x_b)
        ln = layernorm(latents, ln_l_g, ln_l_b)
        q = ln @ Wq.T
        kv = jnp.concatenate([xn @ Wkv.T, ln @ Wlkv.T], axis=1)
        k, v = (kv[..., :INNER], kv[..., INNER:])
        split_heads = lambda t: t.reshape(t.shape[0], t.shape[1], HEADS, DIM_HEAD).transpose(0, 2, 1, 3)
        q, k, v = (split_heads(q), split_heads(k), split_heads(v))
        qn = rmsnorm(q, qn_g) * SCALE
        kn = rmsnorm(k, kn_g)
        attn = jnp.einsum('bhid,bhjd->bhij', qn, kn)
        full_mask = jnp.pad(mask, ((0, 0), (0, m)), constant_values=True)
        attn = jnp.where(full_mask[:, None, None, :], attn, -jnp.finfo(attn.dtype).max)
        attn = jax.nn.softmax(attn, axis=-1)
        out = jnp.einsum('bhij,bhjd->bhid', attn, v)
        out = out.transpose(0, 2, 1, 3).reshape(b, m, INNER)
        return out @ Wo.T + bo

    def _L0_ffn_ref(x, w_router, w1, b1, w2, b2):
        import jax, jax.numpy as jnp
        import numpy as np
        B, S, D, H, E, K = (4, 512, 256, 1024, 8, 2)
        CAPACITY_FACTOR = 1.5
        C = int(CAPACITY_FACTOR * B * S * K / E)
        Bs, Ss, Ds = x.shape
        N = Bs * Ss
        xf = x.reshape(N, Ds)
        logits = xf @ w_router
        probs = jax.nn.softmax(logits, axis=-1)
        gate, eidx = jax.lax.top_k(probs, K)
        gate = gate / jnp.sum(gate, axis=-1, keepdims=True)
        oh = jax.nn.one_hot(eidx, E, dtype=jnp.float32)
        ohf = oh.reshape(N * K, E)
        pos = jnp.cumsum(ohf, axis=0) - 1.0
        posk = jnp.sum(pos * ohf, axis=-1).reshape(N, K).astype(jnp.int32)
        keep = posk < C
        gate = gate * keep.astype(gate.dtype)
        e_flat = eidx.reshape(-1)
        p_flat = jnp.where(keep, posk, 0).reshape(-1)
        contrib = (xf[:, None, :] * keep[..., None].astype(xf.dtype)).reshape(N * K, Ds)
        expert_in = jnp.zeros((E, C, Ds), dtype=xf.dtype).at[e_flat, p_flat].add(contrib)
        h = jax.nn.relu(jnp.einsum('ecd,edh->ech', expert_in, w1) + b1[:, None, :])
        expert_out = jnp.einsum('ech,eho->eco', h, w2) + b2[:, None, :]
        tok = expert_out[e_flat, p_flat].reshape(N, K, -1)
        y = jnp.sum(tok * gate[..., None], axis=1)
        return y.reshape(Bs, Ss, -1)
    x = x + _L0_attn_ref(_layernorm(x, axis=-1), L0_attn_Wq, L0_attn_bq, L0_attn_Wk, L0_attn_bk, L0_attn_Wv, L0_attn_bv, L0_attn_Wm, L0_attn_bm)
    x = x + _L0_xattn_ref(ctx_768, _layernorm(x, axis=-1), mask_BxS2_bk0, L0_xattn_ln_x_g, L0_xattn_ln_x_b, L0_xattn_ln_l_g, L0_xattn_ln_l_b, L0_xattn_qn_g, L0_xattn_kn_g, L0_xattn_Wq, L0_xattn_Wkv, L0_xattn_Wlkv, L0_xattn_Wo, L0_xattn_bo)
    x = x + _L0_ffn_ref(_layernorm(x, axis=-1), L0_ffn_w_router, L0_ffn_w1, L0_ffn_b1, L0_ffn_w2, L0_ffn_b2)
    return x

_drawn_inputs = setup_inputs


def setup_inputs(seed=0):
    import zlib

    import numpy as np

    out = dict(_drawn_inputs(seed))
    spreads = {'L0_xattn_ln_x_g': (1.0, 0.2),
     'L0_xattn_ln_x_b': (0.0, 0.1),
     'L0_xattn_ln_l_g': (1.0, 0.2),
     'L0_xattn_ln_l_b': (0.0, 0.1),
     'L0_xattn_qn_g': (1.0, 0.588),
     'L0_xattn_kn_g': (1.0, 0.561),
     'L0_xattn_bo': (0.0, 0.1),
     'L0_ffn_b1': (0.0, 0.297),
     'L0_ffn_b2': (0.0, 0.1)}
    factors = {'L0_attn_Wq': 3.331, 'L0_attn_bq': 8.0, 'L0_attn_Wk': 3.295, 'L0_attn_bk': 8.0}
    for name, (base, spread) in spreads.items():
        noise = np.random.default_rng([zlib.crc32(name.encode()), seed]).standard_normal(out[name].shape)
        drawn = base * np.exp(spread * noise) if base else spread * noise
        out[name] = jnp.asarray(drawn.astype(out[name].dtype))
    for name, factor in factors.items():
        out[name] = (out[name] * factor).astype(out[name].dtype)
    return out
```

```python
from contextlib import ExitStack

import concourse.bass as bass
from concourse import mybir

ALU = mybir.AluOpType
ACT = mybir.ActivationFunctionType
F32 = mybir.dt.float32
BF16 = mybir.dt.bfloat16
U32 = mybir.dt.uint32
U8 = mybir.dt.uint8
AX = mybir.AxisListType
ds = bass.ds

P = 128
B, S, D = 8, 512, 256
C = D // P
T = S // P
H, HS = 16, 16
SC, DC = 1601, 192
CT = -(-SC // P)
SCP = CT * P
KT = CT + T
XH, XD = 4, 64
E, HID, CAP = 8, 1024, 768
ST = CAP // P
HC = HID // P
EPS, RMS_EPS = 1e-5, 1e-8
NEG = -1e30
HEADROOM = 70.0
FAR = 1.0e6

Q_PARTS = [0, 0, 0, 1, 1, 2]
K_PARTS = [0, 1, 2, 0, 1, 0]
NPART = len(Q_PARTS)
MAXROW = NPART * HS

MADE = 32
DVE_STEPS = 58
POOL_STEPS = 7


class Count:

    def __init__(self, sem, per, before=0):
        self.sem, self.per, self.before = sem, per, before

    def at(self, turn, k):
        return turn * self.per + (self.before + k)


def decoder(nc, a, out):
    with ExitStack() as ctx:
        dram = lambda n, s, d: nc.dram_tensor(n, s, d, kind="Internal").ap()
        scratch = {
            "expert_in": dram("expert_in", (E * CAP, D), F32),
            "expert_out": dram("expert_out", (E * CAP, D), F32),
            "resid": dram("resid", (B, S, D), F32),
            "parts": dram("parts", (2, 3, D, S), BF16),
            "maxima": dram("maxima", (H * T, P), BF16),
        }
        kept = {n: ctx.enter_context(nc.sbuf_tensor(n, s, d)) for n, s, d in (
            ("gates", [P, B, 2, T], F32), ("gather_at", [P, B, 2, T], U32), ("ident", [P, P], F32))}
        attention_and_routing(nc, a, kept, scratch)
        experts_and_combine(nc, a, kept, scratch, out)


def attention_and_routing(nc, a, kept, scratch):
    with ExitStack() as ctx:
        sb = lambda n, s, d=F32: ctx.enter_context(nc.sbuf_tensor(n, s, d))
        sem = lambda n: ctx.enter_context(nc.semaphore(n))
        ident = kept["ident"]

        identb = sb("identb", [P, P], BF16)
        hide_kq = sb("hide_kq", [P, P], BF16)
        hide_qk = sb("hide_qk", [P, P], BF16)
        before = sb("before", [P, P])
        ones = sb("ones", [P, P])
        halves = sb("halves", [P, 2])
        minus_half = sb("minus_half", [P, KT * XH])
        rank = sb("rank", [P, T, E])
        w_self = {n: sb("w_" + n, [P, C, D]) for n in ("Wq", "Wk", "Wv", "Wm")}
        b_self = {n: sb("b_" + n, [P, C]) for n in ("bq", "bk")}
        spread = {n: sb("s_" + n, [P, D]) for n in ("bv", "bm", "bo")}
        xwqT = sb("xwqT", [P, C, D])
        xwoT = sb("xwoT", [P, C, D])
        xwlT = sb("xwlT", [P, C, 2 * D])
        xwcT = sb("xwcT", [P, C, 2 * D])
        router = sb("router", [P, C, E])
        ln_x = sb("ln_x", [P, C, 2])
        ln_l = sb("ln_l", [P, C, 2])
        gcol = sb("gcol", [P, 2])
        grow = sb("grow", [P, 2, XD])
        gqk = sb("gqk", [P, 1])
        shift = sb("shift", [P, 1])
        mask8 = sb("mask8", [B * CT, P], U8)
        maskf = sb("maskf", [B * CT, P])
        hide = sb("hide", [P, B * CT])
        ctx_bias = sb("ctx_bias", [P, B * CT])

        xb = sb("xb", [P, T, D])
        xn = sb("xn", [P, T, D])
        xnT = sb("xnT", [P, C, S])
        stats = sb("stats", [P, CT, 6])
        mv = sb("mv", [P, CT, 2])
        var = sb("var", [P, CT])
        inv = sb("inv", [P, CT])
        inv2 = sb("inv2", [P, T])
        qk = [sb("qT", [P, C, S]), sb("kT", [P, C, S])]
        part = [sb(f"part{i}", [P, 3, C, S], BF16) for i in range(2)]
        stack = [sb("q_stack", [P, H, S], BF16), sb("k_stack", [P, H, S], BF16)]
        v_self = sb("v_self", [P, T, H, HS + 1])
        cb = sb("cb", [P, CT, D])
        cT = sb("cT", [P, C, SCP])
        xk = sb("xk", [P, C, KT * P])
        cT_flat = cT[:].rearrange("p c s -> p (c s)")
        raw = cT_flat[:, 0:4 * D].rearrange("p (t d) -> p t d", t=4)
        xk2 = cT_flat[:, 0:KT * P]
        xv = sb("xv", [P, KT, XH, XD + 1])
        k_ss = sb("k_ss", [P, KT * XH])
        k_inv = sb("k_inv", [P, KT * XH])
        key_bias = sb("key_bias", [P, KT])
        nmax_pad = sb("nmax", [P, P])
        nmax = nmax_pad[:, 0:H * T].rearrange("p (h t) -> p h t", h=H)
        nmaxT = sb("nmaxT", [H * T, P], BF16)
        NPR = 10
        pr = sb("pr", [P, NPR, S])
        rec = sb("rec", [P, 4 * T])
        at = sb("at", [P, T, D])
        atT = sb("atT", [P, C, S])
        rest = at[:].rearrange("p t d -> p (t d)").rearrange("p (c s) -> p c s", c=C)
        qz = sb("qz", [P, XH, S])
        q_ss = sb("q_ss", [P, T * XH])
        q_inv = sb("q_inv", [P, T * XH])
        carry = sb("carry", [P, E])
        r = {n: sb("r_" + n, [P, T, E]) for n in ("lg", "ex", "pr", "eq", "oh0", "oh1", "m", "pos", "t")}
        c = {n: sb("c_" + n, [P, T]) for n in ("mx", "sm", "rc", "m0", "m1", "r0", "r1", "p0", "p1",
                                               "k0", "k1", "b0", "b1", "f0", "f1")}
        slot = [sb(f"slot{i}", [P, T], U32) for i in range(2)]
        tick = sb("tick", [1, 16])
        vtick = sb("vtick", [1, 4])

        psum = ctx.enter_context(nc.psum_tensor("psum", [P, 8, 512], F32))
        NG, NO, NS = 2, 2, 4
        G = lambda i: psum[:, i % NG, :]
        O = lambda i: psum[:, NG + i % NO, :]
        SX = lambda i: psum[:, NG + NO + i % NS, :]

        TOOK, NGU = {}, 0
        for kind, uses in (("xnT", C), ("q", C), ("k", C), ("v", T // 2), ("ctxT", C * -(-CT // 4)),
                           ("ctx_k", C * -(-SCP // 512)), ("ctx_v", -(-CT // 2)), ("max", H // 2 * 5), ("maxT", 1),
                           ("attnT", C), ("x1", T // 2), ("latT", C), ("xq", T // 2), ("latent_k", C),
                           ("latent_v", T // 2), ("xqT", C), ("k_squares", 1), ("xattnT", C), ("x2", T // 2),
                           ("xfT", C), ("logits", 1), ("places", 1)):
            NGU += uses
            TOOK[kind] = NGU
        NSU = H // 2 * 5 + XH * KT
        NOU = H // 4 + XH
        sems = {n: sem(n) for n in (
            "weights_loaded", "raw_loaded", "constants_made", "weight_turned", "weight_copied", "setup_step",
            "slots_cleared", "tables_made", "halves_made")}
        C_ = lambda n, per, before=0: Count(sem(n), per, before)
        g_ready, g_taken = C_("product_ready", NGU), C_("product_taken", NGU)
        s_ready, s_done = C_("scores_ready", NSU), C_("exps_done", NSU)
        pr_used = C_("probs_used", H // 2 + XH * KT)
        o_taken = C_("sums_taken", NOU)
        x_in, c_in = C_("x_loaded", 16), C_("context_loaded", 32)
        v_step = C_("vector_step", DVE_STEPS)
        p_step = C_("pool_step", POOL_STEPS)
        normed = C_("tokens_normed", 3)
        c_normed = C_("context_normed", 1)
        padded = C_("variance_padded", 5)
        powered = C_("inverse_ready", 6)
        split = C_("parts_made", 6)
        stored = C_("parts_stored", 6 * 16)
        stacked = C_("parts_stacked", 2 * NPART * 16)
        xb_biased = C_("bias_added", 2)
        kb_ready = C_("key_bias_ready", 1)
        sq_ready = C_("squares_ready", C)
        sq_used = C_("squares_used", C - 1)
        q_normed = C_("queries_normed", 1)
        max_out, max_in = C_("maxima_stored", 16), C_("maxima_placed", 16)
        x2_out = C_("residual_stored", 16)
        ex_ready = C_("logit_exps_ready", 1)
        hot_ready = C_("choices_ready", 1)
        slots_ready, scattered = C_("slots_ready", 2), C_("rows_scattered", 2 * T * 16)
        turn_done = C_("turn_done", 1, 1)

        block = ctx.enter_context(nc.Block())
        full, left = SC // P, SC % P
        LOADS = []
        for n in ("Wq", "Wk", "Wv", "Wm"):
            LOADS.append((w_self[n][:], a["L0_attn_" + n].rearrange("(c p) n -> p c n", p=P)))
        for n in ("bq", "bk"):
            LOADS.append((b_self[n][:], a["L0_attn_" + n].rearrange("(c p) -> p c", p=P)))
        for n, src in (("bv", "L0_attn_bv"), ("bm", "L0_attn_bm"), ("bo", "L0_xattn_bo")):
            LOADS.append((spread[n][:], a[src].partition_broadcast(P)))
        LOADS.append((router[:], a["L0_ffn_w_router"].rearrange("(c p) n -> p c n", p=P)))
        for i, n in enumerate(("g", "b")):
            LOADS.append((ln_l[:, :, i], a["L0_xattn_ln_l_" + n].rearrange("(c p) -> p c", p=P)))
            v = a["L0_xattn_ln_x_" + n].rearrange("(p a) -> p a", a=1)
            LOADS.append((ln_x[:, 0, i:i + 1], v[0:P, :]))
            LOADS.append((ln_x[0:DC - P, 1, i:i + 1], v[P:DC, :]))
        for i, n in enumerate(("qn_g", "kn_g")):
            v = a["L0_xattn_" + n]
            LOADS.append((grow[:, i, :], v.partition_broadcast(P)))
            for h in range(2):
                LOADS.append((gcol[h * XD:(h + 1) * XD, i:i + 1], v.rearrange("(p a) -> p a", a=1)))
        for b in range(B):
            m = a["mask_BxS2_bk0"][b, :]
            LOADS.append((mask8[b * CT:b * CT + full, :], m[0:full * P].rearrange("(t p) -> t p", p=P)))
            LOADS.append((mask8[b * CT + full:b * CT + full + 1, 0:left],
                          m[full * P:SC].rearrange("(a p) -> a p", a=1)))
        TURNED = [("Wq", 2, D, xwqT), ("Wo", 2, D, xwoT), ("Wlkv", 4, D, xwlT), ("Wkv", 4, DC, xwcT)]
        chunks = lambda w: [(k, min(P, w - k * P)) for k in range(-(-w // P))]

        @block.sync
        def _(sp):
            sp.wait_ge(sems["constants_made"], 4)
            for dst, src in LOADS:
                sp.dma_start(dst, src, allow_slow_non_contiguous=True).then_inc(sems["weights_loaded"], 16)
            for i, (n, t, w, _) in enumerate(TURNED):
                if i:
                    sp.wait_ge(sems["weight_turned"], C * i)
                sp.dma_start(raw[:, 0:t, 0:w], a["L0_xattn_" + n].rearrange("(t p) n -> p t n", p=P)
                             ).then_inc(sems["raw_loaded"], 16)
            for s in range(E * CAP // (P * T)):
                sp.dma_start(scratch["expert_in"][s * P * T:(s + 1) * P * T, :]
                             .rearrange("(t p) d -> p t d", p=P), xn[:]).then_inc(sems["slots_cleared"], 16)
            sp.wait_ge(sems["slots_cleared"], 16 * (E * CAP // (P * T)))
            with sp.Fori(0, B) as b:
                sp.wait_ge(turn_done.sem, turn_done.at(b, 0))
                sp.dma_start(xb[:], a["x"][ds(b, 1), :, :].rearrange("a (t p) d -> p (a t) d", p=P)
                             ).then_inc(x_in.sem, 16)
                sp.dma_start(cb[:, 0:full, 0:DC], a["ctx_768"][ds(b, 1), 0:full * P, :]
                             .rearrange("a (t p) d -> p (a t) d", p=P)).then_inc(c_in.sem, 16)
                sp.dma_start(cb[0:left, full, 0:DC], a["ctx_768"][ds(b, 1), full * P:SC, :]
                             .rearrange("a p d -> (a p) d")).then_inc(c_in.sem, 16)
                for i in range(2):
                    for j in range(3):
                        sp.wait_ge(split.sem, split.at(b, 3 * i + j + 1))
                        sp.dma_start(scratch["parts"][i, j, :, :].rearrange("(c p) s -> p c s", p=P),
                                     part[i][:, j, :, :]).then_inc(stored.sem, 16)
                sp.wait_ge(stored.sem, stored.at(b, 6 * 16))
                for i, order in enumerate((Q_PARTS, K_PARTS)):
                    for j, p in enumerate(order):
                        sp.dma_start(stack[i][j * HS:(j + 1) * HS, :, :],
                                     scratch["parts"][i, p, :, :].rearrange("(h d) s -> d h s", d=HS)
                                     ).then_inc(stacked.sem, 16)
                sp.wait_ge(g_taken.sem, g_taken.at(b, TOOK["maxT"]))
                sp.dma_start(scratch["maxima"], nmaxT[:]).then_inc(max_out.sem, 16)
                sp.wait_ge(max_out.sem, max_out.at(b, 16))
                sp.dma_start(stack[0][MAXROW:MAXROW + 1, :, :], scratch["maxima"]
                             .rearrange("(a h t) p -> a h (t p)", a=1, h=H)).then_inc(max_in.sem, 16)
                sp.wait_ge(g_taken.sem, g_taken.at(b, TOOK["x2"]))
                sp.dma_start(scratch["resid"][ds(b, 1), :, :].rearrange("a (t p) d -> p (a t) d", p=P), xb[:]
                             ).then_inc(x2_out.sem, 16)

        @block.gpsimd
        def _(pool):
            made = sems["constants_made"]
            nc.gpsimd.memset(mask8[:], 0).then_inc(made, 1)
            nc.gpsimd.memset(cb[:], 0.0).then_inc(made, 1)
            nc.gpsimd.memset(xn[:], 0.0).then_inc(made, 1)
            nc.gpsimd.memset(ln_x[:], 0.0).then_inc(made, 1)
            nc.gpsimd.memset(xwcT[:], 0.0).then_inc(made, 1)
            nc.gpsimd.memset(nmax_pad[:], 0.0).then_inc(made, 1)
            zero_in = [(ident, ALU.not_equal, 1.0, 0.0, -1), (identb, ALU.not_equal, 1.0, 0.0, -1),
                       (hide_kq, ALU.is_ge, NEG, 0.0, 1), (hide_qk, ALU.is_ge, NEG, 0.0, -1),
                       (before, ALU.is_gt, 0.0, 1.0, 1)]
            for m, _, _, base, _ in zero_in:
                nc.gpsimd.memset(m[:], base).then_inc(made, 1)
            nc.gpsimd.memset(ones[:], 1.0).then_inc(made, 1)
            nc.gpsimd.memset(halves[:], 0.0).then_inc(made, 1)
            nc.gpsimd.memset(minus_half[:], -0.5).then_inc(made, 1)
            nc.gpsimd.memset(qz[:], 0.0).then_inc(made, 1)
            nc.gpsimd.memset(stack[1][:], 1.0).then_inc(made, 1)
            nc.gpsimd.memset(v_self[:], 1.0).then_inc(made, 1)
            nc.gpsimd.memset(xv[:], 1.0).then_inc(made, 1)
            nc.gpsimd.memset(carry[:], 0.0).then_inc(made, 1)
            for e in range(E):
                nc.gpsimd.memset(rank[:, :, e], float(E - e)).then_inc(made, 1)
            pool.wait_ge(made, 19 + E)
            for m, op, fill, _, sign in zero_in:
                nc.gpsimd.affine_select(out=m[:], in_=m[:], compare_op=op, fill=fill, base=0,
                                        pattern=[[sign, P]], channel_multiplier=-sign).then_inc(made, 1)
            pool.wait_ge(made, MADE)
            pool.wait_ge(sems["slots_cleared"], 16 * (E * CAP // (P * T)))
            nc.gpsimd.memset(tick[:, 0:1], 0.0).then_inc(turn_done.sem, 1)

            with pool.Fori(0, B) as b:
                n = [0]

                def step(ins):
                    n[0] += 1
                    ins.then_inc(p_step.sem, 1)
                    pool.wait_ge(p_step.sem, p_step.at(b, n[0]))

                def power(dst, src):
                    w = src.shape[1]
                    nc.gpsimd.tensor_tensor(dst, src, minus_half[:, 0:w], ALU.pow).then_inc(powered.sem, 1)

                ticks = [0]

                def held():
                    ticks[0] += 1
                    nc.gpsimd.tensor_tensor(tick[:, ticks[0]:ticks[0] + 1], ones[0:1, 0:1], ones[0:1, 0:1], ALU.add)

                pool.wait_ge(turn_done.sem, turn_done.at(b, 0))
                pool.wait_ge(padded.sem, padded.at(b, 1))
                power(inv[:, 0:T], var[:, 0:T])
                pool.wait_ge(padded.sem, padded.at(b, 2))
                power(inv[:, 0:CT], var[:, 0:CT])
                nc.gpsimd.tensor_copy(key_bias[:, 0:CT], ctx_bias[:, ds(b * CT, CT)]).then_inc(kb_ready.sem, 1)
                pool.wait_ge(normed.sem, normed.at(b, 1))
                for t in range(T):
                    add = nc.gpsimd.tensor_tensor(xb[:, t, :], xb[:, t, :], spread["bm"][:], ALU.add)
                add.then_inc(xb_biased.sem, 1)
                for i in range(2):
                    pool.wait_ge(g_taken.sem, g_taken.at(b, (TOOK["q"], TOOK["k"])[i]))
                    if i:
                        pool.wait_ge(split.sem, split.at(b, 3))
                    held()
                    nc.gpsimd.tensor_copy(part[i][:, 0], qk[i][:]).then_inc(split.sem, 1)
                    pool.wait_ge(split.sem, split.at(b, 3 * i + 1))
                    step(nc.gpsimd.tensor_tensor(rest, qk[i][:], part[i][:, 0], ALU.subtract))
                    held()
                    nc.gpsimd.tensor_copy(part[i][:, 1], rest).then_inc(split.sem, 1)
                    pool.wait_ge(split.sem, split.at(b, 3 * i + 2))
                    nc.gpsimd.tensor_tensor(part[i][:, 2], rest, part[i][:, 1], ALU.subtract
                                            ).then_inc(split.sem, 1)
                pool.wait_ge(padded.sem, padded.at(b, 3))
                step(nc.gpsimd.tensor_tensor(inv[:, 0:T], var[:, 0:T], minus_half[:, 0:T], ALU.pow))
                step(nc.gpsimd.tensor_tensor(inv2[:], inv[:, 0:T], inv[:, 0:T], ALU.mult))
                step(nc.gpsimd.tensor_tensor(inv2[:], inv2[:], mv[:, 0:T, 1], ALU.mult))
                held()
                step(nc.gpsimd.tensor_scalar(inv2[:], inv2[:], EPS, None, ALU.add))
                step(nc.gpsimd.tensor_tensor(inv2[:], inv2[:], minus_half[:, 0:T], ALU.pow))
                nc.gpsimd.tensor_tensor(inv[:, 0:T], inv[:, 0:T], inv2[:], ALU.mult).then_inc(powered.sem, 1)
                pool.wait_ge(normed.sem, normed.at(b, 2))
                for t in range(T):
                    add = nc.gpsimd.tensor_tensor(xb[:, t, :], xb[:, t, :], spread["bo"][:], ALU.add)
                add.then_inc(xb_biased.sem, 1)
                pool.wait_ge(padded.sem, padded.at(b, 4))
                power(q_inv[:], q_ss[:])
                for k in range(C):
                    pool.wait_ge(g_taken.sem, g_taken.at(b, TOOK["latent_k"] - 1 + k))
                    if k:
                        pool.wait_ge(sq_used.sem, sq_used.at(b, k))
                    nc.gpsimd.tensor_tensor(xk2, xk[:, k, :], xk[:, k, :], ALU.mult).then_inc(sq_ready.sem, 1)
                pool.wait_ge(g_taken.sem, g_taken.at(b, TOOK["k_squares"]))
                power(k_inv[:], k_ss[:])
                pool.wait_ge(padded.sem, padded.at(b, 5))
                power(inv[:, 0:T], var[:, 0:T])
                pool.wait_ge(slots_ready.sem, slots_ready.at(b, 2))
                held()
                for t in range(T):
                    for k in range(2):
                        nc.gpsimd.indirect_dma_start(
                            scratch["expert_in"], bass.IndirectOffsetOnAxis(slot[k][:, t:t + 1], 0), xn[:, t, :],
                            None, bounds_check=E * CAP - 1, oob_is_err=False).then_inc(scattered.sem, 16)
                pool.wait_ge(scattered.sem, scattered.at(b, 2 * T * 16))
                pool.wait_ge(x2_out.sem, x2_out.at(b, 16))
                held()
                nc.gpsimd.memset(tick[:, 0:1], 0.0).then_inc(turn_done.sem, 1)
                assert n[0] == p_step.per, n

        @block.scalar
        def _(act):
            with act.Fori(0, B) as b:
                act.wait_ge(turn_done.sem, turn_done.at(b, 0))
                for pair in range(H // 2):
                    if pair >= 2:
                        act.wait_ge(pr_used.sem, pr_used.at(b, pair - 1))
                    for u in range(5):
                        i = 5 * pair + u
                        act.wait_ge(s_ready.sem, s_ready.at(b, i + 1))
                        nc.scalar.activation(pr[:, i % NPR, :], SX(i), ACT.Exp).then_inc(s_done.sem, 1)
                act.wait_ge(kb_ready.sem, kb_ready.at(b, 1))
                act.wait_ge(powered.sem, powered.at(b, 5))
                for h in range(XH):
                    for j in range(KT):
                        i = H // 2 * 5 + h * KT + j
                        act.wait_ge(s_ready.sem, s_ready.at(b, i + 1))
                        m = h * KT + j - NPR
                        act.wait_ge(pr_used.sem, pr_used.at(b, H // 2 + max(m + 1, 0)))
                        bias = key_bias[:, j:j + 1] if j < CT else shift[:, 0:1]
                        nc.scalar.activation(pr[:, i % NPR, :], SX(i), ACT.Exp, bias=bias,
                                             scale=k_inv[:, j * XH + h:j * XH + h + 1]).then_inc(s_done.sem, 1)
                act.wait_ge(g_taken.sem, g_taken.at(b, TOOK["logits"]))
                nc.scalar.activation(r["ex"][:], r["lg"][:], ACT.Exp).then_inc(ex_ready.sem, 1)

        @block.tensor
        def _(pe):
            mm, turn = nc.tensor.matmul, nc.tensor.transpose
            pe.wait_ge(sems["constants_made"], MADE)
            k = 0
            for i, (_, t, w, dst) in enumerate(TURNED):
                pe.wait_ge(sems["raw_loaded"], 16 * (i + 1))
                for ch, cw in chunks(w):
                    if k >= 4:
                        pe.wait_ge(sems["weight_copied"], k - 3)
                    for j in range(t):
                        last = turn(SX(k)[0:cw, j * P:(j + 1) * P], raw[:, j, ch * P:ch * P + cw], ident[:])
                    last.then_inc(sems["weight_turned"], 1)
                    k += 1
            pe.wait_ge(sems["setup_step"], 1)
            pe.wait_ge(sems["weight_copied"], k - 3)
            turn(SX(k)[:, 0:B * CT], maskf[:], ident[0:B * CT, 0:B * CT]).then_inc(sems["weight_turned"], 1)
            pe.wait_ge(sems["tables_made"], 1)
            pe.wait_ge(sems["weights_loaded"], 16 * len(LOADS))

            with pe.Fori(0, B) as b:
                g, s, o = [0], [0], [0]

                def bank():
                    g[0] += 1
                    if g[0] > NG:
                        pe.wait_ge(g_taken.sem, g_taken.at(b, g[0] - NG))
                    return G(g[0] - 1)

                def sbank():
                    s[0] += 1
                    if s[0] > NS:
                        pe.wait_ge(s_done.sem, s_done.at(b, s[0] - NS))
                    return SX(s[0] - 1)

                def turned(src, tiles, width=D):
                    for ch, cw in chunks(width):
                        for t0 in range(0, tiles, 4):
                            dst = bank()
                            for t in range(t0, min(t0 + 4, tiles)):
                                last = turn(dst[0:cw, (t - t0) * P:(t - t0 + 1) * P],
                                            src[:, t, ch * P:ch * P + cw], ident[:])
                            last.then_inc(g_ready.sem, 1)

                def to_features(w, col, src, width, n, contract=D):
                    for t0 in range(0, n, 512):
                        dst = bank()
                        tw = min(512, n - t0)
                        for ch, cw in chunks(contract):
                            last = mm(dst[:, 0:tw], w[0:cw, ch, col:col + width], src[0:cw, ch, t0:t0 + tw],
                                      start=ch == 0, stop=ch == C - 1)
                        last.then_inc(g_ready.sem, 1)

                def to_tokens(w, col, src, tiles, contract=D):
                    for t0 in range(0, tiles, 2):
                        dst = bank()
                        for t in range(t0, min(t0 + 2, tiles)):
                            for ch, cw in chunks(contract):
                                last = mm(dst[:, (t - t0) * D:(t - t0 + 1) * D], src[0:cw, ch, t * P:(t + 1) * P],
                                          w[0:cw, ch, col:col + D], start=ch == 0, stop=ch == C - 1)
                        last.then_inc(g_ready.sem, 1)

                pe.wait_ge(normed.sem, normed.at(b, 1))
                turned(xn, T)
                pe.wait_ge(g_taken.sem, g_taken.at(b, g[0]))
                for n in ("Wq", "Wk"):
                    for oc in range(C):
                        to_features(w_self[n], oc * P, xnT, P, S)
                to_tokens(w_self["Wv"], 0, xnT, T)
                pe.wait_ge(c_normed.sem, c_normed.at(b, 1))
                turned(cb, CT)
                pe.wait_ge(g_taken.sem, g_taken.at(b, g[0]))
                for oc in range(C):
                    to_features(xwcT, oc * P, cT, P, SCP)
                to_tokens(xwcT, D, cT, CT)

                pe.wait_ge(stacked.sem, stacked.at(b, 2 * NPART * 16))
                qs, ks = stack

                def seen(dst, h, q):
                    w = (q + 1) * P
                    mm(dst[:, 0:w], qs[0:MAXROW, h, q * P:w], ks[0:MAXROW, h, 0:w], start=True, stop=False)
                    return mm(dst[:, q * P:w], identb[:], hide_qk[:], start=False, stop=True)

                for h in range(0, H, 2):
                    for hh in (h, h + 1):
                        seen(bank(), hh, 3).then_inc(g_ready.sem, 1)
                        dst = bank()
                        seen(dst, hh, 2)
                        seen(dst[:, 3 * P:], hh, 0).then_inc(g_ready.sem, 1)
                    dst = bank()
                    seen(dst, h, 1)
                    seen(dst[:, 2 * P:], h + 1, 1).then_inc(g_ready.sem, 1)
                dst = bank()
                pe.wait_ge(g_taken.sem, g_taken.at(b, g[0] - 1))
                turn(dst[:, 0:P], nmax_pad[:], ident[:]).then_inc(g_ready.sem, 1)

                def scored(dst, h, k):
                    w = S - k * P
                    mm(dst[:, 0:w], ks[0:MAXROW + 1, h, k * P:(k + 1) * P], qs[0:MAXROW + 1, h, k * P:S],
                       start=True, stop=False)
                    return mm(dst[:, 0:P], identb[:], hide_kq[:], start=False, stop=True)

                def scores(pair):
                    h = 2 * pair
                    for hh in (h, h + 1):
                        scored(sbank(), hh, 0).then_inc(s_ready.sem, 1)
                        dst = sbank()
                        scored(dst, hh, 1)
                        scored(dst[:, 3 * P:], hh, 3).then_inc(s_ready.sem, 1)
                    dst = sbank()
                    scored(dst, h, 2)
                    scored(dst[:, 2 * P:], h + 1, 2).then_inc(s_ready.sem, 1)

                def summed(pair):
                    if pair % 2 == 0:
                        o[0] += 1
                        if o[0] > NO:
                            pe.wait_ge(o_taken.sem, o_taken.at(b, o[0] - NO))
                    acc = O(o[0] - 1)[:, 0:4 * T * (HS + 1)].rearrange("p (h t d) -> p h t d", h=4, t=T)
                    pe.wait_ge(s_done.sem, s_done.at(b, 5 * pair + 5))
                    for hh in range(2):
                        h = 2 * pair + hh
                        lies = [(2 * hh, 0), (2 * hh + 1, 0), (4, 2 * P * hh), (2 * hh + 1, 3 * P)]
                        for q in range(T):
                            for k in range(q + 1):
                                u, col = lies[k]
                                col += (q - k) * P
                                last = mm(acc[:, h % 4, q, :], pr[:, (5 * pair + u) % NPR, col:col + P],
                                          v_self[:, k, h, :], start=k == 0, stop=k == q)
                    last.then_inc(pr_used.sem, 1)
                    return last

                pe.wait_ge(max_in.sem, max_in.at(b, 16))
                scores(0)
                for pair in range(H // 2):
                    if pair + 1 < H // 2:
                        scores(pair + 1)
                    summed(pair)

                pe.wait_ge(o_taken.sem, o_taken.at(b, o[0]))
                turned(at, T)
                pe.wait_ge(g_taken.sem, g_taken.at(b, g[0]))
                to_tokens(w_self["Wm"], 0, atT, T)

                pe.wait_ge(normed.sem, normed.at(b, 2))
                turned(xn, T)
                pe.wait_ge(g_taken.sem, g_taken.at(b, g[0]))
                to_tokens(xwqT, 0, xnT, T)
                for oc in range(C):
                    to_features(xwlT, oc * P, xnT, P, S)
                to_tokens(xwlT, D, xnT, T)
                for ch in range(C):
                    dst = bank()
                    if ch == 0:
                        pe.wait_ge(q_normed.sem, q_normed.at(b, 1))
                    for t in range(T):
                        last = turn(dst[:, t * P:(t + 1) * P], at[:, t, ch * P:(ch + 1) * P], ident[:])
                    last.then_inc(g_ready.sem, 1)
                dst = bank()
                for ch in range(C):
                    pe.wait_ge(sq_ready.sem, sq_ready.at(b, ch + 1))
                    for j in range(KT):
                        last = mm(dst[:, j * XH + 2 * ch:j * XH + 2 * ch + 2], xk2[:, j * P:(j + 1) * P], halves[:],
                                  start=True, stop=True)
                    last.then_inc(sq_used.sem if ch < C - 1 else g_ready.sem, 1)
                pe.wait_ge(g_taken.sem, g_taken.at(b, g[0] - 1))

                def xscores(h, j):
                    dst = sbank()
                    mm(dst, xk[:, h // 2, j * P:(j + 1) * P], qz[:, h, :], start=True, stop=True
                       ).then_inc(s_ready.sem, 1)

                units = [(h, j) for h in range(XH) for j in range(KT)]
                for u in range(3):
                    xscores(*units[u])
                for u, (h, j) in enumerate(units):
                    if u + 3 < len(units):
                        xscores(*units[u + 3])
                    if j == 0:
                        o[0] += 1
                        pe.wait_ge(o_taken.sem, o_taken.at(b, o[0] - NO))
                    i = H // 2 * 5 + u
                    pe.wait_ge(s_done.sem, s_done.at(b, i + 1))
                    for q in range(T):
                        last = mm(O(o[0] - 1)[:, q * (XD + 1):(q + 1) * (XD + 1)], pr[:, i % NPR, q * P:(q + 1) * P],
                                  xv[:, j, h, :], start=j == 0 and q == 0, stop=j == KT - 1, skip_group_check=True)
                    last.then_inc(pr_used.sem, 1)

                pe.wait_ge(o_taken.sem, o_taken.at(b, o[0]))
                turned(at, T)
                pe.wait_ge(g_taken.sem, g_taken.at(b, g[0]))
                to_tokens(xwoT, 0, atT, T)

                pe.wait_ge(normed.sem, normed.at(b, 3))
                turned(xn, T)
                pe.wait_ge(g_taken.sem, g_taken.at(b, g[0]))
                dst = bank()
                for t in range(T):
                    for ch in range(C):
                        last = mm(dst[:, t * E:(t + 1) * E], xnT[:, ch, t * P:(t + 1) * P], router[:, ch, :],
                                  start=ch == 0, stop=ch == C - 1)
                last.then_inc(g_ready.sem, 1)
                pe.wait_ge(hot_ready.sem, hot_ready.at(b, 1))
                dst = bank()
                for t in range(T + 1):
                    for u in range(min(t + 1, T)):
                        last = mm(dst[:, t * E:(t + 1) * E], before[:] if u == t else ones[:], r["m"][:, u, :],
                                  start=u == 0, stop=u == min(t, T - 1))
                last.then_inc(g_ready.sem, 1)
                assert (g[0], s[0], o[0]) == (NGU, NSU, NOU), (g, s, o)

        @block.vector
        def _(dve):
            V = nc.vector
            made = sems["setup_step"]
            dve.wait_ge(sems["constants_made"], MADE)
            dve.wait_ge(sems["weights_loaded"], 16 * len(LOADS))
            V.tensor_copy(maskf[:], mask8[:]).then_inc(made, 1)
            for h in range(2):
                V.memset(halves[h * XD:(h + 1) * XD, h:h + 1], 1.0).then_inc(sems["halves_made"], 1)
            V.tensor_tensor(grow[:, 0, :], grow[:, 0, :], grow[:, 1, :], ALU.mult).then_inc(made, 1)
            V.scalar_tensor_tensor(out=gqk[:], in0=gcol[:, 0:1], scalar=XD ** -0.5, in1=gcol[:, 1:2],
                                   op0=ALU.mult, op1=ALU.mult).then_inc(made, 1)
            dve.wait_ge(made, 3)
            V.tensor_reduce(shift[:], grow[:, 0, :], AX.X, ALU.max, apply_absolute_value=True).then_inc(made, 1)
            dve.wait_ge(made, 4)
            V.tensor_scalar(shift[:], shift[:], XD ** 0.5, -HEADROOM, ALU.mult, ALU.add).then_inc(made, 1)
            dve.wait_ge(made, 5)
            V.tensor_scalar(shift[:], shift[:], 0.0, -1.0, ALU.max, ALU.mult).then_inc(made, 1)
            k = 0
            for _, t, w, dst in TURNED:
                for ch, cw in chunks(w):
                    dve.wait_ge(sems["weight_turned"], k + 1)
                    V.tensor_copy(dst[0:cw, ch, 0:t * P], SX(k)[0:cw, 0:t * P]).then_inc(sems["weight_copied"], 1)
                    k += 1
            dve.wait_ge(sems["weight_turned"], k + 1)
            V.tensor_scalar(hide[:], SX(k)[:, 0:B * CT], -1.0, -NEG, ALU.add, ALU.mult).then_inc(made, 1)
            dve.wait_ge(made, 7)
            dve.wait_ge(sems["halves_made"], 2)
            V.tensor_scalar(ctx_bias[:], hide[:], shift[:, 0:1], None, ALU.add).then_inc(sems["tables_made"], 1)
            dve.wait_ge(sems["tables_made"], 1)

            with dve.Fori(0, B) as b:
                g, o, n = [0], [0], [0]

                def took():
                    g[0] += 1
                    dve.wait_ge(g_ready.sem, g_ready.at(b, g[0]))
                    return G(g[0] - 1)

                def step(ins):
                    n[0] += 1
                    ins.then_inc(v_step.sem, 1)
                    dve.wait_ge(v_step.sem, v_step.at(b, n[0]))

                def variances(src, tiles, k):
                    for t in range(tiles):
                        last = V.bn_stats(stats[:, t, :], src[:, t, :])
                    step(last)
                    V.memset(vtick[:, min(k, 4) - 1:min(k, 4)], 0.0)
                    for t in range(tiles):
                        last = V.bn_aggr(mv[:, t, :], stats[:, t, :])
                    step(last)
                    V.tensor_scalar(var[:, 0:tiles], mv[:, 0:tiles, 1], EPS, None, ALU.add).then_inc(padded.sem, 1)
                    dve.wait_ge(powered.sem, powered.at(b, k))

                def normalise(dst, src, tiles, done):
                    for t in range(tiles):
                        last = V.tensor_scalar(dst[:, t, :], src[:, t, :], mv[:, t, 0:1], inv[:, t:t + 1],
                                               ALU.subtract, ALU.mult)
                    last.then_inc(done.sem, 1)

                def copied(dst, tiles=T, width=D, gain=None):
                    for ch, cw in chunks(width):
                        for t0 in range(0, tiles, 4):
                            w = min(4, tiles - t0) * P
                            src, to = took()[0:cw, 0:w], dst[0:cw, ch, t0 * P:t0 * P + w]
                            if gain is None:
                                ins = V.tensor_copy(to, src)
                            else:
                                ins = V.tensor_scalar(to, src, gain[0:cw, ch, 0:1], gain[0:cw, ch, 1:2],
                                                      ALU.mult, ALU.add)
                            ins.then_inc(g_taken.sem, 1)

                dve.wait_ge(turn_done.sem, turn_done.at(b, 0))
                dve.wait_ge(x_in.sem, x_in.at(b, 16))
                variances(xb, T, 1)
                normalise(xn, xb, T, normed)
                dve.wait_ge(normed.sem, normed.at(b, 1))
                dve.wait_ge(c_in.sem, c_in.at(b, 32))
                variances(cb[:, :, 0:DC], CT, 2)
                normalise(cb[:, :, 0:DC], cb[:, :, 0:DC], CT, c_normed)
                copied(xnT)
                for i, (n_, scale) in enumerate((("bq", HS ** -0.5), ("bk", 1.0))):
                    for oc in range(C):
                        V.tensor_scalar(qk[i][:, oc, :], took(), b_self[n_][:, oc:oc + 1], scale,
                                        ALU.add, ALU.mult).then_inc(g_taken.sem, 1)
                for t0 in range(0, T, 2):
                    src = took()
                    for t in range(t0, t0 + 2):
                        ins = V.tensor_tensor(v_self[:, t, :, 0:HS],
                                              src[:, (t - t0) * D:(t - t0 + 1) * D].rearrange("p (h d) -> p h d", h=H),
                                              spread["bv"][:].rearrange("p (h d) -> p h d", h=H), ALU.add)
                    ins.then_inc(g_taken.sem, 1)
                copied(cT, CT, gain=ln_x)
                for oc in range(C):
                    for t0 in range(0, SCP, 512):
                        w = min(512, SCP - t0)
                        V.tensor_copy(xk[:, oc, t0:t0 + w], took()[:, 0:w]).then_inc(g_taken.sem, 1)

                def values(first, tiles):
                    for t0 in range(0, tiles, 2):
                        w = min(2, tiles - t0)
                        V.tensor_copy(xv[:, first + t0:first + t0 + w, :, 0:XD],
                                      took()[:, 0:w * D].rearrange("p (t h d) -> p t h d", t=w, h=XH)
                                      ).then_inc(g_taken.sem, 1)
                values(0, CT)

                def largest(src, h, q, at_=0):
                    return V.tensor_reduce(nmax[:, h, q:q + 1], src[:, at_:at_ + (q + 1) * P], AX.X, ALU.max,
                                           negate=True)
                for h in range(0, H, 2):
                    for hh in (h, h + 1):
                        largest(took(), hh, 3).then_inc(g_taken.sem, 1)
                        src = took()
                        largest(src, hh, 2)
                        largest(src, hh, 0, 3 * P).then_inc(g_taken.sem, 1)
                    src = took()
                    largest(src, h, 1)
                    largest(src, h + 1, 1, 2 * P).then_inc(g_taken.sem, 1)
                V.tensor_copy(nmaxT[:], took()[0:H * T, 0:P]).then_inc(g_taken.sem, 1)

                def divided(heads, width, dst, used):
                    o[0] += 1
                    dve.wait_ge(pr_used.sem, pr_used.at(b, used))
                    sums = O(o[0] - 1)[:, 0:heads * T * (width + 1)].rearrange("p (m d) -> p m d", d=width + 1)
                    m = heads * T
                    if o[0] > 1:
                        dve.wait_ge(o_taken.sem, o_taken.at(b, o[0] - 1))
                    step(V.reciprocal(rec[:, 0:m], sums[:, :, width]))
                    V.tensor_tensor(dst, sums[:, :, 0:width].rearrange("p (h t) d -> p h t d", h=heads),
                                    rec[:, 0:m].rearrange("p (h t) -> p h t", h=heads).unsqueeze(3)
                                    .to_broadcast([P, heads, T, width]), ALU.mult).then_inc(o_taken.sem, 1)
                for q in range(H // 4):
                    divided(4, HS, at[:, :, q * 4 * HS:(q + 1) * 4 * HS].rearrange("p t (h d) -> p h t d", h=4), 2 * (q + 1))
                copied(atT)

                def add_residual():
                    for t0 in range(0, T, 2):
                        V.tensor_tensor(xb[:, t0:t0 + 2, :], took().rearrange("p (t d) -> p t d", t=2),
                                        xb[:, t0:t0 + 2, :], ALU.add).then_inc(g_taken.sem, 1)
                dve.wait_ge(xb_biased.sem, xb_biased.at(b, 1))
                add_residual()
                dve.wait_ge(g_taken.sem, g_taken.at(b, g[0]))

                variances(xb, T, 3)
                normalise(xn, xb, T, normed)
                copied(xnT, gain=ln_l)
                for t0 in range(0, T, 2):
                    V.tensor_copy(at[:, t0:t0 + 2, :], took().rearrange("p (t d) -> p t d", t=2)
                                  ).then_inc(g_taken.sem, 1)
                dve.wait_ge(g_taken.sem, g_taken.at(b, g[0]))
                step(V.tensor_tensor(xn[:], at[:], at[:], ALU.mult))
                step(V.tensor_reduce(q_ss[:], xn[:].rearrange("p t (h d) -> p (t h) d", h=XH), AX.X, ALU.add))
                V.tensor_scalar(q_ss[:], q_ss[:], 1.0 / XD, RMS_EPS ** 2, ALU.mult, ALU.max).then_inc(padded.sem, 1)
                for oc in range(C):
                    V.tensor_copy(xk[:, oc, SCP:], took()).then_inc(g_taken.sem, 1)
                values(CT, T)
                dve.wait_ge(powered.sem, powered.at(b, 4))
                V.tensor_tensor(at[:].rearrange("p t (h d) -> p (t h) d", h=XH),
                                at[:].rearrange("p t (h d) -> p (t h) d", h=XH),
                                q_inv[:].unsqueeze(2).to_broadcast([P, T * XH, XD]), ALU.mult).then_inc(q_normed.sem, 1)
                for ch in range(C):
                    src = took()
                    for h in range(2):
                        lo, hi = h * XD, (h + 1) * XD
                        ins = V.tensor_scalar(qz[lo:hi, 2 * ch + h, :], src[lo:hi, :], gqk[lo:hi, 0:1], None, ALU.mult)
                    ins.then_inc(g_taken.sem, 1)
                V.tensor_scalar(k_ss[:], took()[:, 0:KT * XH], 1.0 / XD, RMS_EPS ** 2, ALU.mult, ALU.max).then_inc(g_taken.sem, 1)
                for h in range(XH):
                    divided(1, XD, at[:, :, h * XD:(h + 1) * XD].unsqueeze(1), H // 2 + (h + 1) * KT)
                copied(atT)
                dve.wait_ge(xb_biased.sem, xb_biased.at(b, 2))
                add_residual()
                dve.wait_ge(g_taken.sem, g_taken.at(b, g[0]))

                variances(xb, T, 6)
                normalise(xn, xb, T, normed)
                copied(xnT)
                lg = took()[:, 0:T * E].rearrange("p (t e) -> p t e", t=T)
                wide = lambda x: x[:].unsqueeze(2).to_broadcast([P, T, E])
                step(V.tensor_reduce(c["mx"][:], lg, AX.X, ALU.max))
                V.tensor_tensor(r["lg"][:], lg, wide(c["mx"]), ALU.subtract).then_inc(g_taken.sem, 1)
                dve.wait_ge(ex_ready.sem, ex_ready.at(b, 1))
                step(V.tensor_reduce(c["sm"][:], r["ex"][:], AX.X, ALU.add))
                step(V.reciprocal(c["rc"][:], c["sm"][:]))
                step(V.tensor_tensor(r["pr"][:], r["ex"][:], wide(c["rc"]), ALU.mult))
                for k in range(2):
                    step(V.tensor_reduce(c[f"m{k}"][:], r["pr"][:], AX.X, ALU.max))
                    step(V.tensor_tensor(r["eq"][:], r["pr"][:], wide(c[f"m{k}"]), ALU.is_equal))
                    step(V.tensor_tensor(r["t"][:], r["eq"][:], rank[:], ALU.mult))
                    step(V.tensor_reduce(c[f"r{k}"][:], r["t"][:], AX.X, ALU.max))
                    step(V.tensor_tensor(r[f"oh{k}"][:], rank[:], wide(c[f"r{k}"]), ALU.is_equal))
                    if k == 0:
                        step(V.scalar_tensor_tensor(out=r["pr"][:], in0=r["oh0"][:], scalar=-2.0, in1=r["pr"][:],
                                                    op0=ALU.mult, op1=ALU.add))
                V.tensor_tensor(r["m"][:], r["oh0"][:], r["oh1"][:], ALU.add).then_inc(hot_ready.sem, 1)
                src = took()
                step(V.tensor_tensor(r["pos"][:], src[:, 0:T * E].rearrange("p (t e) -> p t e", t=T),
                                     carry[:].unsqueeze(1).to_broadcast([P, T, E]), ALU.add))
                V.tensor_tensor(carry[:], src[:, T * E:(T + 1) * E], carry[:], ALU.add).then_inc(g_taken.sem, 1)
                dve.wait_ge(g_taken.sem, g_taken.at(b, g[0]))
                step(V.tensor_tensor(c["sm"][:], c["m0"][:], c["m1"][:], ALU.add))
                step(V.reciprocal(c["rc"][:], c["sm"][:]))
                for k in range(2):
                    p_, k_, b_, f_ = (c[f"{x}{k}"] for x in "pkbf")
                    step(V.tensor_tensor(r["t"][:], r["pos"][:], r[f"oh{k}"][:], ALU.mult))
                    step(V.tensor_reduce(p_[:], r["t"][:], AX.X, ALU.add))
                    step(V.tensor_scalar(k_[:], p_[:], float(CAP), None, ALU.is_lt))
                    step(V.tensor_scalar(b_[:], c[f"r{k}"][:], -float(CAP), float(E * CAP), ALU.mult, ALU.add))
                    step(V.tensor_tensor(p_[:], p_[:], k_[:], ALU.mult))
                    step(V.tensor_tensor(p_[:], p_[:], b_[:], ALU.add))
                    step(V.tensor_copy(kept["gather_at"][:, ds(b, 1), k, :], p_[:].unsqueeze(1)))
                    step(V.tensor_scalar(f_[:], k_[:], -FAR, FAR, ALU.mult, ALU.add))
                    step(V.tensor_tensor(f_[:], f_[:], p_[:], ALU.add))
                    step(V.tensor_copy(slot[k][:], f_[:]))
                    step(V.tensor_tensor(f_[:], c[f"m{k}"][:], c["rc"][:], ALU.mult))
                    V.tensor_tensor(kept["gates"][:, ds(b, 1), k, :], f_[:].unsqueeze(1), k_[:].unsqueeze(1),
                                    ALU.mult).then_inc(slots_ready.sem, 1)
                    dve.wait_ge(slots_ready.sem, slots_ready.at(b, k + 1))
                assert (g[0], o[0], n[0]) == (NGU, NOU, v_step.per), (g, o, n)


def experts_and_combine(nc, a, kept, scratch, out):
    with ExitStack() as ctx:
        sb = lambda n, s, d=F32: ctx.enter_context(nc.sbuf_tensor(n, s, d))
        sem = lambda n: ctx.enter_context(nc.semaphore(n))
        ident = kept["ident"]
        HALF = CAP // 2
        w1 = [sb(f"w1_{i}", [P, C, HID]) for i in range(2)]
        w2 = [sb(f"w2_{i}", [P, HC, D]) for i in range(2)]
        b1 = [sb(f"b1_{i}", [P, HC]) for i in range(2)]
        b1_rows = sb("b1_rows", [E * HC, P])
        b1T = sb("b1T", [P, E * HC])
        b2 = [sb(f"b2_{i}", [P, D]) for i in range(2)]
        xe = [sb(f"xe_{i}", [P, ST, D]) for i in range(2)]
        xeT = [sb(f"xeT_{i}", [P, C, CAP]) for i in range(2)]
        hT = [sb(f"hT_{i}", [P, HC, CAP]) for i in range(2)]
        oe = [sb(f"oe_{i}", [P, ST, D]) for i in range(2)]
        rows_at = [sb(f"rows_at_{i}", [P, 2, T], U32) for i in range(2)]
        gate = [sb(f"gate_{i}", [P, 2, T]) for i in range(2)]
        tick = sb("tick2", [1, 9])
        y = [sb(f"y_{i}", [P, 2, T, D]) for i in range(2)]
        res = [sb(f"res_{i}", [P, T, D]) for i in range(2)]
        psum = ctx.enter_context(nc.psum_tensor("psum2", [P, 8, 512], F32))
        NR = 4
        G = lambda i: psum[:, i % NR, :]
        A = lambda i: psum[:, NR + i % NR, :]
        GX, GO, GA = 2 * C, ST // 2, HC * 2

        C_ = lambda n, per, before=0: Count(sem(n), per, before)
        loaded = [C_(f"weights_in_{i}", 4 * 16) for i in range(2)]
        g_ready, g_taken = C_("ffn_product_ready", 2 * (GX + GO)), C_("ffn_product_taken", 2 * (GX + GO), 1)
        h_ready, h_done = C_("hidden_ready", 2 * GA), C_("hidden_done", 2 * GA, 1)
        stored = [C_(f"expert_rows_stored_{i}", 16, 1) for i in range(2)]
        copied_ = C_("indices_copied", 2 * 2)
        gathered = [C_(f"rows_gathered_{i}", 2 * T * 16) for i in range(2)]
        res_in = [C_(f"residual_in_{i}", 16) for i in range(2)]
        added = C_("rows_added", 2 * 2, 1)
        out_done = [C_(f"output_stored_{i}", 16, 1) for i in range(2)]
        b1_in, b1_turned, b1_kept = sem("b1_loaded"), sem("b1_turned"), sem("b1_kept")
        b1_here = C_("b1_copied", 2)
        block = ctx.enter_context(nc.Block())

        @block.sync
        def _(sp):
            sp.dma_start(b1_rows[:], a["L0_ffn_b1"].rearrange("e (c p) -> (e c) p", p=P)).then_inc(b1_in, 16)
            with sp.Fori(0, E // 2) as i:
                for j in range(2):
                    e = 2 * i + j
                    sp.wait_ge(stored[j].sem, stored[j].at(i, 0))
                    row = lambda x: x[ds(e, 1), :]
                    sp.dma_start(xe[j][:], scratch["expert_in"][ds(e * CAP, CAP), :]
                                 .rearrange("(t p) d -> p t d", p=P)).then_inc(loaded[j].sem, 16)
                    sp.dma_start(w1[j][:], a["L0_ffn_w1"][ds(e, 1), :, :].rearrange("a (c p) n -> p (a c) n", p=P)
                                 ).then_inc(loaded[j].sem, 16)
                    sp.dma_start(w2[j][:], a["L0_ffn_w2"][ds(e, 1), :, :].rearrange("a (c p) n -> p (a c) n", p=P)
                                 ).then_inc(loaded[j].sem, 16)
                    sp.dma_start(b2[j][:], row(a["L0_ffn_b2"]).rearrange("a n -> (a n)").partition_broadcast(P)
                                 ).then_inc(loaded[j].sem, 16)
            with sp.Fori(0, B // 2) as i:
                for j in range(2):
                    sp.wait_ge(out_done[j].sem, out_done[j].at(i, 0))
                    sp.dma_start(res[j][:], scratch["resid"][ds(2 * i + j, 1), :, :]
                                 .rearrange("a (t p) d -> p (a t) d", p=P)).then_inc(res_in[j].sem, 16)

        @block.scalar
        def _(act):
            act.wait_ge(b1_turned, 1)
            nc.scalar.activation(b1T[:], A(0)[:, 0:E * HC], ACT.Copy).then_inc(b1_kept, 1)
            act.wait_ge(b1_kept, 1)
            with act.Fori(0, E // 2) as i:
                n = 0
                for j in range(2):
                    nc.scalar.activation(b1[j][:], b1T[:, ds((2 * i + j) * HC, HC)], ACT.Copy).then_inc(b1_here.sem, 1)
                    act.wait_ge(b1_here.sem, b1_here.at(i, j + 1))
                    act.wait_ge(loaded[j].sem, loaded[j].at(i, 4 * 16))
                    for hc in range(HC):
                        for half in range(2):
                            act.wait_ge(h_ready.sem, h_ready.at(i, n + 1))
                            nc.scalar.activation(hT[j][:, hc, half * HALF:(half + 1) * HALF], A(n)[:, 0:HALF],
                                                 ACT.Relu, bias=b1[j][:, hc:hc + 1]).then_inc(h_done.sem, 1)
                            n += 1
                    act.wait_ge(g_taken.sem, g_taken.at(i, (j + 1) * (GX + GO)))
                    act.dma_start(scratch["expert_out"][ds((2 * i + j) * CAP, CAP), :]
                                  .rearrange("(t p) d -> p t d", p=P), oe[j][:]).then_inc(stored[j].sem, 16)
            for j in range(2):
                act.wait_ge(stored[j].sem, stored[j].at(E // 2, 0))
            with act.Fori(0, B // 2) as i:
                for j in range(2):
                    act.wait_ge(added.sem, added.at(i, 2 * j + 2))
                    act.dma_start(out[ds(2 * i + j, 1), :, :].rearrange("a (t p) d -> p (a t) d", p=P), res[j][:]
                                  ).then_inc(out_done[j].sem, 16)
            for j in range(2):
                act.wait_ge(out_done[j].sem, out_done[j].at(B // 2, 0))

        @block.tensor
        def _(pe):
            mm = nc.tensor.matmul
            pe.wait_ge(b1_in, 16)
            nc.tensor.transpose(A(0)[:, 0:E * HC], b1_rows[:], ident[0:E * HC, 0:E * HC]).then_inc(b1_turned, 1)
            pe.wait_ge(b1_kept, 1)
            with pe.Fori(0, E // 2) as i:
                g, n = [0], 0

                def bank():
                    g[0] += 1
                    if g[0] > NR:
                        pe.wait_ge(g_taken.sem, g_taken.at(i, g[0] - NR))
                    else:
                        pe.wait_ge(g_taken.sem, g_taken.at(i, 0))
                    return G(g[0] - 1)

                for j in range(2):
                    pe.wait_ge(loaded[j].sem, loaded[j].at(i, 4 * 16))
                    for ch in range(C):
                        for half in range(2):
                            dst = bank()
                            for t in range(ST // 2):
                                last = nc.tensor.transpose(dst[:, t * P:(t + 1) * P],
                                                           xe[j][:, half * (ST // 2) + t, ch * P:(ch + 1) * P], ident[:])
                            last.then_inc(g_ready.sem, 1)
                    pe.wait_ge(g_taken.sem, g_taken.at(i, g[0]))
                    for hc in range(HC):
                        for half in range(2):
                            pe.wait_ge(h_done.sem, h_done.at(i, max(n + 1 - NR, 0)))
                            for ch in range(C):
                                last = mm(A(n)[:, 0:HALF], w1[j][:, ch, hc * P:(hc + 1) * P],
                                          xeT[j][:, ch, half * HALF:(half + 1) * HALF], start=ch == 0, stop=ch == C - 1)
                            last.then_inc(h_ready.sem, 1)
                            n += 1
                    for t in range(ST):
                        if t % 2 == 0:
                            dst = bank()
                        if t == 0:
                            pe.wait_ge(h_done.sem, h_done.at(i, n))
                        for hc in range(HC):
                            last = mm(dst[:, t % 2 * D:(t % 2 + 1) * D], hT[j][:, hc, t * P:(t + 1) * P], w2[j][:, hc, :],
                                      start=hc == 0, stop=hc == HC - 1)
                        if t % 2:
                            last.then_inc(g_ready.sem, 1)

        @block.vector
        def _(dve):
            V = nc.vector
            with dve.Fori(0, E // 2) as i:
                g = [0]

                def took():
                    g[0] += 1
                    dve.wait_ge(g_ready.sem, g_ready.at(i, g[0]))
                    return G(g[0] - 1)

                for j in range(2):
                    for ch in range(C):
                        for half in range(2):
                            V.tensor_copy(xeT[j][:, ch, half * HALF:(half + 1) * HALF], took()[:, 0:HALF]
                                          ).then_inc(g_taken.sem, 1)
                    dve.wait_ge(loaded[j].sem, loaded[j].at(i, 4 * 16))
                    dve.wait_ge(stored[j].sem, stored[j].at(i, 0))
                    for t in range(0, ST, 2):
                        V.tensor_tensor(oe[j][:, t:t + 2, :], took().rearrange("p (t d) -> p t d", t=2),
                                        b2[j][:].unsqueeze(1).to_broadcast([P, 2, D]), ALU.add).then_inc(g_taken.sem, 1)
            with dve.Fori(0, B // 2) as i:
                for j in range(2):
                    dve.wait_ge(gathered[j].sem, gathered[j].at(i, 2 * T * 16))
                    dve.wait_ge(res_in[j].sem, res_in[j].at(i, 16))
                    dve.wait_ge(copied_.sem, copied_.at(i, 2 * j + 2))
                    for k in range(2):
                        for t in range(T):
                            last = V.scalar_tensor_tensor(out=res[j][:, t, :], in0=y[j][:, k, t, :],
                                                          scalar=gate[j][:, k, t:t + 1], in1=res[j][:, t, :],
                                                          op0=ALU.mult, op1=ALU.add)
                        last.then_inc(added.sem, 1)
                        dve.wait_ge(added.sem, added.at(i, 2 * j + k + 1))

        @block.gpsimd
        def _(pool):
            for i, x in enumerate((g_taken, h_done, *stored, added, *out_done)):
                nc.gpsimd.memset(tick[:, 2 + i:3 + i], 0.0).then_inc(x.sem, 1)
            for j in range(2):
                pool.wait_ge(stored[j].sem, stored[j].at(E // 2, 0))
            with pool.Fori(0, B // 2) as i:
                for j in range(2):
                    pool.wait_ge(added.sem, added.at(i, 0))
                    nc.gpsimd.tensor_copy(rows_at[j][:].unsqueeze(1), kept["gather_at"][:, ds(2 * i + j, 1), :, :]
                                          ).then_inc(copied_.sem, 1)
                    nc.gpsimd.tensor_copy(gate[j][:].unsqueeze(1), kept["gates"][:, ds(2 * i + j, 1), :, :]
                                          ).then_inc(copied_.sem, 1)
                    pool.wait_ge(copied_.sem, copied_.at(i, 2 * j + 2))
                    nc.gpsimd.tensor_tensor(tick[:, j:j + 1], ident[0:1, 0:1], ident[0:1, 0:1], ALU.add)
                    for k in range(2):
                        for t in range(T):
                            nc.gpsimd.indirect_dma_start(
                                y[j][:, k, t, :], None, scratch["expert_out"],
                                bass.IndirectOffsetOnAxis(rows_at[j][:, k, t:t + 1], 0),
                                bounds_check=E * CAP - 1, oob_is_err=False).then_inc(gathered[j].sem, 16)


_INS = ["x", "ctx_768", "mask_BxS2_bk0", "L0_attn_Wq", "L0_attn_bq", "L0_attn_Wk", "L0_attn_bk", "L0_attn_Wv",
        "L0_attn_bv", "L0_attn_Wm", "L0_attn_bm", "L0_xattn_ln_x_g", "L0_xattn_ln_x_b", "L0_xattn_ln_l_g",
        "L0_xattn_ln_l_b", "L0_xattn_qn_g", "L0_xattn_kn_g", "L0_xattn_Wq", "L0_xattn_Wkv", "L0_xattn_Wlkv",
        "L0_xattn_Wo", "L0_xattn_bo", "L0_ffn_w_router", "L0_ffn_w1", "L0_ffn_b1", "L0_ffn_w2", "L0_ffn_b2"]


def kernel(**inputs):
    import numpy as _np
    import concourse.bacc as _bacc
    from concourse import mybir as _mybir
    from concourse.bass_utils import run_bass_kernel_spmd as _run

    nc = _bacc.Bacc("TRN2", target_bir_lowering=False, num_devices=1)
    arrays, a = {}, {}
    for name in _INS:
        x = _np.ascontiguousarray(inputs[name])
        arrays[f"in_{name}"] = x
        a[name] = nc.dram_tensor(f"in_{name}", x.shape, _mybir.dt.from_np(x.dtype), kind="ExternalInput").ap()
    out = nc.dram_tensor("out", (B, S, D), F32, kind="ExternalOutput").ap()
    decoder(nc, a, out)
    r = _run(nc, [arrays], core_ids=[0])
    return r.results[0]["out"]
```

```python
from contextlib import ExitStack

import concourse.bass as bass
from concourse import mybir

ALU = mybir.AluOpType
ACT = mybir.ActivationFunctionType
F32 = mybir.dt.float32
BF16 = mybir.dt.bfloat16
U32 = mybir.dt.uint32
U8 = mybir.dt.uint8
AX = mybir.AxisListType
ds = bass.ds

P = 128
B, S, D = 8, 512, 256
C = D // P
T = S // P
H, HS = 16, 16
SC, DC = 1601, 192
CT = -(-SC // P)
SCP = CT * P
KT = CT + T
XH, XD = 4, 64
E, HID, CAP = 8, 1024, 768
ST = CAP // P
HC = HID // P
EPS, RMS_EPS = 1e-5, 1e-8
NEG = -1e30
HEADROOM = 70.0
FAR = 1.0e6

Q_PARTS = [0, 0, 0, 1, 1, 2]
K_PARTS = [0, 1, 2, 0, 1, 0]
NPART = len(Q_PARTS)
MAXROW = NPART * HS

MADE = 35
DVE_STEPS = {"s": 10, "x": 48}
POOL_STEPS = 5

FIRST, BOTH, LAST = "first", "both", "last"
STAGES = {FIRST: "s", BOTH: "sx", LAST: "x"}
NXU = XH * KT
NSU = H // 2 * 5
AHEAD = 3
HEAD_ROWS = 32
HEADS_UP = P // HEAD_ROWS
NG, NS = 2, 4
NPS, NPX = 10, 5


def steps(kind):
    plan = []

    def put(at_, name, i=0):
        plan.append((at_, name, i))

    head_ = [("x_base", 0), ("load", 0), ("c_k", 0), ("l_T", 0), ("l_k", 0), ("s_stats", 0), ("l_q", 0), ("s_norm", 0),
             ("l_ss", 0), ("s_T", 0), ("s_q", 0), ("s_q", 1), ("l_ss", 1), ("l_v", 0), ("s_rest", 0), ("s_rest", 1),
             ("s_v", 0), ("s_parts", 0), ("s_parts", 1), ("l_qT", 0), ("c_v", 0)]
    for k, (name, i) in enumerate(head_):
        put(k - 100, name, i)
    for u in range(-AHEAD, NXU):
        if u + AHEAD < NXU:
            put(u, "x_scores", u + AHEAD)
        if u >= 0:
            put(u + 0.1, "x_sums", u)
    for k, name in enumerate(("sc_stats", "sc_norm", "sc_T")):
        put(CONTEXT_AT + CONTEXT_PACE * k, name)
    for i in range(NSU):
        put(MAX_AT + i * MAX_PACE, "s_max", i)
    put(MAX_AT + NSU * MAX_PACE, "s_maxT")
    for i in range(NSU):
        put(SCORES_AT + i * SCORES_PACE, "s_scores", i)
    for p in range(H // 2):
        put(SCORES_AT + (5 * p + 4) * SCORES_PACE + SUMS_LAG, "s_sums", p)
    for k in range(H // HEADS_UP):
        put(SCORES_AT + (10 * k + 9) * SCORES_PACE + SUMS_LAG + HEAD_LAG, "s_head", k)
    for h in range(XH):
        put((h + 1) * KT - 1 + HEAD_LAG, "x_head", h)
    for k, name in enumerate(("x_T", "x_out", "r_stats", "r_norm", "r_T", "r_logits", "r_best", "r_places")):
        put(NXU + 1 + TAIL_PACE * k, name)
    for k, name in enumerate(("s_outT", "s_out", "sl_stats", "sl_norm")):
        put(200 + k, name)
    order = sorted(plan, key=lambda x: x[0])
    return [(name, i) for _, name, i in order if ("s" if name[0] == "s" or name == "load" else "x") in STAGES[kind]]


CONTEXT_AT, CONTEXT_PACE = 1.2, 3.0
MAX_AT, MAX_PACE = 6.5, 0.5
SCORES_AT, SCORES_PACE, SUMS_LAG = 33.5, 1.2, 3.0
HEAD_LAG, TAIL_PACE = 1.0, 1.5
PRODUCTS = {"l_T": C, "sc_T": C * -(-CT // 4), "l_q": T // 2, "l_k": C, "l_v": T // 2, "s_T": C, "s_q": C, "s_v": T // 2,
            "c_k": C * -(-SCP // 512), "l_qT": C, "c_v": -(-CT // 2), "l_ss": 1, "s_max": 1, "s_maxT": 1, "x_T": C, "s_head": 1, "x_head": 1,
            "x_out": T // 2, "r_T": C, "r_logits": 1, "r_places": 1, "s_outT": C, "s_out": T // 2}
SCORES = {"x_scores": 1, "s_scores": 1}


def placed(banks):
    after, total = {}, {}
    for kind in (FIRST, BOTH, LAST):
        n, after[kind] = 0, {}
        for step in steps(kind):
            n += banks.get(step[0], 0)
            after[kind][step] = n
        total[kind] = n
    return after, total


class Section:

    def __init__(self, kind, turn):
        self.kind, self.turn = kind, turn
        self.s = (turn, 1 if kind == BOTH else 0)
        self.x = (turn, 0)
        self.steps = steps(kind)


def sections(engine):
    yield Section(FIRST, 0)
    with engine.Fori(0, B - 1) as turn:
        yield Section(BOTH, turn)
    yield Section(LAST, B - 1)


def rows(element):
    turn, plus = element
    return ds(turn + plus, 1)


class Count:

    def __init__(self, sem, per, before=0):
        self.sem, self.per, self.before = sem, per, before

    def at(self, turn, k):
        return turn * self.per + (self.before + k)

    def of(self, element, k):
        turn, plus = element
        return turn * self.per + (self.before + plus * self.per + k)


class Tally:

    def __init__(self, sem, total):
        self.sem, self.total = sem, total

    def at(self, sec, k):
        if sec.kind == FIRST:
            return k
        return sec.turn * self.total[BOTH] + (self.total[FIRST] + k)


def decoder(nc, a, out):
    with ExitStack() as ctx:
        dram = lambda n, s, d: nc.dram_tensor(n, s, d, kind="Internal").ap()
        scratch = {
            "expert_in": dram("expert_in", (E * CAP, D), F32),
            "expert_out": dram("expert_out", (E * CAP, D), F32),
            "resid": dram("resid", (B, S, D), F32),
            "parts": dram("parts", (2, 3, D, S), BF16),
            "maxima": dram("maxima", (H * T, P), BF16),
        }
        kept = {n: ctx.enter_context(nc.sbuf_tensor(n, s, d)) for n, s, d in (
            ("gates", [P, B, 2, T], F32), ("gather_at", [P, B, 2, T], U32), ("ident", [P, P], F32))}
        attention_and_routing(nc, a, kept, scratch)
        experts_and_combine(nc, a, kept, scratch, out)


def attention_and_routing(nc, a, kept, scratch):
    with ExitStack() as ctx:
        sb = lambda n, s, d=F32: ctx.enter_context(nc.sbuf_tensor(n, s, d))
        sem = lambda n: ctx.enter_context(nc.semaphore(n))
        ident = kept["ident"]

        identb = sb("identb", [P, P], BF16)
        hide_kq = sb("hide_kq", [P, P], BF16)
        hide_qk = sb("hide_qk", [P, P], BF16)
        before = sb("before", [P, P])
        ones = sb("ones", [P, P])
        halves = sb("halves", [P, 2])
        minus_half = sb("minus_half", [P, KT * XH])
        eps = sb("eps", [P, T])
        rank = sb("rank", [P, T, E])
        w_self = {n: sb("w_" + n, [P, C, D]) for n in ("Wq", "Wk", "Wv", "Wm")}
        b_self = {n: sb("b_" + n, [P, C]) for n in ("bq", "bk")}
        spread = {n: sb("s_" + n, [P, D]) for n in ("bv", "bm", "bo")}
        xwqT = sb("xwqT", [P, C, D])
        xwoT = sb("xwoT", [P, C, D])
        xwlT = sb("xwlT", [P, C, 2 * D])
        xwcT = sb("xwcT", [P, C, 2 * D])
        router = sb("router", [P, C, E])
        ln_x = sb("ln_x", [P, C, 2])
        ln_l = sb("ln_l", [P, C, 2])
        gcol = sb("gcol", [P, 2])
        grow = sb("grow", [P, 2, XD])
        gqk = sb("gqk", [P, 1])
        shift = sb("shift", [P, 1])
        mask8 = sb("mask8", [B * CT, P], U8)
        maskf = sb("maskf", [B * CT, P])
        hide = sb("hide", [P, B * CT])
        ctx_bias = sb("ctx_bias", [P, B * CT])

        xs = sb("xs", [P, T, D])
        xx = sb("xx", [P, T, D])
        xn_s, xn_x = sb("xn_s", [P, T, D]), sb("xn_x", [P, T, D])
        xnT_s, xnT_x = sb("xnT_s", [P, C, S]), sb("xnT_x", [P, C, S])
        at_s, at_x = sb("at_s", [P, T, D]), sb("at_x", [P, T, D])
        stats = sb("stats", [P, CT, 6])
        tiles_of = {"s": T, "l": T, "c": CT, "r": T}
        mv = {n: sb("mv_" + n, [P, t, 2]) for n, t in tiles_of.items()}
        var = {n: sb("var_" + n, [P, t]) for n, t in tiles_of.items()}
        inv = {n: sb("inv_" + n, [P, t]) for n, t in tiles_of.items()}
        inv2 = sb("inv2", [P, T])
        stack = [sb("q_stack", [P, H, S], BF16), sb("k_stack", [P, H, S], BF16)]
        v_self = sb("v_self", [P, T, H, HEAD_ROWS])
        cb = sb("cb", [P, CT, D])
        cT = sb("cT", [P, C, SCP])
        xk = sb("xk", [P, C, KT * P])
        raw = cT[:].rearrange("p c s -> p (c s)")[:, 0:4 * D].rearrange("p (t d) -> p t d", t=4)
        xv = sb("xv", [P, KT, XH, XD + 1])
        k_ss = sb("k_ss", [P, KT * XH])
        k_inv = sb("k_inv", [P, KT * XH])
        key_bias = sb("key_bias", [P, KT])
        nmax_pad = sb("nmax", [P, P])
        nmax = nmax_pad[:, 0:H * T].rearrange("p (h t) -> p h t", h=H)
        nmaxT = sb("nmaxT", [H * T, P], BF16)
        pr_s = sb("pr_s", [P, NPS, S])
        pr_x = sb("pr_x", [P, NPX, S])
        xk2 = pr_x[:].rearrange("p n s -> p (n s)")[:, 0:KT * P]
        pr_flat = pr_s[:].rearrange("p n s -> p (n s)")
        pair = lambda x: x.rearrange("p (c s) -> p c s", c=C)
        qk = [pair(pr_flat[:, i * C * S:(i + 1) * C * S]) for i in range(2)]
        part_flat = pr_flat[:, 2 * C * S:].bitcast(BF16)
        part = [part_flat[:, i * 3 * C * S:(i + 1) * 3 * C * S].rearrange("p (j c s) -> p j c s", j=3, c=C)
                for i in range(2)]
        rest = [pair(x[:].rearrange("p t d -> p (t d)")) for x in (at_s, xn_s)]
        rec = {"s": sb("rec_s", [P, T * HEADS_UP]), "x": sb("rec_x", [P, T])}
        sumT_s, sumT_x = sb("sumT_s", [P, S]), sb("sumT_x", [P, S])
        qz = sb("qz", [P, XH, S])
        q_ss = sb("q_ss", [P, T * XH])
        q_inv = sb("q_inv", [P, T * XH])
        carry = sb("carry", [P, E])
        r = {n: sb("r_" + n, [P, T, E]) for n in ("lg", "ex", "pr", "eq", "oh0", "oh1", "m", "pos", "t")}
        c = {n: sb("c_" + n, [P, T]) for n in ("mx", "sm", "rc", "m0", "m1", "r0", "r1", "p0", "p1",
                                               "k0", "k1", "b0", "b1", "f0", "f1")}
        slot = [sb(f"slot{i}", [P, T], U32) for i in range(2)]
        tick = sb("tick", [1, 16])
        vtick = sb("vtick", [1, 4])

        psum = ctx.enter_context(nc.psum_tensor("psum", [P, 8, 512], F32))
        G = lambda i: psum[:, i % NG, :]
        O = {"s": psum[:, NG, :], "x": psum[:, NG + 1, :]}
        SX = lambda i: psum[:, NG + 2 + i % NS, :]

        TOOK, n_products = placed(PRODUCTS)
        SCORED, n_scores = placed(SCORES)
        sems = {n: sem(n) for n in (
            "weights_loaded", "raw_loaded", "constants_made", "weight_turned", "weight_copied", "setup_step",
            "slots_cleared", "tables_made", "halves_made")}
        g_ready, g_taken = Tally(sem("product_ready"), n_products), Tally(sem("product_taken"), n_products)
        s_ready, s_done = Tally(sem("scores_ready"), n_scores), Tally(sem("exps_done"), n_scores)
        v_step = Tally(sem("vector_step"), {k: sum(DVE_STEPS[x] for x in st) for k, st in STAGES.items()})
        C_ = lambda n, per, before=0: Count(sem(n), per, before)
        x_in, c_in = C_("x_loaded", 16), C_("context_loaded", 32)
        normed = {n: C_(f"normed_{n}", 1) for n in tiles_of}
        padded = {n: C_(f"variance_padded_{n}", 1) for n in tiles_of}
        powered = {n: C_(f"inverse_ready_{n}", 1) for n in tiles_of}
        q_padded, q_powered = C_("query_squares_ready", 1), C_("query_inverse_ready", 1)
        k_powered = C_("key_inverse_ready", C)
        xs_biased, xx_made = C_("self_bias_added", 1), C_("cross_bias_added", 1)
        rounded = C_("parts_rounded", 4)
        rested = C_("rests_made", 4)
        stored = C_("parts_stored", 6 * 16)
        stacked = C_("parts_stacked", 2 * NPART * 16)
        max_out, max_in = C_("maxima_stored", 16), C_("maxima_placed", 16)
        used = {"s": C_("self_probs_used", H // 2), "x": C_("cross_probs_used", NXU)}
        o_taken = {"s": C_("self_sums_taken", H // 4), "x": C_("cross_sums_taken", XH)}
        kb_ready = C_("key_bias_ready", 1)
        sq_ready = C_("key_squares_made", C)
        q_normed = C_("queries_normed", 1)
        x2_out = C_("residual_stored", 16, 1)
        ex_ready = C_("logit_exps_ready", 1)
        hot_ready = C_("choices_ready", 1)
        p_step = C_("pool_step", POOL_STEPS)
        slots_ready, scattered = C_("slots_ready", 2), C_("rows_scattered", 2 * T * 16)
        rows_free = C_("rows_free", 1, 1)

        block = ctx.enter_context(nc.Block())
        full, left = SC // P, SC % P
        LOADS = []
        for n in ("Wq", "Wk", "Wv", "Wm"):
            LOADS.append((w_self[n][:], a["L0_attn_" + n].rearrange("(c p) n -> p c n", p=P)))
        for n in ("bq", "bk"):
            LOADS.append((b_self[n][:], a["L0_attn_" + n].rearrange("(c p) -> p c", p=P)))
        for n, src in (("bv", "L0_attn_bv"), ("bm", "L0_attn_bm"), ("bo", "L0_xattn_bo")):
            LOADS.append((spread[n][:], a[src].partition_broadcast(P)))
        LOADS.append((router[:], a["L0_ffn_w_router"].rearrange("(c p) n -> p c n", p=P)))
        for i, n in enumerate(("g", "b")):
            LOADS.append((ln_l[:, :, i], a["L0_xattn_ln_l_" + n].rearrange("(c p) -> p c", p=P)))
            v = a["L0_xattn_ln_x_" + n].rearrange("(p a) -> p a", a=1)
            LOADS.append((ln_x[:, 0, i:i + 1], v[0:P, :]))
            LOADS.append((ln_x[0:DC - P, 1, i:i + 1], v[P:DC, :]))
        for i, n in enumerate(("qn_g", "kn_g")):
            v = a["L0_xattn_" + n]
            LOADS.append((grow[:, i, :], v.partition_broadcast(P)))
            for h in range(2):
                LOADS.append((gcol[h * XD:(h + 1) * XD, i:i + 1], v.rearrange("(p a) -> p a", a=1)))
        for b in range(B):
            m = a["mask_BxS2_bk0"][b, :]
            LOADS.append((mask8[b * CT:b * CT + full, :], m[0:full * P].rearrange("(t p) -> t p", p=P)))
            LOADS.append((mask8[b * CT + full:b * CT + full + 1, 0:left],
                          m[full * P:SC].rearrange("(a p) -> a p", a=1)))
        TURNED = [("Wq", 2, D, xwqT), ("Wo", 2, D, xwoT), ("Wlkv", 4, D, xwlT), ("Wkv", 4, DC, xwcT)]
        chunks = lambda w: [(k, min(P, w - k * P)) for k in range(-(-w // P))]

        @block.sync
        def _(sp):
            sp.wait_ge(sems["constants_made"], 4)
            for dst, src in LOADS:
                sp.dma_start(dst, src, allow_slow_non_contiguous=True).then_inc(sems["weights_loaded"], 16)
            for i, (n, t, w, _) in enumerate(TURNED):
                if i:
                    sp.wait_ge(sems["weight_turned"], C * i)
                sp.dma_start(raw[:, 0:t, 0:w], a["L0_xattn_" + n].rearrange("(t p) n -> p t n", p=P)
                             ).then_inc(sems["raw_loaded"], 16)
            for sec in sections(sp):
                for name, i in sec.steps:
                    if name == "load":
                        if sec.kind == BOTH:
                            sp.wait_ge(xx_made.sem, xx_made.of(sec.x, 1))
                            sp.wait_ge(normed["l"].sem, normed["l"].of(sec.x, 1))
                        sp.dma_start(xs[:], a["x"][rows(sec.s), :, :].rearrange("a (t p) d -> p (a t) d", p=P)
                                     ).then_inc(x_in.sem, 16)
                        sp.dma_start(cb[:, 0:full, 0:DC], a["ctx_768"][rows(sec.s), 0:full * P, :]
                                     .rearrange("a (t p) d -> p (a t) d", p=P)).then_inc(c_in.sem, 16)
                        sp.dma_start(cb[0:left, full, 0:DC], a["ctx_768"][rows(sec.s), full * P:SC, :]
                                     .rearrange("a p d -> (a p) d")).then_inc(c_in.sem, 16)
                    elif name == "s_parts" and i == 1:
                        for j in range(3):
                            for qk_ in range(2):
                                if j < 2:
                                    sp.wait_ge(rounded.sem, rounded.of(sec.s, 2 * j + qk_ + 1))
                                else:
                                    sp.wait_ge(rested.sem, rested.of(sec.s, 2 + qk_ + 1))
                                sp.dma_start(scratch["parts"][qk_, j, :, :].rearrange("(c p) s -> p c s", p=P),
                                             part[qk_][:, j, :, :]).then_inc(stored.sem, 16)
                        sp.wait_ge(stored.sem, stored.of(sec.s, 6 * 16))
                        for qk_, order in enumerate((Q_PARTS, K_PARTS)):
                            for j, p in enumerate(order):
                                sp.dma_start(stack[qk_][j * HS:(j + 1) * HS, :, :],
                                             scratch["parts"][qk_, p, :, :].rearrange("(h d) s -> d h s", d=HS)
                                             ).then_inc(stacked.sem, 16)
                    elif name == "s_maxT":
                        sp.wait_ge(g_taken.sem, g_taken.at(sec, TOOK[sec.kind][name, i]))
                        sp.dma_start(scratch["maxima"], nmaxT[:]).then_inc(max_out.sem, 16)
                        sp.wait_ge(max_out.sem, max_out.of(sec.s, 16))
                        sp.dma_start(stack[0][MAXROW:MAXROW + 1, :, :], scratch["maxima"]
                                     .rearrange("(a h t) p -> a h (t p)", a=1, h=H)).then_inc(max_in.sem, 16)
                    elif name == "r_stats":
                        sp.wait_ge(g_taken.sem, g_taken.at(sec, TOOK[sec.kind]["x_out", 0]))
                        sp.dma_start(scratch["resid"][rows(sec.x), :, :].rearrange("a (t p) d -> p (a t) d", p=P),
                                     xx[:]).then_inc(x2_out.sem, 16)
            sp.wait_ge(x2_out.sem, x2_out.at(B, 0))

        @block.gpsimd
        def _(pool):
            made = sems["constants_made"]
            nc.gpsimd.memset(mask8[:], 0).then_inc(made, 1)
            nc.gpsimd.memset(cb[:], 0.0).then_inc(made, 1)
            nc.gpsimd.memset(xn_x[:], 0.0).then_inc(made, 1)
            nc.gpsimd.memset(ln_x[:], 0.0).then_inc(made, 1)
            nc.gpsimd.memset(xwcT[:], 0.0).then_inc(made, 1)
            nc.gpsimd.memset(nmax_pad[:], 0.0).then_inc(made, 1)
            zero_in = [(ident, ALU.not_equal, 1.0, 0.0, -1), (identb, ALU.not_equal, 1.0, 0.0, -1),
                       (hide_kq, ALU.is_ge, NEG, 0.0, 1), (hide_qk, ALU.is_ge, NEG, 0.0, -1),
                       (before, ALU.is_gt, 0.0, 1.0, 1)]
            for m, _, _, base, _ in zero_in:
                nc.gpsimd.memset(m[:], base).then_inc(made, 1)
            nc.gpsimd.memset(ones[:], 1.0).then_inc(made, 1)
            nc.gpsimd.memset(halves[:], 0.0).then_inc(made, 1)
            nc.gpsimd.memset(minus_half[:], -0.5).then_inc(made, 1)
            nc.gpsimd.memset(eps[:], EPS).then_inc(made, 1)
            nc.gpsimd.memset(qz[:], 0.0).then_inc(made, 1)
            nc.gpsimd.memset(stack[1][:], 1.0).then_inc(made, 1)
            nc.gpsimd.memset(v_self[:], 0.0).then_inc(made, 1)
            nc.gpsimd.memset(xv[:], 1.0).then_inc(made, 1)
            nc.gpsimd.memset(sumT_x[:], 0.0).then_inc(made, 1)
            nc.gpsimd.memset(carry[:], 0.0).then_inc(made, 1)
            for e in range(E):
                nc.gpsimd.memset(rank[:, :, e], float(E - e)).then_inc(made, 1)
            pool.wait_ge(made, 21 + E)
            for m, op, fill, _, sign in zero_in:
                nc.gpsimd.affine_select(out=m[:], in_=m[:], compare_op=op, fill=fill, base=0,
                                        pattern=[[sign, P]], channel_multiplier=-sign).then_inc(made, 1)
            nc.gpsimd.memset(v_self[:, :, :, HS], 1.0).then_inc(made, 1)
            pool.wait_ge(made, MADE)
            nc.gpsimd.memset(tick[:, 0:1], 0.0).then_inc(x2_out.sem, 1)

            for sec in sections(pool):
                n, ticks = [0], [1]

                def step(ins):
                    n[0] += 1
                    ins.then_inc(p_step.sem, 1)
                    pool.wait_ge(p_step.sem, p_step.of(sec.s, n[0]))

                def held():
                    ticks[0] += 1
                    nc.gpsimd.tensor_tensor(tick[:, ticks[0]:ticks[0] + 1], ones[0:1, 0:1], ones[0:1, 0:1], ALU.add)

                def power(k):
                    pool.wait_ge(padded[k].sem, padded[k].of(sec.x if k == "r" else sec.s, 1))
                    nc.gpsimd.tensor_tensor(inv[k][:], var[k][:], minus_half[:, 0:tiles_of[k]], ALU.pow
                                            ).then_inc(powered[k].sem, 1)

                def biased(dst, src, bias, done):
                    for t in range(T):
                        add = nc.gpsimd.tensor_tensor(dst[:, t, :], src[:, t, :], spread[bias][:], ALU.add)
                    add.then_inc(done.sem, 1)

                if sec.kind != FIRST:
                    pool.wait_ge(g_taken.sem, g_taken.at(sec, 0))
                for name, i in sec.steps:
                    if name == "sl_norm":
                        pool.wait_ge(padded["l"].sem, padded["l"].of(sec.s, 1))
                        i1 = inv["l"][:]
                        step(nc.gpsimd.tensor_tensor(i1, var["l"][:], minus_half[:, 0:T], ALU.pow))
                        step(nc.gpsimd.tensor_tensor(inv2[:], i1, i1, ALU.mult))
                        step(nc.gpsimd.tensor_tensor(inv2[:], inv2[:], mv["l"][:, :, 1], ALU.mult))
                        step(nc.gpsimd.tensor_tensor(inv2[:], inv2[:], eps[:], ALU.add))
                        step(nc.gpsimd.tensor_tensor(inv2[:], inv2[:], minus_half[:, 0:T], ALU.pow))
                        nc.gpsimd.tensor_tensor(i1, i1, inv2[:], ALU.mult).then_inc(powered["l"].sem, 1)
                    elif name == "sc_norm":
                        power("c")
                    elif name == "x_base":
                        nc.gpsimd.tensor_copy(key_bias[:, 0:CT], ctx_bias[:, ds(sec.x[0] * CT, CT)]
                                              ).then_inc(kb_ready.sem, 1)
                        pool.wait_ge(x2_out.sem, x2_out.of(sec.x, 0))
                        biased(xx, xs, "bo", xx_made)
                    elif name == "s_norm":
                        power("s")
                    elif name == "s_T":
                        pool.wait_ge(normed["s"].sem, normed["s"].of(sec.s, 1))
                        biased(xs, xs, "bm", xs_biased)
                    elif name == "l_qT":
                        pool.wait_ge(q_padded.sem, q_padded.of(sec.x, 1))
                        nc.gpsimd.tensor_tensor(q_inv[:], q_ss[:], minus_half[:, 0:T * XH], ALU.pow
                                                ).then_inc(q_powered.sem, 1)
                    elif name == "l_ss":
                        pool.wait_ge(g_taken.sem, g_taken.at(sec, TOOK[sec.kind][name, i]))
                        two = lambda x: x[:].rearrange("p (j h) -> p j h", h=XH)[:, :, 2 * i:2 * i + 2]
                        nc.gpsimd.tensor_tensor(two(k_inv), two(k_ss), two(minus_half), ALU.pow
                                                ).then_inc(k_powered.sem, 1)
                    elif name == "r_norm":
                        power("r")
                    elif name == "r_places":
                        pool.wait_ge(slots_ready.sem, slots_ready.of(sec.x, 2))
                        held()
                        for t in range(T):
                            for k in range(2):
                                nc.gpsimd.indirect_dma_start(
                                    scratch["expert_in"], bass.IndirectOffsetOnAxis(slot[k][:, t:t + 1], 0),
                                    at_x[:, t, :], None, bounds_check=E * CAP - 1, oob_is_err=False
                                    ).then_inc(scattered.sem, 16)
                        pool.wait_ge(scattered.sem, scattered.of(sec.x, 2 * T * 16))
                        held()
                        nc.gpsimd.memset(tick[:, 0:1], 0.0).then_inc(rows_free.sem, 1)
                if sec.kind == FIRST:
                    pool.wait_ge(sems["slots_cleared"], 16 * (E * CAP // (P * T)))
                    nc.gpsimd.memset(tick[:, 1:2], 0.0).then_inc(rows_free.sem, 1)
                assert n[0] == (p_step.per if "s" in STAGES[sec.kind] else 0), n
        @block.scalar
        def _(act):
            act.wait_ge(sems["constants_made"], 4)
            for s in range(E * CAP // (P * T)):
                act.dma_start(scratch["expert_in"][s * P * T:(s + 1) * P * T, :]
                              .rearrange("(t p) d -> p t d", p=P), xn_x[:]).then_inc(sems["slots_cleared"], 16)
            for sec in sections(act):
                if sec.kind != FIRST:
                    act.wait_ge(g_taken.sem, g_taken.at(sec, 0))
                took = TOOK[sec.kind]
                for name, i in sec.steps:
                    k = SCORED[sec.kind][name, i]
                    if name == "s_q":
                        act.wait_ge(g_taken.sem, g_taken.at(sec, took[name, i]))
                        nc.scalar.activation(part[i][:, 0], qk[i], ACT.Copy).then_inc(rounded.sem, 1)
                    elif name == "s_rest":
                        act.wait_ge(rested.sem, rested.of(sec.s, i + 1))
                        nc.scalar.activation(part[i][:, 1], rest[i], ACT.Copy).then_inc(rounded.sem, 1)
                    elif name == "l_ss":
                        if i == 0:
                            act.wait_ge(g_taken.sem, g_taken.at(sec, took["c_k", 0]))
                            act.wait_ge(g_taken.sem, g_taken.at(sec, took["l_k", 0]))
                        else:
                            act.wait_ge(g_ready.sem, g_ready.at(sec, took[name, i - 1]))
                        nc.scalar.activation(xk2, xk[:, i, :], ACT.Square).then_inc(sq_ready.sem, 1)
                    elif name == "s_scores":
                        act.wait_ge(s_ready.sem, s_ready.at(sec, k))
                        if i >= NPS:
                            act.wait_ge(used["s"].sem, used["s"].of(sec.s, (i - NPS) // 5 + 1))
                        nc.scalar.activation(pr_s[:, i % NPS, :], SX(k - 1), ACT.Exp).then_inc(s_done.sem, 1)
                    elif name == "x_scores":
                        act.wait_ge(s_ready.sem, s_ready.at(sec, k))
                        h, j = divmod(i, KT)
                        if i == 0:
                            act.wait_ge(kb_ready.sem, kb_ready.of(sec.x, 1))
                            act.wait_ge(g_ready.sem, g_ready.at(sec, took["l_ss", C - 1]))
                        if i % (2 * KT) == 0:
                            act.wait_ge(k_powered.sem, k_powered.of(sec.x, i // (2 * KT) + 1))
                        if i >= NPX:
                            act.wait_ge(used["x"].sem, used["x"].of(sec.x, i - NPX + 1))
                        bias = key_bias[:, j:j + 1] if j < CT else shift[:, 0:1]
                        nc.scalar.activation(pr_x[:, i % NPX, :], SX(k - 1), ACT.Exp, bias=bias,
                                             scale=k_inv[:, j * XH + h:j * XH + h + 1]).then_inc(s_done.sem, 1)
                    elif name == "r_logits":
                        act.wait_ge(g_taken.sem, g_taken.at(sec, took[name, i]))
                        nc.scalar.activation(r["ex"][:], r["lg"][:], ACT.Exp).then_inc(ex_ready.sem, 1)

        @block.tensor
        def _(pe):
            mm, turn = nc.tensor.matmul, nc.tensor.transpose
            pe.wait_ge(sems["constants_made"], MADE)
            k = 0
            for i, (_, t, w, dst) in enumerate(TURNED):
                pe.wait_ge(sems["raw_loaded"], 16 * (i + 1))
                for ch, cw in chunks(w):
                    if k >= 4:
                        pe.wait_ge(sems["weight_copied"], k - 3)
                    for j in range(t):
                        last = turn(SX(k)[0:cw, j * P:(j + 1) * P], raw[:, j, ch * P:ch * P + cw], ident[:])
                    last.then_inc(sems["weight_turned"], 1)
                    k += 1
            pe.wait_ge(sems["setup_step"], 1)
            pe.wait_ge(sems["weight_copied"], k - 3)
            turn(SX(k)[:, 0:B * CT], maskf[:], ident[0:B * CT, 0:B * CT]).then_inc(sems["weight_turned"], 1)
            pe.wait_ge(sems["tables_made"], 1)
            pe.wait_ge(sems["weights_loaded"], 16 * len(LOADS))

            for sec in sections(pe):
                g, s = [0], [0]
                took = TOOK[sec.kind]

                def bank():
                    g[0] += 1
                    if g[0] > NG:
                        pe.wait_ge(g_taken.sem, g_taken.at(sec, g[0] - NG))
                    return G(g[0] - 1)

                def sbank():
                    s[0] += 1
                    if s[0] > NS:
                        pe.wait_ge(s_done.sem, s_done.at(sec, s[0] - NS))
                    return SX(s[0] - 1)

                def whole(*step):
                    pe.wait_ge(g_taken.sem, g_taken.at(sec, took[step]))

                def turned(src, tiles, width=D):
                    for ch, cw in chunks(width):
                        for t0 in range(0, tiles, 4):
                            dst = bank()
                            for t in range(t0, min(t0 + 4, tiles)):
                                last = turn(dst[0:cw, (t - t0) * P:(t - t0 + 1) * P],
                                            src[:, t, ch * P:ch * P + cw], ident[:])
                            last.then_inc(g_ready.sem, 1)

                def to_features(w, col, src, width, n, contract=D):
                    for t0 in range(0, n, 512):
                        dst = bank()
                        tw = min(512, n - t0)
                        for ch, cw in chunks(contract):
                            last = mm(dst[:, 0:tw], w[0:cw, ch, col:col + width], src[0:cw, ch, t0:t0 + tw],
                                      start=ch == 0, stop=ch == C - 1)
                        last.then_inc(g_ready.sem, 1)

                def to_tokens(w, col, src, tiles, contract=D):
                    for t0 in range(0, tiles, 2):
                        dst = bank()
                        for t in range(t0, min(t0 + 2, tiles)):
                            for ch, cw in chunks(contract):
                                last = mm(dst[:, (t - t0) * D:(t - t0 + 1) * D], src[0:cw, ch, t * P:(t + 1) * P],
                                          w[0:cw, ch, col:col + D], start=ch == 0, stop=ch == C - 1)
                        last.then_inc(g_ready.sem, 1)

                qs, ks = stack

                def seen(dst, h, q):
                    w = (q + 1) * P
                    mm(dst[:, 0:w], qs[0:MAXROW, h, q * P:w], ks[0:MAXROW, h, 0:w], start=True, stop=False)
                    return mm(dst[:, q * P:w], identb[:], hide_qk[:], start=False, stop=True)

                def scored(dst, h, k):
                    w = S - k * P
                    mm(dst[:, 0:w], ks[0:MAXROW + 1, h, k * P:(k + 1) * P], qs[0:MAXROW + 1, h, k * P:S],
                       start=True, stop=False)
                    return mm(dst[:, 0:P], identb[:], hide_kq[:], start=False, stop=True)

                if sec.kind != FIRST:
                    pe.wait_ge(g_taken.sem, g_taken.at(sec, 0))
                for name, i in sec.steps:
                    if name == "s_T":
                        pe.wait_ge(normed["s"].sem, normed["s"].of(sec.s, 1))
                        turned(xn_s, T)
                    elif name == "s_q":
                        if i == 0:
                            whole("s_T", 0)
                        for oc in range(C):
                            to_features(w_self[("Wq", "Wk")[i]], oc * P, xnT_s, P, S)
                    elif name == "s_v":
                        to_tokens(w_self["Wv"], 0, xnT_s, T)
                    elif name == "s_max":
                        pair_, u = divmod(i, 5)
                        if i == 0:
                            pe.wait_ge(stacked.sem, stacked.of(sec.s, 2 * NPART * 16))
                        dst = bank()
                        if u == 4:
                            seen(dst, 2 * pair_, 1)
                            last = seen(dst[:, 2 * P:], 2 * pair_ + 1, 1)
                        elif u % 2 == 0:
                            last = seen(dst, 2 * pair_ + u // 2, 3)
                        else:
                            seen(dst, 2 * pair_ + u // 2, 2)
                            last = seen(dst[:, 3 * P:], 2 * pair_ + u // 2, 0)
                        last.then_inc(g_ready.sem, 1)
                    elif name == "s_maxT":
                        whole("s_max", NSU - 1)
                        turn(bank()[:, 0:P], nmax_pad[:], ident[:]).then_inc(g_ready.sem, 1)
                    elif name == "s_scores":
                        pair_, u = divmod(i, 5)
                        dst = sbank()
                        if i == 0:
                            pe.wait_ge(max_in.sem, max_in.of(sec.s, 16))
                        if u == 4:
                            scored(dst, 2 * pair_, 2)
                            last = scored(dst[:, 2 * P:], 2 * pair_ + 1, 2)
                        elif u % 2 == 0:
                            last = scored(dst, 2 * pair_ + u // 2, 0)
                        else:
                            scored(dst, 2 * pair_ + u // 2, 1)
                            last = scored(dst[:, 3 * P:], 2 * pair_ + u // 2, 3)
                        last.then_inc(s_ready.sem, 1)
                    elif name == "s_sums":
                        if i % 2 == 0 and i:
                            pe.wait_ge(o_taken["s"].sem, o_taken["s"].of(sec.s, i // 2))
                        if i == 0:
                            whole("s_v", 0)
                        pe.wait_ge(s_done.sem, s_done.at(sec, SCORED[sec.kind]["s_scores", 5 * i + 4]))
                        for hh in range(2):
                            h = 2 * i + hh
                            lies = [(2 * hh, 0), (2 * hh + 1, 0), (4, 2 * P * hh), (2 * hh + 1, 3 * P)]
                            row = h % HEADS_UP * HEAD_ROWS
                            for k, (u, col) in enumerate(lies):
                                last = mm(O["s"][row:row + HEAD_ROWS, k * P:S], v_self[:, k, h, :],
                                          pr_s[:, (5 * i + u) % NPS, col:col + S - k * P], start=k == 0,
                                          stop=k == T - 1, tile_position=(0, row), skip_group_check=True)
                        last.then_inc(used["s"].sem, 1)
                    elif name == "s_head":
                        dst = bank()
                        pe.wait_ge(o_taken["s"].sem, o_taken["s"].of(sec.s, i + 1))
                        for t in range(T):
                            last = turn(dst[:, t * P:(t + 1) * P], sumT_s[:, t * P:(t + 1) * P], ident[:])
                        last.then_inc(g_ready.sem, 1)
                    elif name == "s_outT":
                        whole("s_head", H // HEADS_UP - 1)
                        turned(at_s, T)
                    elif name == "s_out":
                        whole("s_outT", 0)
                        to_tokens(w_self["Wm"], 0, xnT_s, T)
                    elif name == "l_T":
                        pe.wait_ge(normed["l"].sem, normed["l"].of(sec.x, 1))
                        turned(xn_x, T)
                    elif name == "l_q":
                        to_tokens(xwqT, 0, xnT_x, T)
                    elif name == "l_k":
                        whole("l_T", 0)
                        for oc in range(C):
                            to_features(xwlT, oc * P, xnT_x, P, S)
                    elif name == "l_v":
                        to_tokens(xwlT, D, xnT_x, T)
                    elif name == "sc_T":
                        pe.wait_ge(normed["c"].sem, normed["c"].of(sec.s, 1))
                        turned(cb, CT)
                    elif name == "c_k":
                        for oc in range(C):
                            to_features(xwcT, oc * P, cT, P, SCP)
                    elif name == "c_v":
                        to_tokens(xwcT, D, cT, CT)
                    elif name == "l_qT":
                        pe.wait_ge(q_normed.sem, q_normed.of(sec.x, 1))
                        turned(at_x, T)
                    elif name == "l_ss":
                        dst = bank()
                        pe.wait_ge(sq_ready.sem, sq_ready.of(sec.x, i + 1))
                        for j in range(KT):
                            last = mm(dst[:, 2 * j:2 * j + 2], xk2[:, j * P:(j + 1) * P], halves[:],
                                      start=True, stop=True)
                        last.then_inc(g_ready.sem, 1)
                    elif name == "x_scores":
                        h, j = divmod(i, KT)
                        dst = sbank()
                        if i == 0:
                            whole("l_qT", 0)
                        mm(dst, xk[:, h // 2, j * P:(j + 1) * P], qz[:, h, :], start=True, stop=True
                           ).then_inc(s_ready.sem, 1)
                    elif name == "x_sums":
                        h, j = divmod(i, KT)
                        if i == 0:
                            whole("c_v", 0)
                        if j == 0 and h:
                            pe.wait_ge(o_taken["x"].sem, o_taken["x"].of(sec.x, h))
                        pe.wait_ge(s_done.sem, s_done.at(sec, SCORED[sec.kind]["x_scores", i]))
                        mm(O["x"][0:XD + 1, :], xv[:, j, h, :], pr_x[:, i % NPX, :], start=j == 0, stop=j == KT - 1
                           ).then_inc(used["x"].sem, 1)
                    elif name == "x_head":
                        dst = bank()
                        pe.wait_ge(o_taken["x"].sem, o_taken["x"].of(sec.x, i + 1))
                        for t in range(T):
                            last = turn(dst[:, t * P:(t + 1) * P], sumT_x[:, t * P:(t + 1) * P], ident[:])
                        last.then_inc(g_ready.sem, 1)
                    elif name == "x_T":
                        whole("x_head", XH - 1)
                        turned(at_x, T)
                    elif name == "x_out":
                        whole("x_T", 0)
                        to_tokens(xwoT, 0, xnT_x, T)
                    elif name == "r_T":
                        pe.wait_ge(normed["r"].sem, normed["r"].of(sec.x, 1))
                        turned(at_x, T)
                    elif name == "r_logits":
                        whole("r_T", 0)
                        dst = bank()
                        for t in range(T):
                            for ch in range(C):
                                last = mm(dst[:, t * E:(t + 1) * E], xnT_x[:, ch, t * P:(t + 1) * P],
                                          router[:, ch, :], start=ch == 0, stop=ch == C - 1)
                        last.then_inc(g_ready.sem, 1)
                    elif name == "r_places":
                        dst = bank()
                        pe.wait_ge(hot_ready.sem, hot_ready.of(sec.x, 1))
                        for t in range(T + 1):
                            for u in range(min(t + 1, T)):
                                last = mm(dst[:, t * E:(t + 1) * E], before[:] if u == t else ones[:],
                                          r["m"][:, u, :], start=u == 0, stop=u == min(t, T - 1))
                        last.then_inc(g_ready.sem, 1)
                    assert g[0] == took[name, i] and s[0] == SCORED[sec.kind][name, i], (name, i, g, s)

        @block.vector
        def _(dve):
            V = nc.vector
            made = sems["setup_step"]
            dve.wait_ge(sems["constants_made"], MADE)
            dve.wait_ge(sems["weights_loaded"], 16 * len(LOADS))
            V.tensor_copy(maskf[:], mask8[:]).then_inc(made, 1)
            for h in range(2):
                V.memset(halves[h * XD:(h + 1) * XD, h:h + 1], 1.0).then_inc(sems["halves_made"], 1)
            V.tensor_tensor(grow[:, 0, :], grow[:, 0, :], grow[:, 1, :], ALU.mult).then_inc(made, 1)
            V.scalar_tensor_tensor(out=gqk[:], in0=gcol[:, 0:1], scalar=XD ** -0.5, in1=gcol[:, 1:2],
                                   op0=ALU.mult, op1=ALU.mult).then_inc(made, 1)
            dve.wait_ge(made, 3)
            V.tensor_reduce(shift[:], grow[:, 0, :], AX.X, ALU.max, apply_absolute_value=True).then_inc(made, 1)
            dve.wait_ge(made, 4)
            V.tensor_scalar(shift[:], shift[:], XD ** 0.5, -HEADROOM, ALU.mult, ALU.add).then_inc(made, 1)
            dve.wait_ge(made, 5)
            V.tensor_scalar(shift[:], shift[:], 0.0, -1.0, ALU.max, ALU.mult).then_inc(made, 1)
            k = 0
            for _, t, w, dst in TURNED:
                for ch, cw in chunks(w):
                    dve.wait_ge(sems["weight_turned"], k + 1)
                    V.tensor_copy(dst[0:cw, ch, 0:t * P], SX(k)[0:cw, 0:t * P]).then_inc(sems["weight_copied"], 1)
                    k += 1
            dve.wait_ge(sems["weight_turned"], k + 1)
            V.tensor_scalar(hide[:], SX(k)[:, 0:B * CT], -1.0, -NEG, ALU.add, ALU.mult).then_inc(made, 1)
            dve.wait_ge(made, 7)
            dve.wait_ge(sems["halves_made"], 2)
            V.tensor_scalar(ctx_bias[:], hide[:], shift[:, 0:1], None, ALU.add).then_inc(sems["tables_made"], 1)
            dve.wait_ge(sems["tables_made"], 1)

            for sec in sections(dve):
                g, n = [0], [0]

                def took():
                    g[0] += 1
                    dve.wait_ge(g_ready.sem, g_ready.at(sec, g[0]))
                    return G(g[0] - 1)

                def step(ins):
                    n[0] += 1
                    ins.then_inc(v_step.sem, 1)
                    dve.wait_ge(v_step.sem, v_step.at(sec, n[0]))

                def variances(k, src, column):
                    for t in range(tiles_of[k]):
                        last = V.bn_stats(stats[:, t, :], src[:, t, :])
                    step(last)
                    V.memset(vtick[:, column:column + 1], 0.0)
                    for t in range(tiles_of[k]):
                        last = V.bn_aggr(mv[k][:, t, :], stats[:, t, :])
                    step(last)
                    V.tensor_scalar(var[k][:], mv[k][:, :, 1], EPS, None, ALU.add).then_inc(padded[k].sem, 1)

                def normalise(k, dst, src):
                    dve.wait_ge(powered[k].sem, powered[k].of(sec.x if k == "r" else sec.s, 1))
                    for t in range(tiles_of[k]):
                        last = V.tensor_scalar(dst[:, t, :], src[:, t, :], mv[k][:, t, 0:1], inv[k][:, t:t + 1],
                                               ALU.subtract, ALU.mult)
                    last.then_inc(normed[k].sem, 1)

                def copied(dst, tiles=T, width=D, gain=None):
                    for ch, cw in chunks(width):
                        for t0 in range(0, tiles, 4):
                            w = min(4, tiles - t0) * P
                            src, to = took()[0:cw, 0:w], dst[0:cw, ch, t0 * P:t0 * P + w]
                            if gain is None:
                                ins = V.tensor_copy(to, src)
                            else:
                                ins = V.tensor_scalar(to, src, gain[0:cw, ch, 0:1], gain[0:cw, ch, 1:2],
                                                      ALU.mult, ALU.add)
                            ins.then_inc(g_taken.sem, 1)

                def values(first, tiles):
                    for t0 in range(0, tiles, 2):
                        w = min(2, tiles - t0)
                        V.tensor_copy(xv[:, first + t0:first + t0 + w, :, 0:XD],
                                      took()[:, 0:w * D].rearrange("p (t h d) -> p t h d", t=w, h=XH)
                                      ).then_inc(g_taken.sem, 1)

                def largest(src, h, q, at_=0):
                    return V.tensor_reduce(nmax[:, h, q:q + 1], src[:, at_:at_ + (q + 1) * P], AX.X, ALU.max,
                                           negate=True)

                def laid_down(stage, dst, height, sums_done):
                    dve.wait_ge(used[stage].sem, used[stage].of(sec.s if stage == "s" else sec.x, sums_done))
                    V.tensor_copy(dst[0:height, :], O[stage][0:height, :]).then_inc(o_taken[stage].sem, 1)

                def divided(stage, heads, width, dst):
                    sums = took().rearrange("p (t h d) -> p t h d", t=T, h=heads)
                    dve.wait_ge(g_taken.sem, g_taken.at(sec, g[0] - 1))
                    over = rec[stage][:].rearrange("p (t h) -> p t h", t=T)
                    step(V.reciprocal(over, sums[:, :, :, width]))
                    V.tensor_tensor(dst.rearrange("p t (h d) -> p t h d", h=heads), sums[:, :, :, 0:width],
                                    over.unsqueeze(3).to_broadcast([P, T, heads, width]), ALU.mult
                                    ).then_inc(g_taken.sem, 1)

                def add_residual(x):
                    for t0 in range(0, T, 2):
                        V.tensor_tensor(x[:, t0:t0 + 2, :], took().rearrange("p (t d) -> p t d", t=2),
                                        x[:, t0:t0 + 2, :], ALU.add).then_inc(g_taken.sem, 1)

                wide = lambda x: x[:].unsqueeze(2).to_broadcast([P, T, E])
                if sec.kind != FIRST:
                    dve.wait_ge(g_taken.sem, g_taken.at(sec, 0))
                for name, i in sec.steps:
                    if name == "s_stats":
                        dve.wait_ge(x_in.sem, x_in.of(sec.s, 16))
                        variances("s", xs, 0)
                    elif name == "s_norm":
                        normalise("s", xn_s, xs)
                    elif name == "s_T":
                        copied(xnT_s)
                    elif name == "s_q":
                        for oc in range(C):
                            V.tensor_scalar(qk[i][:, oc, :], took(), b_self[("bq", "bk")[i]][:, oc:oc + 1],
                                            (HS ** -0.5, 1.0)[i], ALU.add, ALU.mult).then_inc(g_taken.sem, 1)
                    elif name == "s_rest":
                        dve.wait_ge(rounded.sem, rounded.of(sec.s, i + 1))
                        V.tensor_tensor(rest[i], qk[i], part[i][:, 0], ALU.subtract).then_inc(rested.sem, 1)
                    elif name == "s_parts":
                        dve.wait_ge(rounded.sem, rounded.of(sec.s, 2 + i + 1))
                        V.tensor_tensor(part[i][:, 2], rest[i], part[i][:, 1], ALU.subtract).then_inc(rested.sem, 1)
                    elif name == "s_v":
                        for t0 in range(0, T, 2):
                            src = took()
                            for t in range(t0, t0 + 2):
                                ins = V.tensor_tensor(
                                    v_self[:, t, :, 0:HS],
                                    src[:, (t - t0) * D:(t - t0 + 1) * D].rearrange("p (h d) -> p h d", h=H),
                                    spread["bv"][:].rearrange("p (h d) -> p h d", h=H), ALU.add)
                            ins.then_inc(g_taken.sem, 1)
                    elif name == "s_max":
                        pair_, u = divmod(i, 5)
                        src = took()
                        if u == 4:
                            largest(src, 2 * pair_, 1)
                            last = largest(src, 2 * pair_ + 1, 1, 2 * P)
                        elif u % 2 == 0:
                            last = largest(src, 2 * pair_ + u // 2, 3)
                        else:
                            largest(src, 2 * pair_ + u // 2, 2)
                            last = largest(src, 2 * pair_ + u // 2, 0, 3 * P)
                        last.then_inc(g_taken.sem, 1)
                    elif name == "s_maxT":
                        V.tensor_copy(nmaxT[:], took()[0:H * T, 0:P]).then_inc(g_taken.sem, 1)
                    elif name == "s_sums" and i % 2:
                        laid_down("s", sumT_s, P, i + 1)
                    elif name == "s_head":
                        divided("s", HEADS_UP, HS, at_s[:, :, i * HEADS_UP * HS:(i + 1) * HEADS_UP * HS])
                    elif name == "s_outT":
                        copied(xnT_s)
                    elif name == "s_out":
                        dve.wait_ge(xs_biased.sem, xs_biased.of(sec.s, 1))
                        add_residual(xs)
                    elif name == "sl_stats":
                        dve.wait_ge(g_taken.sem, g_taken.at(sec, g[0]))
                        variances("l", xs, 1)
                    elif name == "sl_norm":
                        if sec.kind == FIRST:
                            dve.wait_ge(sems["slots_cleared"], 16 * (E * CAP // (P * T)))
                        normalise("l", xn_x, xs)
                    elif name == "sc_stats":
                        dve.wait_ge(c_in.sem, c_in.of(sec.s, 32))
                        variances("c", cb[:, :, 0:DC], 2)
                    elif name == "sc_norm":
                        normalise("c", cb[:, :, 0:DC], cb[:, :, 0:DC])
                    elif name == "l_T":
                        copied(xnT_x, gain=ln_l)
                    elif name == "sc_T":
                        copied(cT, CT, gain=ln_x)
                    elif name == "l_q":
                        dve.wait_ge(rows_free.sem, rows_free.of(sec.x, 0))
                        for t0 in range(0, T, 2):
                            V.tensor_copy(at_x[:, t0:t0 + 2, :], took().rearrange("p (t d) -> p t d", t=2)
                                          ).then_inc(g_taken.sem, 1)
                        dve.wait_ge(g_taken.sem, g_taken.at(sec, g[0]))
                        step(V.tensor_tensor(xn_x[:], at_x[:], at_x[:], ALU.mult))
                        step(V.tensor_reduce(q_ss[:], xn_x[:].rearrange("p t (h d) -> p (t h) d", h=XH), AX.X,
                                             ALU.add))
                        V.tensor_scalar(q_ss[:], q_ss[:], 1.0 / XD, RMS_EPS ** 2, ALU.mult, ALU.max
                                        ).then_inc(q_padded.sem, 1)
                    elif name == "l_k":
                        for oc in range(C):
                            V.tensor_copy(xk[:, oc, SCP:], took()).then_inc(g_taken.sem, 1)
                    elif name == "l_v":
                        values(CT, T)
                        dve.wait_ge(q_powered.sem, q_powered.of(sec.x, 1))
                        V.tensor_tensor(at_x[:].rearrange("p t (h d) -> p (t h) d", h=XH),
                                        at_x[:].rearrange("p t (h d) -> p (t h) d", h=XH),
                                        q_inv[:].unsqueeze(2).to_broadcast([P, T * XH, XD]), ALU.mult
                                        ).then_inc(q_normed.sem, 1)
                    elif name == "c_k":
                        for oc in range(C):
                            for t0 in range(0, SCP, 512):
                                w = min(512, SCP - t0)
                                V.tensor_copy(xk[:, oc, t0:t0 + w], took()[:, 0:w]).then_inc(g_taken.sem, 1)
                    elif name == "c_v":
                        values(0, CT)
                    elif name == "l_qT":
                        for ch in range(C):
                            src = took()
                            for h in range(2):
                                lo, hi = h * XD, (h + 1) * XD
                                ins = V.tensor_scalar(qz[lo:hi, 2 * ch + h, :], src[lo:hi, :], gqk[lo:hi, 0:1], None,
                                                      ALU.mult)
                            ins.then_inc(g_taken.sem, 1)
                    elif name == "l_ss":
                        V.tensor_scalar(k_ss[:].rearrange("p (j h) -> p j h", h=XH)[:, :, 2 * i:2 * i + 2],
                                        took()[:, 0:2 * KT].rearrange("p (j h) -> p j h", h=2), 1.0 / XD,
                                        RMS_EPS ** 2, ALU.mult, ALU.max).then_inc(g_taken.sem, 1)
                    elif name == "x_sums" and i % KT == KT - 1:
                        laid_down("x", sumT_x, XD + 1, i + 1)
                    elif name == "x_head":
                        divided("x", 1, XD, at_x[:, :, i * XD:(i + 1) * XD])
                    elif name == "x_T":
                        copied(xnT_x)
                    elif name == "x_out":
                        dve.wait_ge(xx_made.sem, xx_made.of(sec.x, 1))
                        add_residual(xx)
                    elif name == "r_stats":
                        dve.wait_ge(g_taken.sem, g_taken.at(sec, g[0]))
                        variances("r", xx, 3)
                    elif name == "r_norm":
                        normalise("r", at_x, xx)
                    elif name == "r_T":
                        copied(xnT_x)
                    elif name == "r_logits":
                        lg = took()[:, 0:T * E].rearrange("p (t e) -> p t e", t=T)
                        step(V.tensor_reduce(c["mx"][:], lg, AX.X, ALU.max))
                        V.tensor_tensor(r["lg"][:], lg, wide(c["mx"]), ALU.subtract).then_inc(g_taken.sem, 1)
                    elif name == "r_best":
                        dve.wait_ge(ex_ready.sem, ex_ready.of(sec.x, 1))
                        step(V.tensor_reduce(c["sm"][:], r["ex"][:], AX.X, ALU.add))
                        step(V.reciprocal(c["rc"][:], c["sm"][:]))
                        step(V.tensor_tensor(r["pr"][:], r["ex"][:], wide(c["rc"]), ALU.mult))
                        for k in range(2):
                            step(V.tensor_reduce(c[f"m{k}"][:], r["pr"][:], AX.X, ALU.max))
                            step(V.tensor_tensor(r["eq"][:], r["pr"][:], wide(c[f"m{k}"]), ALU.is_equal))
                            step(V.tensor_tensor(r["t"][:], r["eq"][:], rank[:], ALU.mult))
                            step(V.tensor_reduce(c[f"r{k}"][:], r["t"][:], AX.X, ALU.max))
                            step(V.tensor_tensor(r[f"oh{k}"][:], rank[:], wide(c[f"r{k}"]), ALU.is_equal))
                            if k == 0:
                                step(V.scalar_tensor_tensor(out=r["pr"][:], in0=r["oh0"][:], scalar=-2.0, in1=r["pr"][:],
                                                            op0=ALU.mult, op1=ALU.add))
                        V.tensor_tensor(r["m"][:], r["oh0"][:], r["oh1"][:], ALU.add).then_inc(hot_ready.sem, 1)
                    elif name == "r_places":
                        src = took()
                        step(V.tensor_tensor(r["pos"][:], src[:, 0:T * E].rearrange("p (t e) -> p t e", t=T),
                                             carry[:].unsqueeze(1).to_broadcast([P, T, E]), ALU.add))
                        V.tensor_tensor(carry[:], src[:, T * E:(T + 1) * E], carry[:], ALU.add).then_inc(g_taken.sem, 1)
                        dve.wait_ge(g_taken.sem, g_taken.at(sec, g[0]))
                        step(V.tensor_tensor(c["sm"][:], c["m0"][:], c["m1"][:], ALU.add))
                        step(V.reciprocal(c["rc"][:], c["sm"][:]))
                        for k in range(2):
                            p_, k_, b_, f_ = (c[f"{x}{k}"] for x in "pkbf")
                            step(V.tensor_tensor(r["t"][:], r["pos"][:], r[f"oh{k}"][:], ALU.mult))
                            step(V.tensor_reduce(p_[:], r["t"][:], AX.X, ALU.add))
                            step(V.tensor_scalar(k_[:], p_[:], float(CAP), None, ALU.is_lt))
                            step(V.tensor_scalar(b_[:], c[f"r{k}"][:], -float(CAP), float(E * CAP), ALU.mult, ALU.add))
                            step(V.tensor_tensor(p_[:], p_[:], k_[:], ALU.mult))
                            step(V.tensor_tensor(p_[:], p_[:], b_[:], ALU.add))
                            step(V.tensor_copy(kept["gather_at"][:, rows(sec.x), k, :], p_[:].unsqueeze(1)))
                            step(V.tensor_scalar(f_[:], k_[:], -FAR, FAR, ALU.mult, ALU.add))
                            step(V.tensor_tensor(f_[:], f_[:], p_[:], ALU.add))
                            step(V.tensor_copy(slot[k][:], f_[:]))
                            step(V.tensor_tensor(f_[:], c[f"m{k}"][:], c["rc"][:], ALU.mult))
                            V.tensor_tensor(kept["gates"][:, rows(sec.x), k, :], f_[:].unsqueeze(1), k_[:].unsqueeze(1),
                                            ALU.mult).then_inc(slots_ready.sem, 1)
                            dve.wait_ge(slots_ready.sem, slots_ready.of(sec.x, k + 1))
                    assert g[0] == TOOK[sec.kind][name, i], (name, i, g)
                assert n[0] == v_step.total[sec.kind], (sec.kind, n)


def experts_and_combine(nc, a, kept, scratch, out):
    with ExitStack() as ctx:
        sb = lambda n, s, d=F32: ctx.enter_context(nc.sbuf_tensor(n, s, d))
        sem = lambda n: ctx.enter_context(nc.semaphore(n))
        ident = kept["ident"]
        HALF = CAP // 2
        w1 = [sb(f"w1_{i}", [P, C, HID]) for i in range(2)]
        w2 = [sb(f"w2_{i}", [P, HC, D]) for i in range(2)]
        b1 = [sb(f"b1_{i}", [P, HC]) for i in range(2)]
        b1_rows = sb("b1_rows", [E * HC, P])
        b1T = sb("b1T", [P, E * HC])
        b2 = [sb(f"b2_{i}", [P, D]) for i in range(2)]
        xe = [sb(f"xe_{i}", [P, ST, D]) for i in range(2)]
        xeT = [sb(f"xeT_{i}", [P, C, CAP]) for i in range(2)]
        hT = [sb(f"hT_{i}", [P, HC, CAP]) for i in range(2)]
        oe = [sb(f"oe_{i}", [P, ST, D]) for i in range(2)]
        rows_at = [sb(f"rows_at_{i}", [P, 2, T], U32) for i in range(2)]
        gate = [sb(f"gate_{i}", [P, 2, T]) for i in range(2)]
        tick = sb("tick2", [1, 9])
        y = [sb(f"y_{i}", [P, 2, T, D]) for i in range(2)]
        res = [sb(f"res_{i}", [P, T, D]) for i in range(2)]
        psum = ctx.enter_context(nc.psum_tensor("psum2", [P, 8, 512], F32))
        NR = 4
        G = lambda i: psum[:, i % NR, :]
        A = lambda i: psum[:, NR + i % NR, :]
        GX, GO, GA = 2 * C, ST // 2, HC * 2

        C_ = lambda n, per, before=0: Count(sem(n), per, before)
        loaded = [C_(f"weights_in_{i}", 4 * 16) for i in range(2)]
        g_ready, g_taken = C_("ffn_product_ready", 2 * (GX + GO)), C_("ffn_product_taken", 2 * (GX + GO), 1)
        h_ready, h_done = C_("hidden_ready", 2 * GA), C_("hidden_done", 2 * GA, 1)
        stored = [C_(f"expert_rows_stored_{i}", 16, 1) for i in range(2)]
        copied_ = C_("indices_copied", 2 * 2)
        gathered = [C_(f"rows_gathered_{i}", 2 * T * 16) for i in range(2)]
        res_in = [C_(f"residual_in_{i}", 16) for i in range(2)]
        added = C_("rows_added", 2 * 2, 1)
        out_done = [C_(f"output_stored_{i}", 16, 1) for i in range(2)]
        b1_in, b1_turned, b1_kept = sem("b1_loaded"), sem("b1_turned"), sem("b1_kept")
        b1_here = C_("b1_copied", 2)
        block = ctx.enter_context(nc.Block())

        @block.sync
        def _(sp):
            sp.dma_start(b1_rows[:], a["L0_ffn_b1"].rearrange("e (c p) -> (e c) p", p=P)).then_inc(b1_in, 16)
            with sp.Fori(0, E // 2) as i:
                for j in range(2):
                    e = 2 * i + j
                    sp.wait_ge(stored[j].sem, stored[j].at(i, 0))
                    row = lambda x: x[ds(e, 1), :]
                    sp.dma_start(xe[j][:], scratch["expert_in"][ds(e * CAP, CAP), :]
                                 .rearrange("(t p) d -> p t d", p=P)).then_inc(loaded[j].sem, 16)
                    sp.dma_start(w1[j][:], a["L0_ffn_w1"][ds(e, 1), :, :].rearrange("a (c p) n -> p (a c) n", p=P)
                                 ).then_inc(loaded[j].sem, 16)
                    sp.dma_start(w2[j][:], a["L0_ffn_w2"][ds(e, 1), :, :].rearrange("a (c p) n -> p (a c) n", p=P)
                                 ).then_inc(loaded[j].sem, 16)
                    sp.dma_start(b2[j][:], row(a["L0_ffn_b2"]).rearrange("a n -> (a n)").partition_broadcast(P)
                                 ).then_inc(loaded[j].sem, 16)
            with sp.Fori(0, B // 2) as i:
                for j in range(2):
                    sp.wait_ge(out_done[j].sem, out_done[j].at(i, 0))
                    sp.dma_start(res[j][:], scratch["resid"][ds(2 * i + j, 1), :, :]
                                 .rearrange("a (t p) d -> p (a t) d", p=P)).then_inc(res_in[j].sem, 16)

        @block.scalar
        def _(act):
            act.wait_ge(b1_turned, 1)
            nc.scalar.activation(b1T[:], A(0)[:, 0:E * HC], ACT.Copy).then_inc(b1_kept, 1)
            act.wait_ge(b1_kept, 1)
            with act.Fori(0, E // 2) as i:
                n = 0
                for j in range(2):
                    nc.scalar.activation(b1[j][:], b1T[:, ds((2 * i + j) * HC, HC)], ACT.Copy).then_inc(b1_here.sem, 1)
                    act.wait_ge(b1_here.sem, b1_here.at(i, j + 1))
                    act.wait_ge(loaded[j].sem, loaded[j].at(i, 4 * 16))
                    for hc in range(HC):
                        for half in range(2):
                            act.wait_ge(h_ready.sem, h_ready.at(i, n + 1))
                            nc.scalar.activation(hT[j][:, hc, half * HALF:(half + 1) * HALF], A(n)[:, 0:HALF],
                                                 ACT.Relu, bias=b1[j][:, hc:hc + 1]).then_inc(h_done.sem, 1)
                            n += 1
                    act.wait_ge(g_taken.sem, g_taken.at(i, (j + 1) * (GX + GO)))
                    act.dma_start(scratch["expert_out"][ds((2 * i + j) * CAP, CAP), :]
                                  .rearrange("(t p) d -> p t d", p=P), oe[j][:]).then_inc(stored[j].sem, 16)
            for j in range(2):
                act.wait_ge(stored[j].sem, stored[j].at(E // 2, 0))
            with act.Fori(0, B // 2) as i:
                for j in range(2):
                    act.wait_ge(added.sem, added.at(i, 2 * j + 2))
                    act.dma_start(out[ds(2 * i + j, 1), :, :].rearrange("a (t p) d -> p (a t) d", p=P), res[j][:]
                                  ).then_inc(out_done[j].sem, 16)
            for j in range(2):
                act.wait_ge(out_done[j].sem, out_done[j].at(B // 2, 0))

        @block.tensor
        def _(pe):
            mm = nc.tensor.matmul
            pe.wait_ge(b1_in, 16)
            nc.tensor.transpose(A(0)[:, 0:E * HC], b1_rows[:], ident[0:E * HC, 0:E * HC]).then_inc(b1_turned, 1)
            pe.wait_ge(b1_kept, 1)
            with pe.Fori(0, E // 2) as i:
                g, n = [0], 0

                def bank():
                    g[0] += 1
                    if g[0] > NR:
                        pe.wait_ge(g_taken.sem, g_taken.at(i, g[0] - NR))
                    else:
                        pe.wait_ge(g_taken.sem, g_taken.at(i, 0))
                    return G(g[0] - 1)

                for j in range(2):
                    pe.wait_ge(loaded[j].sem, loaded[j].at(i, 4 * 16))
                    for ch in range(C):
                        for half in range(2):
                            dst = bank()
                            for t in range(ST // 2):
                                last = nc.tensor.transpose(dst[:, t * P:(t + 1) * P],
                                                           xe[j][:, half * (ST // 2) + t, ch * P:(ch + 1) * P], ident[:])
                            last.then_inc(g_ready.sem, 1)
                    pe.wait_ge(g_taken.sem, g_taken.at(i, g[0]))
                    for hc in range(HC):
                        for half in range(2):
                            pe.wait_ge(h_done.sem, h_done.at(i, max(n + 1 - NR, 0)))
                            for ch in range(C):
                                last = mm(A(n)[:, 0:HALF], w1[j][:, ch, hc * P:(hc + 1) * P],
                                          xeT[j][:, ch, half * HALF:(half + 1) * HALF], start=ch == 0, stop=ch == C - 1)
                            last.then_inc(h_ready.sem, 1)
                            n += 1
                    for t in range(ST):
                        if t % 2 == 0:
                            dst = bank()
                        if t == 0:
                            pe.wait_ge(h_done.sem, h_done.at(i, n))
                        for hc in range(HC):
                            last = mm(dst[:, t % 2 * D:(t % 2 + 1) * D], hT[j][:, hc, t * P:(t + 1) * P], w2[j][:, hc, :],
                                      start=hc == 0, stop=hc == HC - 1)
                        if t % 2:
                            last.then_inc(g_ready.sem, 1)

        @block.vector
        def _(dve):
            V = nc.vector
            with dve.Fori(0, E // 2) as i:
                g = [0]

                def took():
                    g[0] += 1
                    dve.wait_ge(g_ready.sem, g_ready.at(i, g[0]))
                    return G(g[0] - 1)

                for j in range(2):
                    for ch in range(C):
                        for half in range(2):
                            V.tensor_copy(xeT[j][:, ch, half * HALF:(half + 1) * HALF], took()[:, 0:HALF]
                                          ).then_inc(g_taken.sem, 1)
                    dve.wait_ge(loaded[j].sem, loaded[j].at(i, 4 * 16))
                    dve.wait_ge(stored[j].sem, stored[j].at(i, 0))
                    for t in range(0, ST, 2):
                        V.tensor_tensor(oe[j][:, t:t + 2, :], took().rearrange("p (t d) -> p t d", t=2),
                                        b2[j][:].unsqueeze(1).to_broadcast([P, 2, D]), ALU.add).then_inc(g_taken.sem, 1)
            with dve.Fori(0, B // 2) as i:
                for j in range(2):
                    dve.wait_ge(gathered[j].sem, gathered[j].at(i, 2 * T * 16))
                    dve.wait_ge(res_in[j].sem, res_in[j].at(i, 16))
                    dve.wait_ge(copied_.sem, copied_.at(i, 2 * j + 2))
                    for k in range(2):
                        for t in range(T):
                            last = V.scalar_tensor_tensor(out=res[j][:, t, :], in0=y[j][:, k, t, :],
                                                          scalar=gate[j][:, k, t:t + 1], in1=res[j][:, t, :],
                                                          op0=ALU.mult, op1=ALU.add)
                        last.then_inc(added.sem, 1)
                        dve.wait_ge(added.sem, added.at(i, 2 * j + k + 1))

        @block.gpsimd
        def _(pool):
            for i, x in enumerate((g_taken, h_done, *stored, added, *out_done)):
                nc.gpsimd.memset(tick[:, 2 + i:3 + i], 0.0).then_inc(x.sem, 1)
            for j in range(2):
                pool.wait_ge(stored[j].sem, stored[j].at(E // 2, 0))
            with pool.Fori(0, B // 2) as i:
                for j in range(2):
                    pool.wait_ge(added.sem, added.at(i, 0))
                    nc.gpsimd.tensor_copy(rows_at[j][:].unsqueeze(1), kept["gather_at"][:, ds(2 * i + j, 1), :, :]
                                          ).then_inc(copied_.sem, 1)
                    nc.gpsimd.tensor_copy(gate[j][:].unsqueeze(1), kept["gates"][:, ds(2 * i + j, 1), :, :]
                                          ).then_inc(copied_.sem, 1)
                    pool.wait_ge(copied_.sem, copied_.at(i, 2 * j + 2))
                    nc.gpsimd.tensor_tensor(tick[:, j:j + 1], ident[0:1, 0:1], ident[0:1, 0:1], ALU.add)
                    for k in range(2):
                        for t in range(T):
                            nc.gpsimd.indirect_dma_start(
                                y[j][:, k, t, :], None, scratch["expert_out"],
                                bass.IndirectOffsetOnAxis(rows_at[j][:, k, t:t + 1], 0),
                                bounds_check=E * CAP - 1, oob_is_err=False).then_inc(gathered[j].sem, 16)


_INS = ["x", "ctx_768", "mask_BxS2_bk0", "L0_attn_Wq", "L0_attn_bq", "L0_attn_Wk", "L0_attn_bk", "L0_attn_Wv",
        "L0_attn_bv", "L0_attn_Wm", "L0_attn_bm", "L0_xattn_ln_x_g", "L0_xattn_ln_x_b", "L0_xattn_ln_l_g",
        "L0_xattn_ln_l_b", "L0_xattn_qn_g", "L0_xattn_kn_g", "L0_xattn_Wq", "L0_xattn_Wkv", "L0_xattn_Wlkv",
        "L0_xattn_Wo", "L0_xattn_bo", "L0_ffn_w_router", "L0_ffn_w1", "L0_ffn_b1", "L0_ffn_w2", "L0_ffn_b2"]


def kernel(**inputs):
    import numpy as _np
    import concourse.bacc as _bacc
    from concourse import mybir as _mybir
    from concourse.bass_utils import run_bass_kernel_spmd as _run

    nc = _bacc.Bacc("TRN2", target_bir_lowering=False, num_devices=1)
    arrays, a = {}, {}
    for name in _INS:
        x = _np.ascontiguousarray(inputs[name])
        arrays[f"in_{name}"] = x
        a[name] = nc.dram_tensor(f"in_{name}", x.shape, _mybir.dt.from_np(x.dtype), kind="ExternalInput").ap()
    out = nc.dram_tensor("out", (B, S, D), F32, kind="ExternalOutput").ap()
    decoder(nc, a, out)
    r = _run(nc, [arrays], core_ids=[0])
    return r.results[0]["out"]
```

```python
from contextlib import ExitStack

import concourse.bass as bass
from concourse import mybir

ALU = mybir.AluOpType
ACT = mybir.ActivationFunctionType
F32 = mybir.dt.float32
BF16 = mybir.dt.bfloat16
U32 = mybir.dt.uint32
U8 = mybir.dt.uint8
AX = mybir.AxisListType
ds = bass.ds

P = 128
B, S, D = 8, 512, 256
C = D // P
T = S // P
H, HS = 16, 16
SC, DC = 1601, 192
CT = -(-SC // P)
SCP = CT * P
KT = CT + T
XH, XD = 4, 64
E, HID, CAP = 8, 1024, 768
ST = CAP // P
HC = HID // P
EPS, RMS_EPS = 1e-5, 1e-8
NEG = -1e30
HEADROOM = 70.0
FAR = 1.0e6

Q_PARTS = [0, 0, 0, 1, 1, 2]
K_PARTS = [0, 1, 2, 0, 1, 0]
NPART = len(Q_PARTS)
MAXROW = NPART * HS

MADE, PADS = 27, 8
DVE_STEPS = {"s": 8, "x": 39}
POOL_STEPS = 5

FIRST, BOTH, LAST = "first", "both", "last"
STAGES = {FIRST: "s", BOTH: "sx", LAST: "x"}
NXU = XH * KT
NSU = H // 2 * 5
AHEAD = 3
HEAD_ROWS = 32
HEADS_UP = P // HEAD_ROWS
NG, NS = 2, 4
NPS, NPX = 10, 5


def steps(kind):
    plan = []

    def put(at_, name, i=0):
        plan.append((at_, name, i))

    opening = [("l_stats", 0), ("c_k", 0), ("c_k", 1), ("l_norm", 0), ("x_base", 0), ("load", 0), ("l_T", 0), ("l_k", 0),
             ("s_stats", 0), ("l_k", 1), ("l_sq", 0), ("s_norm", 0), ("l_q", 0), ("s_T", 0), ("s_q", 0), ("s_q", 1),
             ("l_qss", 0), ("s_rest", 0), ("s_rest", 1), ("l_qn", 0)]
    for k in range(4):
        opening += [("c_v", k), ("l_ss", k)]
    opening += [("l_sq", 1), ("s_parts", 0), ("s_parts", 1), ("l_v", 0)]
    for k in range(3):
        opening += [("c_v", 4 + k), ("l_ss", 4 + k)]
    opening += [("l_v", 1), ("l_ss", 7), ("l_qT", 0), ("s_v", 0)]
    for k, (name, i) in enumerate(opening):
        put(k - 100, name, i)
    for u in range(-AHEAD, NXU):
        if u + AHEAD < NXU:
            put(u, "x_scores", u + AHEAD)
        if u >= 0:
            put(u + 0.1, "x_sums", u)
    for k, name in enumerate(("sc_stats", "sc_norm", "sc_T")):
        put(CONTEXT_AT + CONTEXT_PACE * k, name)
    for i in range(NSU):
        put(MAX_AT + i * MAX_PACE, "s_max", i)
    put(MAX_AT + NSU * MAX_PACE, "s_maxT")
    scores_at = [SCORES_AT + i * SCORES_PACE if i < IN_CROSS else NXU + (i - IN_CROSS) * LATE_PACE for i in range(NSU)]
    for i in range(NSU):
        put(scores_at[i], "s_scores", i)
    for p in range(H // 2):
        put(scores_at[5 * p + 4] + SUMS_LAG, "s_sums", p)
    for k in range(H // HEADS_UP):
        put(scores_at[10 * k + 9] + SUMS_LAG + HEAD_LAG, "s_head", k)
    for h in range(XH):
        put((h + 1) * KT - 1 + HEAD_LAG, "x_head", h)
    for k, name in enumerate(("x_T", "x_out", "r_stats", "r_norm", "r_T", "r_logits", "r_best")):
        put(NXU + 1 + TAIL_PACE * k, name)
    put(PLACES_AT, "r_places")
    for k, name in enumerate(("s_outT", "s_out")):
        put(200 + k, name)
    order = sorted(plan, key=lambda x: x[0])
    return [(name, i) for _, name, i in order if ("s" if name[0] == "s" or name == "load" else "x") in STAGES[kind]]


CONTEXT_AT, CONTEXT_PACE = 1.2, 3.0
MAX_AT, MAX_PACE = 10.0, 0.85
SCORES_AT, SCORES_PACE, SUMS_LAG = 48.0, 2.0, 3.0
IN_CROSS, LATE_PACE = 10, 0.7
HEAD_LAG, TAIL_PACE, PLACES_AT = 2.0, 2.2, 85.0
PRODUCTS = {"l_T": C, "sc_T": C * -(-CT // 4), "l_q": T // 2, "s_T": C, "s_q": C, "s_v": T // 2, "l_qT": C,
            "s_max": 1, "s_maxT": 1, "x_T": C, "s_head": 1, "x_head": 1, "x_out": T // 2, "r_T": C, "r_logits": 1,
            ("l_ss", 0): 1, ("l_ss", 4): 1, "r_places": 1, "s_outT": C, "s_out": T // 2}
SCORES = {"x_scores": 1, "s_scores": 1, "c_k": -(-SCP // 512), "c_v": 1, "l_k": 1, "l_v": 1}
PIECES = 4


def placed(banks):
    after, total = {}, {}
    for kind in (FIRST, BOTH, LAST):
        n, after[kind] = 0, {}
        for step in steps(kind):
            n += banks.get(step[0], 0) or banks.get(step, 0)
            after[kind][step] = n
        total[kind] = n
    return after, total


class Section:

    def __init__(self, kind, turn):
        self.kind, self.turn = kind, turn
        self.s = (turn, 1 if kind == BOTH else 0)
        self.x = (turn, 0)
        self.steps = steps(kind)


def sections(engine):
    yield Section(FIRST, 0)
    with engine.Fori(0, B - 1) as turn:
        yield Section(BOTH, turn)
    yield Section(LAST, B - 1)


def rows(element):
    turn, plus = element
    return ds(turn + plus, 1)


class Count:

    def __init__(self, sem, per, before=0):
        self.sem, self.per, self.before = sem, per, before

    def at(self, turn, k):
        return turn * self.per + (self.before + k)

    def of(self, element, k):
        turn, plus = element
        return turn * self.per + (self.before + plus * self.per + k)


class Tally:

    def __init__(self, sem, total):
        self.sem, self.total = sem, total

    def at(self, sec, k):
        if sec.kind == FIRST:
            return k
        return sec.turn * self.total[BOTH] + (self.total[FIRST] + k)


def decoder(nc, a, out):
    with ExitStack() as ctx:
        dram = lambda n, s, d: nc.dram_tensor(n, s, d, kind="Internal").ap()
        scratch = {
            "expert_in": dram("expert_in", (E * CAP, D), F32),
            "expert_out": dram("expert_out", (E * CAP, D), F32),
            "resid": dram("resid", (B, S, D), F32),
            "parts": dram("parts", (2, 3, D, S), BF16),
            "maxima": dram("maxima", (H * T, P), BF16),
        }
        kept = {n: ctx.enter_context(nc.sbuf_tensor(n, s, d)) for n, s, d in (
            ("gates", [P, B, 2, T], F32), ("gather_at", [P, B, 2, T], U32), ("ident", [P, P], F32))}
        attention_and_routing(nc, a, kept, scratch)
        experts_and_combine(nc, a, kept, scratch, out)


def attention_and_routing(nc, a, kept, scratch):
    with ExitStack() as ctx:
        sb = lambda n, s, d=F32: ctx.enter_context(nc.sbuf_tensor(n, s, d))
        sem = lambda n: ctx.enter_context(nc.semaphore(n))
        ident = kept["ident"]

        identb = sb("identb", [P, P], BF16)
        hide_kq = sb("hide_kq", [P, P], BF16)
        hide_qk = sb("hide_qk", [P, P], BF16)
        before = sb("before", [P, P])
        ones = sb("ones", [P, P])
        halves = sb("halves", [P, 2])
        minus_half = sb("minus_half", [P, KT * XH])
        eps = sb("eps", [P, T])
        rank = sb("rank", [P, T, E])
        w_self = {n: sb("w_" + n, [P, C, D]) for n in ("Wq", "Wk", "Wv", "Wm")}
        b_self = {n: sb("b_" + n, [P, C]) for n in ("bq", "bk")}
        spread = {n: sb("s_" + n, [P, D]) for n in ("bv", "bm", "bo")}
        xwqT = sb("xwqT", [P, C, D])
        xwoT = sb("xwoT", [P, C, D])
        xwlT = sb("xwlT", [P, C, 2 * D])
        xwcT = sb("xwcT", [P, C, 2 * D])
        router = sb("router", [P, C, E])
        ln_x = sb("ln_x", [P, C, 2])
        ln_l = sb("ln_l", [P, C, 2])
        gcol = sb("gcol", [P, 2])
        grow = sb("grow", [P, 2, XD])
        gqk = sb("gqk", [P, 1])
        shift = sb("shift", [P, 1])
        mask8 = sb("mask8", [B * CT, P], U8)
        maskf = sb("maskf", [B * CT, P])
        hide = sb("hide", [P, B * CT])
        ctx_bias = sb("ctx_bias", [P, B * CT])

        xs = sb("xs", [P, T, D])
        xx = sb("xx", [P, T, D])
        xn_s, xn_x = sb("xn_s", [P, T, D]), sb("xn_x", [P, T, D])
        xnT_s, xnT_x = sb("xnT_s", [P, C, S]), sb("xnT_x", [P, C, S])
        at_s, at_x = sb("at_s", [P, T, D]), sb("at_x", [P, T, D])
        stats = sb("stats", [P, CT, 6])
        tiles_of = {"s": T, "l": T, "c": CT, "r": T}
        mv = {n: sb("mv_" + n, [P, t, 2]) for n, t in tiles_of.items()}
        var = {n: sb("var_" + n, [P, t]) for n, t in tiles_of.items()}
        inv = {n: sb("inv_" + n, [P, t]) for n, t in tiles_of.items()}
        inv2 = sb("inv2", [P, T])
        stack = [sb("q_stack", [P, H, S], BF16), sb("k_stack", [P, H, S], BF16)]
        v_self = sb("v_self", [P, T, H, HEAD_ROWS])
        cb = sb("cb", [P, CT, D])
        cT = sb("cT", [P, C, SCP])
        xk = sb("xk", [P, C, KT * P])
        xv = sb("xv", [P, KT, XH, XD + 1])
        k_ss = sb("k_ss", [P, KT * XH])
        k_inv = sb("k_inv", [P, KT * XH])
        key_bias = sb("key_bias", [P, KT])
        nmax_pad = sb("nmax", [P, P])
        nmax = nmax_pad[:, 0:H * T].rearrange("p (h t) -> p h t", h=H)
        nmaxT = sb("nmaxT", [H * T, P], BF16)
        pr_s = sb("pr_s", [P, NPS, S])
        pr_x = sb("pr_x", [P, NPX, S])
        xk2 = pr_x[:].rearrange("p n s -> p (n s)")[:, 0:KT * P]
        pr_flat = pr_s[:].rearrange("p n s -> p (n s)")
        pair = lambda x: x.rearrange("p (c s) -> p c s", c=C)
        qk = [pair(pr_flat[:, i * C * S:(i + 1) * C * S]) for i in range(2)]
        part_flat = pr_flat[:, 2 * C * S:].bitcast(BF16)
        part = [part_flat[:, i * 3 * C * S:(i + 1) * 3 * C * S].rearrange("p (j c s) -> p j c s", j=3, c=C)
                for i in range(2)]
        rest = [pair(x[:].rearrange("p t d -> p (t d)")) for x in (at_s, xn_s)]
        rec = {"s": sb("rec_s", [P, T * HEADS_UP]), "x": sb("rec_x", [P, T])}
        sumT_s, sumT_x = sb("sumT_s", [P, S]), sb("sumT_x", [P, S])
        qz = sb("qz", [P, XH, S])
        q_ss = sb("q_ss", [P, T * XH])
        q_inv = sb("q_inv", [P, T * XH])
        carry = sb("carry", [P, E])
        r = {n: sb("r_" + n, [P, T, E]) for n in ("lg", "ex", "pr", "eq", "m", "pos", "t")}
        c = {n: sb("c_" + n, [P, T]) for n in ("mx", "sm", "rc")}
        chosen, placed_ = sb("chosen", [P, 2, T, E]), sb("chosen_places", [P, 2, T, E])
        ranked, top = sb("ranked", [P, 2, T]), sb("top", [P, 2, T])
        d2 = {n: sb("d2_" + n, [P, 2, T]) for n in ("place", "keep", "base", "f")}
        slot = sb("slot", [P, 2, T], U32)
        tick = sb("tick", [1, 16])
        vtick = sb("vtick", [1, 4])

        psum = ctx.enter_context(nc.psum_tensor("psum", [P, 8, 512], F32))
        G = lambda i: psum[:, i % NG, :]
        O = {"s": psum[:, NG, :], "x": psum[:, NG + 1, :]}
        SX = lambda i: psum[:, NG + 2 + i % NS, :]

        TOOK, n_products = placed(PRODUCTS)
        SCORED, n_scores = placed(SCORES)
        sems = {n: sem(n) for n in (
            "weights_loaded", "raw_loaded", "constants_made", "weight_turned", "weight_copied", "setup_step",
            "slots_cleared", "tables_made", "halves_made", "pads_made")}
        g_ready, g_taken = Tally(sem("product_ready"), n_products), Tally(sem("product_taken"), n_products)
        s_ready, s_done = Tally(sem("scores_ready"), n_scores), Tally(sem("exps_done"), n_scores)
        v_step = Tally(sem("vector_step"), {k: sum(DVE_STEPS[x] for x in st) for k, st in STAGES.items()})
        C_ = lambda n, per, before=0: Count(sem(n), per, before)
        x_in, c_in = C_("x_loaded", 16), C_("context_loaded", 32)
        normed = {n: C_(f"normed_{n}", 1) for n in tiles_of}
        padded = {n: C_(f"variance_padded_{n}", 1) for n in tiles_of}
        powered = {n: C_(f"inverse_ready_{n}", 1) for n in tiles_of}
        q_padded, q_powered = C_("query_squares_ready", 1), C_("query_inverse_ready", 1)
        k_powered = C_("key_inverse_ready", C)
        xs_biased, xx_made = C_("self_bias_added", 1), C_("cross_bias_added", 1)
        rounded = C_("parts_rounded", 4)
        rested = C_("rests_made", 4)
        stored = C_("parts_stored", 6 * 16)
        stacked = C_("parts_stacked", 2 * NPART * 16)
        max_out, max_in = C_("maxima_stored", 16), C_("maxima_placed", 16)
        used = {"s": C_("self_probs_used", H // 2), "x": C_("cross_probs_used", NXU, 1)}
        o_taken = {"s": C_("self_sums_taken", H // 4), "x": C_("cross_sums_taken", XH)}
        kb_ready = C_("key_bias_ready", 1)
        sq_ready = C_("key_squares_made", C)
        q_normed = C_("queries_normed", 1)
        x2_out = C_("residual_stored", 16, 1)
        ex_ready = C_("logit_exps_ready", 1)
        hot_ready = C_("choices_ready", 1)
        p_step = C_("pool_step", POOL_STEPS)
        slots_ready, scattered = C_("slots_ready", 1), C_("rows_scattered", 2 * T * 16)
        rows_free = C_("rows_free", 1, 1)

        block = ctx.enter_context(nc.Block())
        full, left = SC // P, SC % P
        LOADS = []
        for n in ("Wq", "Wk", "Wv", "Wm"):
            LOADS.append((w_self[n][:], a["L0_attn_" + n].rearrange("(c p) n -> p c n", p=P)))
        for n in ("bq", "bk"):
            LOADS.append((b_self[n][:], a["L0_attn_" + n].rearrange("(c p) -> p c", p=P)))
        for n, src in (("bv", "L0_attn_bv"), ("bm", "L0_attn_bm"), ("bo", "L0_xattn_bo")):
            LOADS.append((spread[n][:], a[src].partition_broadcast(P)))
        LOADS.append((router[:], a["L0_ffn_w_router"].rearrange("(c p) n -> p c n", p=P)))
        for i, n in enumerate(("g", "b")):
            LOADS.append((ln_l[:, :, i], a["L0_xattn_ln_l_" + n].rearrange("(c p) -> p c", p=P)))
            v = a["L0_xattn_ln_x_" + n].rearrange("(p a) -> p a", a=1)
            LOADS.append((ln_x[:, 0, i:i + 1], v[0:P, :]))
            LOADS.append((ln_x[0:DC - P, 1, i:i + 1], v[P:DC, :]))
        for i, n in enumerate(("qn_g", "kn_g")):
            v = a["L0_xattn_" + n]
            LOADS.append((grow[:, i, :], v.partition_broadcast(P)))
            for h in range(2):
                LOADS.append((gcol[h * XD:(h + 1) * XD, i:i + 1], v.rearrange("(p a) -> p a", a=1)))
        for b in range(B):
            m = a["mask_BxS2_bk0"][b, :]
            LOADS.append((mask8[b * CT:b * CT + full, :], m[0:full * P].rearrange("(t p) -> t p", p=P)))
            LOADS.append((mask8[b * CT + full:b * CT + full + 1, 0:left],
                          m[full * P:SC].rearrange("(a p) -> a p", a=1)))
        TURNED = [("Wq", 2, D, xwqT), ("Wo", 2, D, xwoT), ("Wlkv", 4, D, xwlT), ("Wkv", 4, DC, xwcT)]
        raw, raw_at = [], 0
        for _, t, w, _ in TURNED:
            raw.append(cT[:].rearrange("p c s -> p (c s)")[:, raw_at:raw_at + t * w].rearrange("p (t d) -> p t d", t=t))
            raw_at += t * w
        chunks = lambda w: [(k, min(P, w - k * P)) for k in range(-(-w // P))]

        @block.sync
        def _(sp):
            for (n, _, _, _), dst in zip(TURNED, raw):
                sp.dma_start(dst, a["L0_xattn_" + n].rearrange("(t p) n -> p t n", p=P)).then_inc(sems["raw_loaded"], 16)
            sp.wait_ge(sems["constants_made"], 3)
            for dst, src in LOADS[::2]:
                sp.dma_start(dst, src, allow_slow_non_contiguous=True).then_inc(sems["weights_loaded"], 16)
            sp.wait_ge(sems["pads_made"], 1)
            for sec in sections(sp):
                for name, i in sec.steps:
                    if name == "load":
                        if sec.kind == BOTH:
                            sp.wait_ge(xx_made.sem, xx_made.of(sec.x, 1))
                            sp.wait_ge(normed["l"].sem, normed["l"].of(sec.x, 1))
                        sp.dma_start(xs[:], a["x"][rows(sec.s), :, :].rearrange("a (t p) d -> p (a t) d", p=P)
                                     ).then_inc(x_in.sem, 16)
                        sp.dma_start(cb[:, 0:full, 0:DC], a["ctx_768"][rows(sec.s), 0:full * P, :]
                                     .rearrange("a (t p) d -> p (a t) d", p=P)).then_inc(c_in.sem, 16)
                        sp.dma_start(cb[0:left, full, 0:DC], a["ctx_768"][rows(sec.s), full * P:SC, :]
                                     .rearrange("a p d -> (a p) d")).then_inc(c_in.sem, 16)
                    elif name == "s_parts" and i == 1:
                        for j in range(3):
                            for qk_ in range(2):
                                if j < 2:
                                    sp.wait_ge(rounded.sem, rounded.of(sec.s, 2 * j + qk_ + 1))
                                else:
                                    sp.wait_ge(rested.sem, rested.of(sec.s, 2 + qk_ + 1))
                                sp.dma_start(scratch["parts"][qk_, j, :, :].rearrange("(c p) s -> p c s", p=P),
                                             part[qk_][:, j, :, :]).then_inc(stored.sem, 16)
                        sp.wait_ge(stored.sem, stored.of(sec.s, 6 * 16))
                        for qk_, order in enumerate((Q_PARTS, K_PARTS)):
                            for j, p in enumerate(order):
                                sp.dma_start(stack[qk_][j * HS:(j + 1) * HS, :, :],
                                             scratch["parts"][qk_, p, :, :].rearrange("(h d) s -> d h s", d=HS)
                                             ).then_inc(stacked.sem, 16)
                    elif name == "s_maxT":
                        sp.wait_ge(g_taken.sem, g_taken.at(sec, TOOK[sec.kind][name, i]))
                        sp.dma_start(scratch["maxima"], nmaxT[:]).then_inc(max_out.sem, 16)
                        sp.wait_ge(max_out.sem, max_out.of(sec.s, 16))
                        sp.dma_start(stack[0][MAXROW:MAXROW + 1, :, :], scratch["maxima"]
                                     .rearrange("(a h t) p -> a h (t p)", a=1, h=H)).then_inc(max_in.sem, 16)
                    elif name == "r_stats":
                        sp.wait_ge(g_taken.sem, g_taken.at(sec, TOOK[sec.kind]["x_out", 0]))
                        sp.dma_start(scratch["resid"][rows(sec.x), :, :].rearrange("a (t p) d -> p (a t) d", p=P),
                                     xx[:]).then_inc(x2_out.sem, 16)
            sp.wait_ge(x2_out.sem, x2_out.at(B, 0))

        @block.gpsimd
        def _(pool):
            made = sems["constants_made"]
            nc.gpsimd.memset(mask8[:], 0).then_inc(made, 1)
            nc.gpsimd.memset(xn_x[:], 0.0).then_inc(made, 1)
            nc.gpsimd.memset(ln_x[:], 0.0).then_inc(made, 1)
            nc.gpsimd.memset(nmax_pad[:], 0.0).then_inc(made, 1)
            zero_in = [(ident, ALU.not_equal, 1.0, 0.0, -1), (identb, ALU.not_equal, 1.0, 0.0, -1),
                       (hide_kq, ALU.is_ge, NEG, 0.0, 1), (hide_qk, ALU.is_ge, NEG, 0.0, -1),
                       (before, ALU.is_gt, 0.0, 1.0, 1)]
            for m, _, _, base, _ in zero_in:
                nc.gpsimd.memset(m[:], base).then_inc(made, 1)
            nc.gpsimd.memset(ones[:], 1.0).then_inc(made, 1)
            nc.gpsimd.memset(halves[:], 0.0).then_inc(made, 1)
            nc.gpsimd.memset(minus_half[:], -0.5).then_inc(made, 1)
            nc.gpsimd.memset(eps[:], EPS).then_inc(made, 1)
            nc.gpsimd.memset(carry[:], 0.0).then_inc(made, 1)
            for e in range(E):
                nc.gpsimd.memset(rank[:, :, e], float(E - e)).then_inc(made, 1)
            pool.wait_ge(made, 14 + E)
            for m, op, fill, _, sign in zero_in:
                nc.gpsimd.affine_select(out=m[:], in_=m[:], compare_op=op, fill=fill, base=0,
                                        pattern=[[sign, P]], channel_multiplier=-sign).then_inc(made, 1)
            pool.wait_ge(made, MADE)
            nc.gpsimd.memset(tick[:, 0:1], 0.0).then_inc(x2_out.sem, 1)
            nc.gpsimd.memset(tick[:, 1:2], 0.0).then_inc(used["x"].sem, 1)

            for sec in sections(pool):
                n, ticks = [0], [2]

                def step(ins):
                    n[0] += 1
                    ins.then_inc(p_step.sem, 1)
                    pool.wait_ge(p_step.sem, p_step.of(sec.x, n[0]))

                def held():
                    ticks[0] += 1
                    nc.gpsimd.tensor_tensor(tick[:, ticks[0]:ticks[0] + 1], ones[0:1, 0:1], ones[0:1, 0:1], ALU.add)

                def power(k):
                    pool.wait_ge(padded[k].sem, padded[k].of(sec.x if k in "lr" else sec.s, 1))
                    nc.gpsimd.tensor_tensor(inv[k][:], var[k][:], minus_half[:, 0:tiles_of[k]], ALU.pow
                                            ).then_inc(powered[k].sem, 1)

                def biased(dst, src, bias, done):
                    for t in range(T):
                        add = nc.gpsimd.tensor_tensor(dst[:, t, :], src[:, t, :], spread[bias][:], ALU.add)
                    add.then_inc(done.sem, 1)

                if sec.kind != FIRST:
                    pool.wait_ge(g_taken.sem, g_taken.at(sec, 0))
                for name, i in sec.steps:
                    if name == "l_norm":
                        pool.wait_ge(padded["l"].sem, padded["l"].of(sec.x, 1))
                        i1 = inv["l"][:]
                        step(nc.gpsimd.tensor_tensor(i1, var["l"][:], minus_half[:, 0:T], ALU.pow))
                        step(nc.gpsimd.tensor_tensor(inv2[:], i1, i1, ALU.mult))
                        step(nc.gpsimd.tensor_tensor(inv2[:], inv2[:], mv["l"][:, :, 1], ALU.mult))
                        step(nc.gpsimd.tensor_tensor(inv2[:], inv2[:], eps[:], ALU.add))
                        step(nc.gpsimd.tensor_tensor(inv2[:], inv2[:], minus_half[:, 0:T], ALU.pow))
                        nc.gpsimd.tensor_tensor(i1, i1, inv2[:], ALU.mult).then_inc(powered["l"].sem, 1)
                    elif name == "sc_norm":
                        power("c")
                    elif name == "x_base":
                        nc.gpsimd.tensor_copy(key_bias[:, 0:CT], ctx_bias[:, ds(sec.x[0] * CT, CT)]
                                              ).then_inc(kb_ready.sem, 1)
                        pool.wait_ge(x2_out.sem, x2_out.of(sec.x, 0))
                        biased(xx, xs, "bo", xx_made)
                    elif name == "s_norm":
                        power("s")
                    elif name == "s_v":
                        pool.wait_ge(normed["s"].sem, normed["s"].of(sec.s, 1))
                        biased(xs, xs, "bm", xs_biased)
                    elif name == "l_qn":
                        pool.wait_ge(q_padded.sem, q_padded.of(sec.x, 1))
                        nc.gpsimd.tensor_tensor(q_inv[:], q_ss[:], minus_half[:, 0:T * XH], ALU.pow
                                                ).then_inc(q_powered.sem, 1)
                    elif name == "l_ss" and i % PIECES == PIECES - 1:
                        ch = i // PIECES
                        pool.wait_ge(g_taken.sem, g_taken.at(sec, TOOK[sec.kind][name, i]))
                        two = lambda x: x[:].rearrange("p (j h) -> p j h", h=XH)[:, :, 2 * ch:2 * ch + 2]
                        nc.gpsimd.tensor_tensor(two(k_inv), two(k_ss), two(minus_half), ALU.pow
                                                ).then_inc(k_powered.sem, 1)
                    elif name == "r_norm":
                        power("r")
                    elif name == "r_places":
                        pool.wait_ge(slots_ready.sem, slots_ready.of(sec.x, 1))
                        held()
                        for t in range(T):
                            for k in range(2):
                                nc.gpsimd.indirect_dma_start(
                                    scratch["expert_in"], bass.IndirectOffsetOnAxis(slot[:, k, t:t + 1], 0),
                                    at_x[:, t, :], None, bounds_check=E * CAP - 1, oob_is_err=False
                                    ).then_inc(scattered.sem, 16)
                        pool.wait_ge(scattered.sem, scattered.of(sec.x, 2 * T * 16))
                        held()
                        nc.gpsimd.memset(tick[:, 0:1], 0.0).then_inc(rows_free.sem, 1)
                if sec.kind == FIRST:
                    pool.wait_ge(sems["slots_cleared"], 16 * (E * CAP // (P * T)))
                    nc.gpsimd.memset(tick[:, 2:3], 0.0).then_inc(rows_free.sem, 1)
                assert n[0] == (p_step.per if "x" in STAGES[sec.kind] else 0), n
        @block.scalar
        def _(act):
            act.wait_ge(sems["constants_made"], 3)
            for dst, src in LOADS[1::2]:
                act.dma_start(dst, src, allow_slow_non_contiguous=True).then_inc(sems["weights_loaded"], 16)
            for s in range(E * CAP // (P * T)):
                act.dma_start(scratch["expert_in"][s * P * T:(s + 1) * P * T, :]
                              .rearrange("(t p) d -> p t d", p=P), xn_x[:]).then_inc(sems["slots_cleared"], 16)
            for sec in sections(act):
                if sec.kind != FIRST:
                    act.wait_ge(used["x"].sem, used["x"].of(sec.x, 0))
                took = TOOK[sec.kind]
                for name, i in sec.steps:
                    k = SCORED[sec.kind][name, i]
                    if name == "s_q":
                        act.wait_ge(g_taken.sem, g_taken.at(sec, took[name, i]))
                        nc.scalar.activation(part[i][:, 0], qk[i], ACT.Copy).then_inc(rounded.sem, 1)
                    elif name == "s_rest":
                        act.wait_ge(rested.sem, rested.of(sec.s, i + 1))
                        nc.scalar.activation(part[i][:, 1], rest[i], ACT.Copy).then_inc(rounded.sem, 1)
                    elif name == "l_sq":
                        act.wait_ge(s_done.sem, s_done.at(sec, SCORED[sec.kind]["l_k", i]))
                        if i:
                            act.wait_ge(g_ready.sem, g_ready.at(sec, took["l_ss", PIECES * i - 1]))
                        nc.scalar.activation(xk2, xk[:, i, :], ACT.Square).then_inc(sq_ready.sem, 1)
                    elif name in ("c_k", "l_k"):
                        keys = SCP if name == "c_k" else S
                        for n, t0 in enumerate(range(0, keys, 512)):
                            w, to = min(512, keys - t0), t0 + (SCP if name == "l_k" else 0)
                            k = SCORED[sec.kind][name, i] - SCORES[name] + n
                            act.wait_ge(s_ready.sem, s_ready.at(sec, k + 1))
                            nc.scalar.activation(xk[:, i, to:to + w], SX(k)[:, 0:w], ACT.Copy).then_inc(s_done.sem, 1)
                    elif name in ("c_v", "l_v"):
                        j, w = (0 if name == "c_v" else CT) + 2 * i, 1 if 2 * i + 1 == CT and name == "c_v" else 2
                        act.wait_ge(s_ready.sem, s_ready.at(sec, k))
                        nc.scalar.activation(xv[:, j:j + w, :, 0:XD],
                                             SX(k - 1)[:, 0:w * D].rearrange("p (t h d) -> p t h d", t=w, h=XH),
                                             ACT.Copy).then_inc(s_done.sem, 1)
                    elif name == "s_scores":
                        act.wait_ge(s_ready.sem, s_ready.at(sec, k))
                        if i >= NPS:
                            act.wait_ge(used["s"].sem, used["s"].of(sec.s, (i - NPS) // 5 + 1))
                        nc.scalar.activation(pr_s[:, i % NPS, :], SX(k - 1), ACT.Exp).then_inc(s_done.sem, 1)
                    elif name == "x_scores":
                        act.wait_ge(s_ready.sem, s_ready.at(sec, k))
                        h, j = divmod(i, KT)
                        if i == 0:
                            act.wait_ge(kb_ready.sem, kb_ready.of(sec.x, 1))
                            act.wait_ge(g_ready.sem, g_ready.at(sec, took["l_ss", C * PIECES - 1]))
                        if i % (2 * KT) == 0:
                            act.wait_ge(k_powered.sem, k_powered.of(sec.x, i // (2 * KT) + 1))
                        if i >= NPX:
                            act.wait_ge(used["x"].sem, used["x"].of(sec.x, i - NPX + 1))
                        bias = key_bias[:, j:j + 1] if j < CT else shift[:, 0:1]
                        nc.scalar.activation(pr_x[:, i % NPX, :], SX(k - 1), ACT.Exp, bias=bias,
                                             scale=k_inv[:, j * XH + h:j * XH + h + 1]).then_inc(s_done.sem, 1)
                    elif name == "r_logits":
                        act.wait_ge(g_taken.sem, g_taken.at(sec, took[name, i]))
                        nc.scalar.activation(r["ex"][:], r["lg"][:], ACT.Exp).then_inc(ex_ready.sem, 1)

        @block.tensor
        def _(pe):
            mm, turn = nc.tensor.matmul, nc.tensor.transpose
            pe.wait_ge(sems["constants_made"], MADE)
            pe.wait_ge(sems["raw_loaded"], 16 * len(TURNED))
            k = 0
            for i, (_, t, w, dst) in enumerate(TURNED):
                for ch, cw in chunks(w):
                    if k >= 4:
                        pe.wait_ge(sems["weight_copied"], k - 3)
                    for j in range(t):
                        last = turn(SX(k)[0:cw, j * P:(j + 1) * P], raw[i][:, j, ch * P:ch * P + cw], ident[:])
                    last.then_inc(sems["weight_turned"], 1)
                    k += 1
            pe.wait_ge(sems["setup_step"], 1)
            pe.wait_ge(sems["weight_copied"], k - 3)
            turn(SX(k)[:, 0:B * CT], maskf[:], ident[0:B * CT, 0:B * CT]).then_inc(sems["weight_turned"], 1)
            pe.wait_ge(sems["tables_made"], 1)
            pe.wait_ge(sems["weights_loaded"], 16 * len(LOADS))

            for sec in sections(pe):
                g, s = [0], [0]
                took = TOOK[sec.kind]

                def bank():
                    g[0] += 1
                    if g[0] > NG or sec.kind != FIRST:
                        pe.wait_ge(g_taken.sem, g_taken.at(sec, max(g[0] - NG, 0)))
                    return G(g[0] - 1)

                def sbank():
                    s[0] += 1
                    if s[0] > NS or sec.kind != FIRST:
                        pe.wait_ge(s_done.sem, s_done.at(sec, max(s[0] - NS, 0)))
                    return SX(s[0] - 1)

                def whole(*step):
                    pe.wait_ge(g_taken.sem, g_taken.at(sec, took[step]))

                def turned(src, tiles, width=D):
                    for ch, cw in chunks(width):
                        for t0 in range(0, tiles, 4):
                            dst = bank()
                            for t in range(t0, min(t0 + 4, tiles)):
                                last = turn(dst[0:cw, (t - t0) * P:(t - t0 + 1) * P],
                                            src[:, t, ch * P:ch * P + cw], ident[:])
                            last.then_inc(g_ready.sem, 1)

                def to_features(w, col, src, width, n, contract=D, bank=bank, ready=g_ready):
                    for t0 in range(0, n, 512):
                        dst = bank()
                        tw = min(512, n - t0)
                        for ch, cw in chunks(contract):
                            last = mm(dst[:, 0:tw], w[0:cw, ch, col:col + width], src[0:cw, ch, t0:t0 + tw],
                                      start=ch == 0, stop=ch == C - 1)
                        last.then_inc(ready.sem, 1)

                def to_tokens(w, col, src, tiles, contract=D, first=0, bank=bank, ready=g_ready):
                    for t0 in range(first, tiles, 2):
                        dst = bank()
                        for t in range(t0, min(t0 + 2, tiles)):
                            for ch, cw in chunks(contract):
                                last = mm(dst[:, (t - t0) * D:(t - t0 + 1) * D], src[0:cw, ch, t * P:(t + 1) * P],
                                          w[0:cw, ch, col:col + D], start=ch == 0, stop=ch == C - 1)
                        last.then_inc(ready.sem, 1)

                to_act = {"bank": sbank, "ready": s_ready}
                qs, ks = stack

                def seen(dst, h, q):
                    w = (q + 1) * P
                    mm(dst[:, 0:w], qs[0:MAXROW, h, q * P:w], ks[0:MAXROW, h, 0:w], start=True, stop=False)
                    return mm(dst[:, q * P:w], identb[:], hide_qk[:], start=False, stop=True)

                def scored(dst, h, k):
                    w = S - k * P
                    mm(dst[:, 0:w], ks[0:MAXROW + 1, h, k * P:(k + 1) * P], qs[0:MAXROW + 1, h, k * P:S],
                       start=True, stop=False)
                    return mm(dst[:, 0:P], identb[:], hide_kq[:], start=False, stop=True)

                for name, i in sec.steps:
                    if name == "s_T":
                        pe.wait_ge(normed["s"].sem, normed["s"].of(sec.s, 1))
                        turned(xn_s, T)
                    elif name == "s_q":
                        if i == 0:
                            whole("s_T", 0)
                        for oc in range(C):
                            to_features(w_self[("Wq", "Wk")[i]], oc * P, xnT_s, P, S)
                    elif name == "s_v":
                        to_tokens(w_self["Wv"], 0, xnT_s, T)
                    elif name == "s_max":
                        pair_, u = divmod(i, 5)
                        if i == 0:
                            pe.wait_ge(stacked.sem, stacked.of(sec.s, 2 * NPART * 16))
                        dst = bank()
                        if u == 4:
                            seen(dst, 2 * pair_, 1)
                            last = seen(dst[:, 2 * P:], 2 * pair_ + 1, 1)
                        elif u % 2 == 0:
                            last = seen(dst, 2 * pair_ + u // 2, 3)
                        else:
                            seen(dst, 2 * pair_ + u // 2, 2)
                            last = seen(dst[:, 3 * P:], 2 * pair_ + u // 2, 0)
                        last.then_inc(g_ready.sem, 1)
                    elif name == "s_maxT":
                        whole("s_max", NSU - 1)
                        turn(bank()[:, 0:P], nmax_pad[:], ident[:]).then_inc(g_ready.sem, 1)
                    elif name == "s_scores":
                        pair_, u = divmod(i, 5)
                        dst = sbank()
                        if i == 0:
                            pe.wait_ge(max_in.sem, max_in.of(sec.s, 16))
                        if u == 4:
                            scored(dst, 2 * pair_, 2)
                            last = scored(dst[:, 2 * P:], 2 * pair_ + 1, 2)
                        elif u % 2 == 0:
                            last = scored(dst, 2 * pair_ + u // 2, 0)
                        else:
                            scored(dst, 2 * pair_ + u // 2, 1)
                            last = scored(dst[:, 3 * P:], 2 * pair_ + u // 2, 3)
                        last.then_inc(s_ready.sem, 1)
                    elif name == "s_sums":
                        if i % 2 == 0 and i:
                            pe.wait_ge(o_taken["s"].sem, o_taken["s"].of(sec.s, i // 2))
                        if i == 0:
                            whole("s_v", 0)
                        pe.wait_ge(s_done.sem, s_done.at(sec, SCORED[sec.kind]["s_scores", 5 * i + 4]))
                        for hh in range(2):
                            h = 2 * i + hh
                            lies = [(2 * hh, 0), (2 * hh + 1, 0), (4, 2 * P * hh), (2 * hh + 1, 3 * P)]
                            row = h % HEADS_UP * HEAD_ROWS
                            for k, (u, col) in enumerate(lies):
                                last = mm(O["s"][row:row + HEAD_ROWS, k * P:S], v_self[:, k, h, :],
                                          pr_s[:, (5 * i + u) % NPS, col:col + S - k * P], start=k == 0,
                                          stop=k == T - 1, tile_position=(0, row), skip_group_check=True)
                        last.then_inc(used["s"].sem, 1)
                    elif name == "s_head":
                        dst = bank()
                        pe.wait_ge(o_taken["s"].sem, o_taken["s"].of(sec.s, i + 1))
                        for t in range(T):
                            last = turn(dst[:, t * P:(t + 1) * P], sumT_s[:, t * P:(t + 1) * P], ident[:])
                        last.then_inc(g_ready.sem, 1)
                    elif name == "s_outT":
                        whole("s_head", H // HEADS_UP - 1)
                        turned(at_s, T)
                    elif name == "s_out":
                        whole("s_outT", 0)
                        to_tokens(w_self["Wm"], 0, xnT_s, T)
                    elif name == "l_T":
                        pe.wait_ge(normed["l"].sem, normed["l"].of(sec.x, 1))
                        turned(xn_x, T)
                    elif name == "l_q":
                        to_tokens(xwqT, 0, xnT_x, T)
                    elif name == "l_k":
                        if i == 0:
                            whole("l_T", 0)
                        to_features(xwlT, i * P, xnT_x, P, S, **to_act)
                    elif name == "l_v":
                        to_tokens(xwlT, D, xnT_x, 2 * i + 2, first=2 * i, **to_act)
                    elif name == "sc_T":
                        pe.wait_ge(normed["c"].sem, normed["c"].of(sec.s, 1))
                        turned(cb, CT)
                    elif name == "c_k":
                        to_features(xwcT, i * P, cT, P, SCP, **to_act)
                    elif name == "c_v":
                        to_tokens(xwcT, D, cT, min(2 * i + 2, CT), first=2 * i, **to_act)
                    elif name == "l_qT":
                        pe.wait_ge(q_normed.sem, q_normed.of(sec.x, 1))
                        turned(at_x, T)
                    elif name == "l_ss":
                        ch, piece = divmod(i, PIECES)
                        if piece == 0:
                            squares_to = bank()
                            pe.wait_ge(sq_ready.sem, sq_ready.of(sec.x, ch + 1))
                        n = -(-KT // PIECES)
                        for j in range(piece * n, min((piece + 1) * n, KT)):
                            last = mm(squares_to[:, 2 * j:2 * j + 2], xk2[:, j * P:(j + 1) * P], halves[:],
                                      start=True, stop=True)
                        if piece == PIECES - 1:
                            last.then_inc(g_ready.sem, 1)
                    elif name == "x_scores":
                        h, j = divmod(i, KT)
                        dst = sbank()
                        if i == 0:
                            whole("l_qT", 0)
                        mm(dst, xk[:, h // 2, j * P:(j + 1) * P], qz[:, h, :], start=True, stop=True
                           ).then_inc(s_ready.sem, 1)
                    elif name == "x_sums":
                        h, j = divmod(i, KT)
                        if i == 0:
                            pe.wait_ge(s_done.sem, s_done.at(sec, SCORED[sec.kind]["l_v", 1]))
                        if j == 0 and h:
                            pe.wait_ge(o_taken["x"].sem, o_taken["x"].of(sec.x, h))
                        pe.wait_ge(s_done.sem, s_done.at(sec, SCORED[sec.kind]["x_scores", i]))
                        mm(O["x"][0:XD + 1, :], xv[:, j, h, :], pr_x[:, i % NPX, :], start=j == 0, stop=j == KT - 1
                           ).then_inc(used["x"].sem, 1)
                    elif name == "x_head":
                        dst = bank()
                        pe.wait_ge(o_taken["x"].sem, o_taken["x"].of(sec.x, i + 1))
                        for t in range(T):
                            last = turn(dst[:, t * P:(t + 1) * P], sumT_x[:, t * P:(t + 1) * P], ident[:])
                        last.then_inc(g_ready.sem, 1)
                    elif name == "x_T":
                        whole("x_head", XH - 1)
                        turned(at_x, T)
                    elif name == "x_out":
                        whole("x_T", 0)
                        to_tokens(xwoT, 0, xnT_x, T)
                    elif name == "r_T":
                        pe.wait_ge(normed["r"].sem, normed["r"].of(sec.x, 1))
                        turned(at_x, T)
                    elif name == "r_logits":
                        whole("r_T", 0)
                        dst = bank()
                        for t in range(T):
                            for ch in range(C):
                                last = mm(dst[:, t * E:(t + 1) * E], xnT_x[:, ch, t * P:(t + 1) * P],
                                          router[:, ch, :], start=ch == 0, stop=ch == C - 1)
                        last.then_inc(g_ready.sem, 1)
                    elif name == "r_places":
                        dst = bank()
                        pe.wait_ge(hot_ready.sem, hot_ready.of(sec.x, 1))
                        for t in range(T + 1):
                            for u in range(min(t + 1, T)):
                                last = mm(dst[:, t * E:(t + 1) * E], before[:] if u == t else ones[:],
                                          r["m"][:, u, :], start=u == 0, stop=u == min(t, T - 1))
                        last.then_inc(g_ready.sem, 1)
                    assert g[0] == took[name, i] and s[0] == SCORED[sec.kind][name, i], (name, i, g, s)

        @block.vector
        def _(dve):
            V = nc.vector
            made, pads = sems["setup_step"], sems["pads_made"]
            V.memset(cb[:], 0.0).then_inc(pads, 1)
            V.memset(xwcT[:], 0.0).then_inc(pads, 1)
            V.memset(v_self[:], 0.0).then_inc(pads, 1)
            V.memset(qz[:], 0.0).then_inc(pads, 1)
            V.memset(stack[1][:], 1.0).then_inc(pads, 1)
            V.memset(xv[:], 1.0).then_inc(pads, 1)
            V.memset(sumT_x[:], 0.0).then_inc(pads, 1)
            dve.wait_ge(pads, 3)
            V.memset(v_self[:, :, :, HS], 1.0).then_inc(pads, 1)
            dve.wait_ge(pads, PADS)
            dve.wait_ge(sems["constants_made"], MADE)
            k = 0
            for _, t, w, dst in TURNED:
                for ch, cw in chunks(w):
                    dve.wait_ge(sems["weight_turned"], k + 1)
                    V.tensor_copy(dst[0:cw, ch, 0:t * P], SX(k)[0:cw, 0:t * P]).then_inc(sems["weight_copied"], 1)
                    k += 1
            dve.wait_ge(sems["weights_loaded"], 16 * len(LOADS))
            V.tensor_copy(maskf[:], mask8[:]).then_inc(made, 1)
            for h in range(2):
                V.memset(halves[h * XD:(h + 1) * XD, h:h + 1], 1.0).then_inc(sems["halves_made"], 1)
            V.tensor_tensor(grow[:, 0, :], grow[:, 0, :], grow[:, 1, :], ALU.mult).then_inc(made, 1)
            V.scalar_tensor_tensor(out=gqk[:], in0=gcol[:, 0:1], scalar=XD ** -0.5, in1=gcol[:, 1:2],
                                   op0=ALU.mult, op1=ALU.mult).then_inc(made, 1)
            dve.wait_ge(made, 3)
            V.tensor_reduce(shift[:], grow[:, 0, :], AX.X, ALU.max, apply_absolute_value=True).then_inc(made, 1)
            dve.wait_ge(made, 4)
            V.tensor_scalar(shift[:], shift[:], XD ** 0.5, -HEADROOM, ALU.mult, ALU.add).then_inc(made, 1)
            dve.wait_ge(made, 5)
            V.tensor_scalar(shift[:], shift[:], 0.0, -1.0, ALU.max, ALU.mult).then_inc(made, 1)
            dve.wait_ge(sems["weight_turned"], k + 1)
            V.tensor_scalar(hide[:], SX(k)[:, 0:B * CT], -1.0, -NEG, ALU.add, ALU.mult).then_inc(made, 1)
            dve.wait_ge(made, 7)
            dve.wait_ge(sems["halves_made"], 2)
            V.tensor_scalar(ctx_bias[:], hide[:], shift[:, 0:1], None, ALU.add).then_inc(sems["tables_made"], 1)
            dve.wait_ge(sems["tables_made"], 1)

            for sec in sections(dve):
                g, n = [0], [0]

                def took():
                    g[0] += 1
                    dve.wait_ge(g_ready.sem, g_ready.at(sec, g[0]))
                    return G(g[0] - 1)

                def step(ins):
                    n[0] += 1
                    ins.then_inc(v_step.sem, 1)
                    dve.wait_ge(v_step.sem, v_step.at(sec, n[0]))

                def variances(k, src, column):
                    for t in range(tiles_of[k]):
                        last = V.bn_stats(stats[:, t, :], src[:, t, :])
                    step(last)
                    V.memset(vtick[:, column:column + 1], 0.0)
                    for t in range(tiles_of[k]):
                        last = V.bn_aggr(mv[k][:, t, :], stats[:, t, :])
                    step(last)
                    V.tensor_scalar(var[k][:], mv[k][:, :, 1], EPS, None, ALU.add).then_inc(padded[k].sem, 1)

                def normalise(k, dst, src):
                    dve.wait_ge(powered[k].sem, powered[k].of(sec.x if k in "lr" else sec.s, 1))
                    for t in range(tiles_of[k]):
                        last = V.tensor_scalar(dst[:, t, :], src[:, t, :], mv[k][:, t, 0:1], inv[k][:, t:t + 1],
                                               ALU.subtract, ALU.mult)
                    last.then_inc(normed[k].sem, 1)

                def copied(dst, tiles=T, width=D, gain=None):
                    for ch, cw in chunks(width):
                        for t0 in range(0, tiles, 4):
                            w = min(4, tiles - t0) * P
                            src, to = took()[0:cw, 0:w], dst[0:cw, ch, t0 * P:t0 * P + w]
                            if gain is None:
                                ins = V.tensor_copy(to, src)
                            else:
                                ins = V.tensor_scalar(to, src, gain[0:cw, ch, 0:1], gain[0:cw, ch, 1:2],
                                                      ALU.mult, ALU.add)
                            ins.then_inc(g_taken.sem, 1)

                def largest(src, h, q, at_=0):
                    return V.tensor_reduce(nmax[:, h, q:q + 1], src[:, at_:at_ + (q + 1) * P], AX.X, ALU.max,
                                           negate=True)

                def laid_down(stage, dst, height, sums_done):
                    dve.wait_ge(used[stage].sem, used[stage].of(sec.s if stage == "s" else sec.x, sums_done))
                    V.tensor_copy(dst[0:height, :], O[stage][0:height, :]).then_inc(o_taken[stage].sem, 1)

                def divided(stage, heads, width, dst):
                    sums = took().rearrange("p (t h d) -> p t h d", t=T, h=heads)
                    dve.wait_ge(g_taken.sem, g_taken.at(sec, g[0] - 1))
                    over = rec[stage][:].rearrange("p (t h) -> p t h", t=T)
                    step(V.reciprocal(over, sums[:, :, :, width]))
                    V.tensor_tensor(dst.rearrange("p t (h d) -> p t h d", h=heads), sums[:, :, :, 0:width],
                                    over.unsqueeze(3).to_broadcast([P, T, heads, width]), ALU.mult
                                    ).then_inc(g_taken.sem, 1)

                def add_residual(x):
                    for t0 in range(0, T, 2):
                        V.tensor_tensor(x[:, t0:t0 + 2, :], took().rearrange("p (t d) -> p t d", t=2),
                                        x[:, t0:t0 + 2, :], ALU.add).then_inc(g_taken.sem, 1)

                wide = lambda x: x.unsqueeze(2).to_broadcast([P, T, E])
                if sec.kind != FIRST:
                    dve.wait_ge(g_taken.sem, g_taken.at(sec, 0))
                for name, i in sec.steps:
                    if name == "s_stats":
                        dve.wait_ge(x_in.sem, x_in.of(sec.s, 16))
                        variances("s", xs, 0)
                    elif name == "s_norm":
                        normalise("s", xn_s, xs)
                    elif name == "s_T":
                        copied(xnT_s)
                    elif name == "s_q":
                        for oc in range(C):
                            V.tensor_scalar(qk[i][:, oc, :], took(), b_self[("bq", "bk")[i]][:, oc:oc + 1],
                                            (HS ** -0.5, 1.0)[i], ALU.add, ALU.mult).then_inc(g_taken.sem, 1)
                    elif name == "s_rest":
                        dve.wait_ge(rounded.sem, rounded.of(sec.s, i + 1))
                        V.tensor_tensor(rest[i], qk[i], part[i][:, 0], ALU.subtract).then_inc(rested.sem, 1)
                    elif name == "s_parts":
                        dve.wait_ge(rounded.sem, rounded.of(sec.s, 2 + i + 1))
                        V.tensor_tensor(part[i][:, 2], rest[i], part[i][:, 1], ALU.subtract).then_inc(rested.sem, 1)
                    elif name == "s_v":
                        for t0 in range(0, T, 2):
                            src = took()
                            for t in range(t0, t0 + 2):
                                ins = V.tensor_tensor(
                                    v_self[:, t, :, 0:HS],
                                    src[:, (t - t0) * D:(t - t0 + 1) * D].rearrange("p (h d) -> p h d", h=H),
                                    spread["bv"][:].rearrange("p (h d) -> p h d", h=H), ALU.add)
                            ins.then_inc(g_taken.sem, 1)
                    elif name == "s_max":
                        pair_, u = divmod(i, 5)
                        src = took()
                        if u == 4:
                            largest(src, 2 * pair_, 1)
                            last = largest(src, 2 * pair_ + 1, 1, 2 * P)
                        elif u % 2 == 0:
                            last = largest(src, 2 * pair_ + u // 2, 3)
                        else:
                            largest(src, 2 * pair_ + u // 2, 2)
                            last = largest(src, 2 * pair_ + u // 2, 0, 3 * P)
                        last.then_inc(g_taken.sem, 1)
                    elif name == "s_maxT":
                        V.tensor_copy(nmaxT[:], took()[0:H * T, 0:P]).then_inc(g_taken.sem, 1)
                    elif name == "s_sums" and i % 2:
                        laid_down("s", sumT_s, P, i + 1)
                    elif name == "s_head":
                        divided("s", HEADS_UP, HS, at_s[:, :, i * HEADS_UP * HS:(i + 1) * HEADS_UP * HS])
                    elif name == "s_outT":
                        copied(xnT_s)
                    elif name == "s_out":
                        dve.wait_ge(xs_biased.sem, xs_biased.of(sec.s, 1))
                        add_residual(xs)
                    elif name == "l_stats":
                        variances("l", xs, 1)
                    elif name == "l_norm":
                        normalise("l", xn_x, xs)
                    elif name == "sc_stats":
                        dve.wait_ge(c_in.sem, c_in.of(sec.s, 32))
                        variances("c", cb[:, :, 0:DC], 2)
                    elif name == "sc_norm":
                        normalise("c", cb[:, :, 0:DC], cb[:, :, 0:DC])
                    elif name == "l_T":
                        copied(xnT_x, gain=ln_l)
                    elif name == "sc_T":
                        copied(cT, CT, gain=ln_x)
                    elif name == "l_q":
                        dve.wait_ge(rows_free.sem, rows_free.of(sec.x, 0))
                        for t0 in range(0, T, 2):
                            V.tensor_copy(at_x[:, t0:t0 + 2, :], took().rearrange("p (t d) -> p t d", t=2)
                                          ).then_inc(g_taken.sem, 1)
                        dve.wait_ge(g_taken.sem, g_taken.at(sec, g[0]))
                    elif name == "l_qss":
                        step(V.tensor_tensor(xn_x[:], at_x[:], at_x[:], ALU.mult))
                        step(V.tensor_reduce(q_ss[:], xn_x[:].rearrange("p t (h d) -> p (t h) d", h=XH), AX.X,
                                             ALU.add))
                        V.tensor_scalar(q_ss[:], q_ss[:], 1.0 / XD, RMS_EPS ** 2, ALU.mult, ALU.max
                                        ).then_inc(q_padded.sem, 1)
                    elif name == "l_qn":
                        dve.wait_ge(q_powered.sem, q_powered.of(sec.x, 1))
                        V.tensor_tensor(at_x[:].rearrange("p t (h d) -> p (t h) d", h=XH),
                                        at_x[:].rearrange("p t (h d) -> p (t h) d", h=XH),
                                        q_inv[:].unsqueeze(2).to_broadcast([P, T * XH, XD]), ALU.mult
                                        ).then_inc(q_normed.sem, 1)
                    elif name == "l_qT":
                        for ch in range(C):
                            src = took()
                            for h in range(2):
                                lo, hi = h * XD, (h + 1) * XD
                                ins = V.tensor_scalar(qz[lo:hi, 2 * ch + h, :], src[lo:hi, :], gqk[lo:hi, 0:1], None,
                                                      ALU.mult)
                            ins.then_inc(g_taken.sem, 1)
                    elif name == "l_ss" and i % PIECES == PIECES - 1:
                        ch = i // PIECES
                        V.tensor_scalar(k_ss[:].rearrange("p (j h) -> p j h", h=XH)[:, :, 2 * ch:2 * ch + 2],
                                        took()[:, 0:2 * KT].rearrange("p (j h) -> p j h", h=2), 1.0 / XD,
                                        RMS_EPS ** 2, ALU.mult, ALU.max).then_inc(g_taken.sem, 1)
                    elif name == "x_sums" and i % KT == KT - 1:
                        laid_down("x", sumT_x, XD + 1, i + 1)
                    elif name == "x_head":
                        divided("x", 1, XD, at_x[:, :, i * XD:(i + 1) * XD])
                    elif name == "x_T":
                        copied(xnT_x)
                    elif name == "x_out":
                        dve.wait_ge(xx_made.sem, xx_made.of(sec.x, 1))
                        add_residual(xx)
                    elif name == "r_stats":
                        dve.wait_ge(g_taken.sem, g_taken.at(sec, g[0]))
                        variances("r", xx, 3)
                    elif name == "r_norm":
                        normalise("r", at_x, xx)
                    elif name == "r_T":
                        copied(xnT_x)
                    elif name == "r_logits":
                        lg = took()[:, 0:T * E].rearrange("p (t e) -> p t e", t=T)
                        step(V.tensor_reduce(c["mx"][:], lg, AX.X, ALU.max))
                        V.tensor_tensor(r["lg"][:], lg, wide(c["mx"][:]), ALU.subtract).then_inc(g_taken.sem, 1)
                    elif name == "r_best":
                        dve.wait_ge(ex_ready.sem, ex_ready.of(sec.x, 1))
                        step(V.tensor_reduce(c["sm"][:], r["ex"][:], AX.X, ALU.add))
                        step(V.reciprocal(c["rc"][:], c["sm"][:]))
                        step(V.tensor_tensor(r["pr"][:], r["ex"][:], wide(c["rc"][:]), ALU.mult))
                        for k in range(2):
                            step(V.tensor_reduce(top[:, k, :], r["pr"][:], AX.X, ALU.max))
                            step(V.tensor_tensor(r["eq"][:], r["pr"][:], wide(top[:, k, :]), ALU.is_equal))
                            step(V.tensor_tensor(r["t"][:], r["eq"][:], rank[:], ALU.mult))
                            step(V.tensor_reduce(ranked[:, k, :], r["t"][:], AX.X, ALU.max))
                            step(V.tensor_tensor(chosen[:, k], rank[:], wide(ranked[:, k, :]), ALU.is_equal))
                            if k == 0:
                                step(V.scalar_tensor_tensor(out=r["pr"][:], in0=chosen[:, 0], scalar=-2.0, in1=r["pr"][:],
                                                            op0=ALU.mult, op1=ALU.add))
                        V.tensor_tensor(r["m"][:], chosen[:, 0], chosen[:, 1], ALU.add).then_inc(hot_ready.sem, 1)
                    elif name == "r_places":
                        src = took()
                        step(V.tensor_tensor(r["pos"][:], src[:, 0:T * E].rearrange("p (t e) -> p t e", t=T),
                                             carry[:].unsqueeze(1).to_broadcast([P, T, E]), ALU.add))
                        V.tensor_tensor(carry[:], src[:, T * E:(T + 1) * E], carry[:], ALU.add
                                        ).then_inc(g_taken.sem, 1)
                        dve.wait_ge(g_taken.sem, g_taken.at(sec, g[0]))
                        step(V.tensor_tensor(c["sm"][:], top[:, 0, :], top[:, 1, :], ALU.add))
                        step(V.reciprocal(c["rc"][:], c["sm"][:]))
                        pl, kp, bs, f = (d2[x][:] for x in ("place", "keep", "base", "f"))
                        step(V.tensor_tensor(placed_[:], chosen[:],
                                             r["pos"][:].unsqueeze(1).to_broadcast([P, 2, T, E]), ALU.mult))
                        step(V.tensor_reduce(pl, placed_[:], AX.X, ALU.add))
                        step(V.tensor_scalar(kp, pl, float(CAP), None, ALU.is_lt))
                        step(V.tensor_scalar(bs, ranked[:], -float(CAP), float(E * CAP), ALU.mult, ALU.add))
                        step(V.tensor_tensor(pl, pl, kp, ALU.mult))
                        step(V.tensor_tensor(pl, pl, bs, ALU.add))
                        step(V.tensor_copy(kept["gather_at"][:, rows(sec.x), :, :], pl.unsqueeze(1)))
                        step(V.tensor_scalar(f, kp, -FAR, FAR, ALU.mult, ALU.add))
                        step(V.tensor_tensor(f, f, pl, ALU.add))
                        V.tensor_copy(slot[:], f).then_inc(slots_ready.sem, 1)
                        dve.wait_ge(slots_ready.sem, slots_ready.of(sec.x, 1))
                        step(V.tensor_tensor(f, top[:], c["rc"][:].unsqueeze(1).to_broadcast([P, 2, T]), ALU.mult))
                        step(V.tensor_tensor(kept["gates"][:, rows(sec.x), :, :], f.unsqueeze(1), kp.unsqueeze(1),
                                             ALU.mult))
                    assert name[0] in "cl" or g[0] == TOOK[sec.kind][name, i], (name, i, g)
                assert n[0] == v_step.total[sec.kind], (sec.kind, n)


def experts_and_combine(nc, a, kept, scratch, out):
    with ExitStack() as ctx:
        sb = lambda n, s, d=F32: ctx.enter_context(nc.sbuf_tensor(n, s, d))
        sem = lambda n: ctx.enter_context(nc.semaphore(n))
        ident = kept["ident"]
        HALF = CAP // 2
        w1 = [sb(f"w1_{i}", [P, C, HID]) for i in range(2)]
        w2 = [sb(f"w2_{i}", [P, HC, D]) for i in range(2)]
        b1 = [sb(f"b1_{i}", [P, HC]) for i in range(2)]
        b1_rows = sb("b1_rows", [E * HC, P])
        b1T = sb("b1T", [P, E * HC])
        b2 = [sb(f"b2_{i}", [P, D]) for i in range(2)]
        xe = [sb(f"xe_{i}", [P, ST, D]) for i in range(2)]
        xeT = [sb(f"xeT_{i}", [P, C, CAP]) for i in range(2)]
        hT = [sb(f"hT_{i}", [P, HC, CAP]) for i in range(2)]
        oe = [sb(f"oe_{i}", [P, ST, D]) for i in range(2)]
        NY = 2
        rows_at = [sb(f"rows_at_{i}", [P, 2, T], U32) for i in range(NY)]
        gate = [sb(f"gate_{i}", [P, 2, T]) for i in range(NY)]
        tick = sb("tick2", [1, 10])
        y = [sb(f"y_{i}", [P, 2, T, D]) for i in range(2)]
        res = [sb(f"res_{i}", [P, T, D]) for i in range(2)]
        psum = ctx.enter_context(nc.psum_tensor("psum2", [P, 8, 512], F32))
        NR = 4
        G = lambda i: psum[:, i % NR, :]
        A = lambda i: psum[:, NR + i % NR, :]
        GX, GO, GA = 2 * C, ST // 2, HC * 2

        C_ = lambda n, per, before=0: Count(sem(n), per, before)
        rows_in = [C_(f"rows_in_{i}", 16) for i in range(2)]
        w1_in = [C_(f"w1_in_{i}", 16) for i in range(2)]
        w2_in = [C_(f"w2_in_{i}", 2 * 16) for i in range(2)]
        g_ready, g_taken = C_("ffn_product_ready", 2 * (GX + GO)), C_("ffn_product_taken", 2 * (GX + GO), 1)
        h_ready, h_done = C_("hidden_ready", 2 * GA), C_("hidden_done", 2 * GA, 1)
        stored = [C_(f"expert_rows_stored_{i}", 16, 1) for i in range(2)]
        copied_ = [C_(f"indices_copied_{i}", 2) for i in range(NY)]
        gathered = [C_(f"rows_gathered_{i}", 2 * T * 16) for i in range(NY)]
        res_in = [C_(f"residual_in_{i}", 16) for i in range(NY)]
        added = [C_(f"rows_added_{i}", 2, 1) for i in range(NY)]
        out_done = [C_(f"output_stored_{i}", 16, 1) for i in range(NY)]
        b1_in, b1_turned, b1_kept = sem("b1_loaded"), sem("b1_turned"), sem("b1_kept")
        b1_here = C_("b1_copied", 2)
        block = ctx.enter_context(nc.Block())

        @block.sync
        def _(sp):
            sp.dma_start(b1_rows[:], a["L0_ffn_b1"].rearrange("e (c p) -> (e c) p", p=P)).then_inc(b1_in, 16)
            with sp.Fori(0, E // 2) as i:
                for j in range(2):
                    if j == 0:
                        sp.wait_ge(h_done.sem, h_done.at(i, 0))
                    sp.dma_start(xe[j][:], scratch["expert_in"][ds((2 * i + j) * CAP, CAP), :]
                                 .rearrange("(t p) d -> p t d", p=P)).then_inc(rows_in[j].sem, 16)
                    sp.dma_start(w1[j][:], a["L0_ffn_w1"][ds(2 * i + j, 1), :, :]
                                 .rearrange("a (c p) n -> p (a c) n", p=P)).then_inc(w1_in[j].sem, 16)
                for j in range(2):
                    sp.wait_ge(stored[j].sem, stored[j].at(i, 0))
                    sp.dma_start(w2[j][:], a["L0_ffn_w2"][ds(2 * i + j, 1), :, :]
                                 .rearrange("a (c p) n -> p (a c) n", p=P)).then_inc(w2_in[j].sem, 16)
                    sp.dma_start(b2[j][:], a["L0_ffn_b2"][ds(2 * i + j, 1), :].rearrange("a n -> (a n)")
                                 .partition_broadcast(P)).then_inc(w2_in[j].sem, 16)
            with sp.Fori(0, B // 2) as i:
                for j in range(2):
                    sp.wait_ge(out_done[j].sem, out_done[j].at(i, 0))
                    sp.dma_start(res[j][:], scratch["resid"][ds(2 * i + j, 1), :, :]
                                 .rearrange("a (t p) d -> p (a t) d", p=P)).then_inc(res_in[j].sem, 16)

        @block.scalar
        def _(act):
            act.wait_ge(b1_turned, 1)
            nc.scalar.activation(b1T[:], A(0)[:, 0:E * HC], ACT.Copy).then_inc(b1_kept, 1)
            act.wait_ge(b1_kept, 1)
            with act.Fori(0, E // 2) as i:
                n = 0
                for j in range(2):
                    nc.scalar.activation(b1[j][:], b1T[:, ds((2 * i + j) * HC, HC)], ACT.Copy).then_inc(b1_here.sem, 1)
                    act.wait_ge(b1_here.sem, b1_here.at(i, j + 1))
                    for hc in range(HC):
                        for half in range(2):
                            act.wait_ge(h_ready.sem, h_ready.at(i, n + 1))
                            nc.scalar.activation(hT[j][:, hc, half * HALF:(half + 1) * HALF], A(n)[:, 0:HALF],
                                                 ACT.Relu, bias=b1[j][:, hc:hc + 1]).then_inc(h_done.sem, 1)
                            n += 1
                for j in range(2):
                    act.wait_ge(g_taken.sem, g_taken.at(i, 2 * GX + (j + 1) * GO))
                    act.dma_start(scratch["expert_out"][ds((2 * i + j) * CAP, CAP), :]
                                  .rearrange("(t p) d -> p t d", p=P), oe[j][:]).then_inc(stored[j].sem, 16)
            for j in range(2):
                act.wait_ge(stored[j].sem, stored[j].at(E // 2, 0))
            with act.Fori(0, B // 2) as i:
                for j in range(2):
                    act.wait_ge(added[j].sem, added[j].at(i, 2))
                    act.dma_start(out[ds(2 * i + j, 1), :, :].rearrange("a (t p) d -> p (a t) d", p=P), res[j][:]
                                  ).then_inc(out_done[j].sem, 16)
            for j in range(2):
                act.wait_ge(out_done[j].sem, out_done[j].at(B // 2, 0))

        @block.tensor
        def _(pe):
            mm = nc.tensor.matmul
            pe.wait_ge(b1_in, 16)
            nc.tensor.transpose(A(0)[:, 0:E * HC], b1_rows[:], ident[0:E * HC, 0:E * HC]).then_inc(b1_turned, 1)
            pe.wait_ge(b1_kept, 1)
            with pe.Fori(0, E // 2) as i:
                g, n = [0], 0

                def bank():
                    g[0] += 1
                    if g[0] > NR:
                        pe.wait_ge(g_taken.sem, g_taken.at(i, g[0] - NR))
                    else:
                        pe.wait_ge(g_taken.sem, g_taken.at(i, 0))
                    return G(g[0] - 1)

                for j in range(2):
                    pe.wait_ge(rows_in[j].sem, rows_in[j].at(i, 16))
                    for ch in range(C):
                        for half in range(2):
                            dst = bank()
                            for t in range(ST // 2):
                                last = nc.tensor.transpose(dst[:, t * P:(t + 1) * P],
                                                           xe[j][:, half * (ST // 2) + t, ch * P:(ch + 1) * P], ident[:])
                            last.then_inc(g_ready.sem, 1)
                for j in range(2):
                    pe.wait_ge(w1_in[j].sem, w1_in[j].at(i, 16))
                    pe.wait_ge(g_taken.sem, g_taken.at(i, (j + 1) * GX))
                    for hc in range(HC):
                        for half in range(2):
                            pe.wait_ge(h_done.sem, h_done.at(i, max(n + 1 - NR, 0)))
                            for ch in range(C):
                                last = mm(A(n)[:, 0:HALF], w1[j][:, ch, hc * P:(hc + 1) * P],
                                          xeT[j][:, ch, half * HALF:(half + 1) * HALF], start=ch == 0, stop=ch == C - 1)
                            last.then_inc(h_ready.sem, 1)
                            n += 1
                for j in range(2):
                    pe.wait_ge(w2_in[j].sem, w2_in[j].at(i, 2 * 16))
                    for t in range(ST):
                        if t % 2 == 0:
                            dst = bank()
                        if t == 0:
                            pe.wait_ge(h_done.sem, h_done.at(i, (j + 1) * GA))
                        for hc in range(HC):
                            last = mm(dst[:, t % 2 * D:(t % 2 + 1) * D], hT[j][:, hc, t * P:(t + 1) * P], w2[j][:, hc, :],
                                      start=hc == 0, stop=hc == HC - 1)
                        if t % 2:
                            last.then_inc(g_ready.sem, 1)

        @block.vector
        def _(dve):
            V = nc.vector
            with dve.Fori(0, E // 2) as i:
                g = [0]

                def took():
                    g[0] += 1
                    dve.wait_ge(g_ready.sem, g_ready.at(i, g[0]))
                    return G(g[0] - 1)

                for j in range(2):
                    for ch in range(C):
                        for half in range(2):
                            V.tensor_copy(xeT[j][:, ch, half * HALF:(half + 1) * HALF], took()[:, 0:HALF]
                                          ).then_inc(g_taken.sem, 1)
                for j in range(2):
                    dve.wait_ge(w2_in[j].sem, w2_in[j].at(i, 2 * 16))
                    dve.wait_ge(stored[j].sem, stored[j].at(i, 0))
                    for t in range(0, ST, 2):
                        V.tensor_tensor(oe[j][:, t:t + 2, :], took().rearrange("p (t d) -> p t d", t=2),
                                        b2[j][:].unsqueeze(1).to_broadcast([P, 2, D]), ALU.add).then_inc(g_taken.sem, 1)
            with dve.Fori(0, B // 2) as i:
                for j in range(2):
                    dve.wait_ge(gathered[j].sem, gathered[j].at(i, 2 * T * 16))
                    dve.wait_ge(res_in[j].sem, res_in[j].at(i, 16))
                    dve.wait_ge(copied_[j].sem, copied_[j].at(i, 2))
                    for k in range(2):
                        for t in range(T):
                            last = V.scalar_tensor_tensor(out=res[j][:, t, :], in0=y[j][:, k, t, :],
                                                          scalar=gate[j][:, k, t:t + 1], in1=res[j][:, t, :],
                                                          op0=ALU.mult, op1=ALU.add)
                        last.then_inc(added[j].sem, 1)
                        dve.wait_ge(added[j].sem, added[j].at(i, k + 1))

        @block.gpsimd
        def _(pool):
            for i, x in enumerate((g_taken, h_done, *stored, *added, *out_done)):
                nc.gpsimd.memset(tick[:, 2 + i:3 + i], 0.0).then_inc(x.sem, 1)
            for j in range(2):
                pool.wait_ge(stored[j].sem, stored[j].at(E // 2, 0))
            with pool.Fori(0, B // 2) as i:
                for j in range(2):
                    pool.wait_ge(added[j].sem, added[j].at(i, 0))
                    nc.gpsimd.tensor_copy(rows_at[j][:].unsqueeze(1), kept["gather_at"][:, ds(2 * i + j, 1), :, :]
                                          ).then_inc(copied_[j].sem, 1)
                    nc.gpsimd.tensor_copy(gate[j][:].unsqueeze(1), kept["gates"][:, ds(2 * i + j, 1), :, :]
                                          ).then_inc(copied_[j].sem, 1)
                    pool.wait_ge(copied_[j].sem, copied_[j].at(i, 2))
                    nc.gpsimd.tensor_tensor(tick[:, j:j + 1], ident[0:1, 0:1], ident[0:1, 0:1], ALU.add)
                    for k in range(2):
                        for t in range(T):
                            nc.gpsimd.indirect_dma_start(
                                y[j][:, k, t, :], None, scratch["expert_out"],
                                bass.IndirectOffsetOnAxis(rows_at[j][:, k, t:t + 1], 0),
                                bounds_check=E * CAP - 1, oob_is_err=False).then_inc(gathered[j].sem, 16)


_INS = ["x", "ctx_768", "mask_BxS2_bk0", "L0_attn_Wq", "L0_attn_bq", "L0_attn_Wk", "L0_attn_bk", "L0_attn_Wv",
        "L0_attn_bv", "L0_attn_Wm", "L0_attn_bm", "L0_xattn_ln_x_g", "L0_xattn_ln_x_b", "L0_xattn_ln_l_g",
        "L0_xattn_ln_l_b", "L0_xattn_qn_g", "L0_xattn_kn_g", "L0_xattn_Wq", "L0_xattn_Wkv", "L0_xattn_Wlkv",
        "L0_xattn_Wo", "L0_xattn_bo", "L0_ffn_w_router", "L0_ffn_w1", "L0_ffn_b1", "L0_ffn_w2", "L0_ffn_b2"]


def kernel(**inputs):
    import numpy as _np
    import concourse.bacc as _bacc
    from concourse import mybir as _mybir
    from concourse.bass_utils import run_bass_kernel_spmd as _run

    nc = _bacc.Bacc("TRN2", target_bir_lowering=False, num_devices=1)
    arrays, a = {}, {}
    for name in _INS:
        x = _np.ascontiguousarray(inputs[name])
        arrays[f"in_{name}"] = x
        a[name] = nc.dram_tensor(f"in_{name}", x.shape, _mybir.dt.from_np(x.dtype), kind="ExternalInput").ap()
    out = nc.dram_tensor("out", (B, S, D), F32, kind="ExternalOutput").ap()
    decoder(nc, a, out)
    r = _run(nc, [arrays], core_ids=[0])
    return r.results[0]["out"]
```
